# Optimizing a Trainium2 kernel written in Bass

```python
import numpy as np
import jax
import jax.numpy as jnp

def _softmax(x, axis=-1):
    return jax.nn.softmax(x, axis=axis)

def _gelu(x):
    return jax.nn.gelu(x, approximate=True)

def _silu(x):
    return jax.nn.silu(x)

def _sigmoid(x):
    return jax.nn.sigmoid(x)

def _layernorm(x, axis=-1, eps=1e-05):
    m = jnp.mean(x, axis=axis, keepdims=True)
    v = jnp.var(x, axis=axis, keepdims=True)
    return (x - m) / jnp.sqrt(v + eps)

def _scatter_add(tgt, idx, src, axis=0):
    return tgt.at[idx].add(src)

def _segment_sum(src, seg, n):
    return jax.ops.segment_sum(src, seg, n)
kernel_name = 'mk_seq_postln_d4_jaxref_r8_a2c246'

def setup_inputs(seed: int=0):
    np.random.seed(seed)
    _w = jnp.asarray

    def _L0_attn_setup():
        import jax, jax.numpy as jnp
        import numpy as np
        D_MODEL = 128
        NHEAD = 16
        HEAD_DIM = D_MODEL // NHEAD
        LN_EPS = 1e-05

        def _retention_scan(v, lam_h):
            B, L, H, DH = v.shape
            a = jnp.broadcast_to(lam_h[None, None, :, None], v.shape)

            def combine(x, y):
                a1, b1 = x
                a2, b2 = y
                return (a1 * a2, a2 * b1 + b2)
            _, states = jax.lax.associative_scan(combine, (a, v), axis=1)
            return states
        key = jax.random.key(seed)
        ks = jax.random.split(key, 6)
        B, L, D = (4, 512, D_MODEL)
        s = 1.0 / np.sqrt(D)
        return {'x': jax.random.normal(ks[0], (B, L, D), jnp.float32), 'Wq': jax.random.normal(ks[1], (D, D), jnp.float32) * s, 'Wv': jax.random.normal(ks[2], (D, D), jnp.float32) * s, 'Wg': jax.random.normal(ks[3], (D, D), jnp.float32) * s, 'Wo': jax.random.normal(ks[4], (D, D), jnp.float32) * s, 'beta': jnp.full((NHEAD,), -0.2, jnp.float32), 'ln_gamma': jnp.ones((D_MODEL,), jnp.float32), 'ln_beta': jnp.zeros((D_MODEL,), jnp.float32)}
    _L0_attn_in = _L0_attn_setup()

    def _L0_ffn_setup():
        import jax, jax.numpy as jnp
        import numpy as np
        DIM = 128

        def _reference_tuple_inner(x, W_r, W_k, W_v, mu_r, mu_k):
            B, T, C = x.shape
            x_prev = jnp.concatenate([jnp.zeros((B, 1, C), x.dtype), x[:, :-1, :]], axis=1)
            xr = mu_r * x + (1.0 - mu_r) * x_prev
            xk = mu_k * x + (1.0 - mu_k) * x_prev
            r = jax.nn.sigmoid(jnp.einsum('btc,dc->btd', xr, W_r))
            k = jnp.einsum('btc,dc->btd', xk, W_k)
            k_act = jnp.square(jax.nn.relu(k))
            out = r * jnp.einsum('btc,dc->btd', k_act, W_v)
            new_state = x[:, -1, :]
            return (out, new_state)
        key = jax.random.key(seed)
        ks = jax.random.split(key, 6)
        B, T, C = (8, 256, DIM)
        x = jax.random.normal(ks[0], (B, T, C), dtype=jnp.float32)
        s = 1.0 / np.sqrt(C)
        W_r = jax.random.uniform(ks[1], (C, C), jnp.float32, -s, s)
        W_k = jax.random.uniform(ks[2], (C, C), jnp.float32, -s, s)
        W_v = jax.random.uniform(ks[3], (C, C), jnp.float32, -s, s)
        mu_r = jax.random.uniform(ks[4], (C,), jnp.float32)
        mu_k = jax.random.uniform(ks[5], (C,), jnp.float32)
        return {'x': x, 'W_r': W_r, 'W_k': W_k, 'W_v': W_v, 'mu_r': mu_r, 'mu_k': mu_k}
    _L0_ffn_in = _L0_ffn_setup()

    def _L1_attn_setup():
        import jax, jax.numpy as jnp
        from jax import lax
        import numpy as np
        B, S, D_IN = (4, 512, 128)
        D_HIDDEN = 256
        N_BLOCKS = 16
        D_INNER = D_HIDDEN // 2
        R_MIN, R_MAX = (0.9, 0.999)
        MAX_IMAG = 0.1

        def _block_diag(x, W, b):
            xb = x.reshape(x.shape[0], x.shape[1], N_BLOCKS, -1)
            y = jnp.einsum('bsnh,nhk->bsnk', xb, W)
            return y.reshape(x.shape[0], x.shape[1], -1) + b

        def _reference_tuple_inner(x, W_in, b_in, Wg_x, bg_x, Wg_a, bg_a, a_real_param, a_imag_param, W_out, b_out):
            xh = x @ W_in + b_in
            gate_x = jax.nn.sigmoid(_block_diag(xh, Wg_x, bg_x))
            gate_a = jax.nn.sigmoid(_block_diag(xh, Wg_a, bg_a))
            magn_a = jnp.power(jax.nn.softplus(a_real_param), gate_a)
            theta = a_imag_param * gate_a * jnp.pi
            a = (magn_a * jnp.exp(1j * theta)).astype(jnp.complex64)
            xc = (xh[..., :D_INNER] + 1j * xh[..., D_INNER:]).astype(jnp.complex64)
            xc = gate_x * xc
            norm = jnp.sqrt(jnp.maximum(1.0 - jnp.square(magn_a), 1e-06))
            xc = norm * xc
            a_t = jnp.swapaxes(a, 0, 1)
            x_t = jnp.swapaxes(xc, 0, 1)

            def step(h, inp):
                a_i, x_i = inp
                h = a_i * h + x_i
                return (h, h)
            h0 = jnp.zeros((x.shape[0], D_INNER), jnp.complex64)
            h_last, hs = lax.scan(step, h0, (a_t, x_t), unroll=8)
            h = jnp.swapaxes(hs, 0, 1)
            h_merged = jnp.concatenate([h.real, h.imag], axis=-1)
            out = h_merged @ W_out + b_out
            h_last_merged = jnp.concatenate([h_last.real, h_last.imag], axis=-1)
            return (out, h_last_merged)
        key = jax.random.key(seed)
        ks = jax.random.split(key, 10)
        x = jax.random.normal(ks[0], (B, S, D_IN), jnp.float32)
        W_in = jax.random.normal(ks[1], (D_IN, D_HIDDEN), jnp.float32) / np.sqrt(D_IN)
        b_in = jnp.zeros((D_HIDDEN,), jnp.float32)
        blk_in, blk_out = (D_HIDDEN // N_BLOCKS, D_INNER // N_BLOCKS)
        Wg_x = jax.random.normal(ks[2], (N_BLOCKS, blk_in, blk_out), jnp.float32) / np.sqrt(blk_in)
        bg_x = jnp.zeros((D_INNER,), jnp.float32)
        Wg_a = jax.random.normal(ks[3], (N_BLOCKS, blk_in, blk_out), jnp.float32) / np.sqrt(blk_in)
        bg_a = jnp.zeros((D_INNER,), jnp.float32)
        u = jax.random.uniform(ks[4], (D_INNER,))
        a_real = jnp.sqrt(u * (R_MAX ** 2 - R_MIN ** 2) + R_MIN ** 2 + 1e-08)
        a_real_param = jnp.log(jnp.exp(a_real) - 1.0)
        a_imag_param = MAX_IMAG * (2.0 * jax.random.uniform(ks[5], (D_INNER,)) - 1.0)
        W_out = jax.random.normal(ks[6], (D_HIDDEN, D_IN), jnp.float32) / np.sqrt(D_HIDDEN)
        b_out = jnp.zeros((D_IN,), jnp.float32)
        return {'x': x, 'W_in': W_in, 'b_in': b_in, 'Wg_x': Wg_x, 'bg_x': bg_x, 'Wg_a': Wg_a, 'bg_a': bg_a, 'a_real_param': a_real_param, 'a_imag_param': a_imag_param, 'W_out': W_out, 'b_out': b_out}
    _L1_attn_in = _L1_attn_setup()

    def _L1_ffn_setup():
        import jax, jax.numpy as jnp
        import numpy as np
        INPUT_SIZE = 128
        OUTPUT_SIZE = 128
        key = jax.random.key(seed)
        kx, kt, kp, ktn, kpn = jax.random.split(key, 5)
        x = jax.random.normal(kx, (8, 256, INPUT_SIZE), dtype=jnp.float32)
        theta = jax.random.normal(kt, (INPUT_SIZE, OUTPUT_SIZE), dtype=jnp.float32) * 0.02
        phi = jax.random.normal(kp, (INPUT_SIZE, OUTPUT_SIZE), dtype=jnp.float32) * 0.02
        theta_noise = jax.random.normal(ktn, (INPUT_SIZE, OUTPUT_SIZE), dtype=jnp.float32) * 0.01
        phi_noise = jax.random.normal(kpn, (INPUT_SIZE, OUTPUT_SIZE), dtype=jnp.float32) * 0.01
        return {'x': x, 'theta': theta, 'phi': phi, 'theta_noise': theta_noise, 'phi_noise': phi_noise}
    _L1_ffn_in = _L1_ffn_setup()

    def _L2_attn_setup():
        import jax, jax.numpy as jnp
        import numpy as np
        NUM_HEADS = 16
        key = jax.random.key(seed)
        kx, kq, kk, kv = jax.random.split(key, 4)
        N, S, D = (2, 512, 128)
        scale = 1.0 / np.sqrt(D)
        x = jax.random.normal(kx, (N, S, D), dtype=jnp.float32)
        Wq = jax.random.normal(kq, (D, D), dtype=jnp.float32) * scale
        Wk = jax.random.normal(kk, (D, D), dtype=jnp.float32) * scale
        Wv = jax.random.normal(kv, (D, D), dtype=jnp.float32) * scale
        return {'x': x, 'Wq': Wq, 'Wk': Wk, 'Wv': Wv}
    _L2_attn_in = _L2_attn_setup()

    def _L2_ffn_setup():
        import jax, jax.numpy as jnp
        import numpy as np
        B, S, D = (4, 256, 128)
        E, K, I = (8, 2, 344)
        key = jax.random.key(seed)
        k0, k1, k2, k3, k4 = jax.random.split(key, 5)
        return {'x': jax.random.normal(k0, (B, S, D), jnp.float32), 'router_w': jax.random.normal(k1, (D, E), jnp.float32) * 0.02, 'w_gate': jax.random.normal(k2, (E, D, I), jnp.float32) * 0.02, 'w_up': jax.random.normal(k3, (E, D, I), jnp.float32) * 0.02, 'w_down': jax.random.normal(k4, (E, I, D), jnp.float32) * 0.02}
    _L2_ffn_in = _L2_ffn_setup()

    def _L3_attn_setup():
        import jax, jax.numpy as jnp
        import numpy as np
        B, L, D = (4, 512, 128)
        PHAZOR_SCALE_START = 32.0
        PHAZOR_SCALE_END = 2048.0
        key = jax.random.key(seed)
        ks = jax.random.split(key, 7)
        x = jax.random.normal(ks[0], (B, L, D), dtype=jnp.float32)
        phazor_init_re = jax.random.normal(ks[1], (D,), dtype=jnp.float32)
        phazor_init_im = jax.random.normal(ks[2], (D,), dtype=jnp.float32)
        phazor_angle = jax.random.normal(ks[3], (D,), dtype=jnp.float32)
        ln_minus_ln_phazor_abs = jax.random.normal(ks[4], (D,), dtype=jnp.float32)
        last_conv_re = jax.random.normal(ks[5], (D,), dtype=jnp.float32)
        last_conv_im = jax.random.normal(ks[6], (D,), dtype=jnp.float32)
        ln_phazor_scale = jnp.exp(jnp.linspace(np.log(1.0 / PHAZOR_SCALE_START), np.log(1.0 / PHAZOR_SCALE_END), D)).astype(jnp.float32)
        return {'x': x, 'phazor_init_re': phazor_init_re, 'phazor_init_im': phazor_init_im, 'phazor_angle': phazor_angle, 'ln_minus_ln_phazor_abs': ln_minus_ln_phazor_abs, 'last_conv_re': last_conv_re, 'last_conv_im': last_conv_im, 'ln_phazor_scale': ln_phazor_scale}
    _L3_attn_in = _L3_attn_setup()

    def _L3_ffn_setup():
        import jax, jax.numpy as jnp
        import numpy as np

        def _bitlinear(x, w_latent):
            scale = jax.lax.stop_gradient(jnp.clip(jnp.mean(jnp.abs(w_latent), axis=1, keepdims=True), 1e-05, None))
            tern = jnp.clip(jnp.round(w_latent / scale), -1.0, 1.0)
            w = w_latent + jax.lax.stop_gradient(tern - w_latent)
            return x @ (w * scale).T
        key = jax.random.key(seed)
        ks = jax.random.split(key, 6)
        dim, hidden, rank = (128, 512, 16)
        B, S = (4, 512)
        x = jax.random.normal(ks[0], (B, S, dim), dtype=jnp.float32)
        w_fc = 0.02 * jax.random.normal(ks[1], (hidden, dim), dtype=jnp.float32)
        w_proj = 0.02 * jax.random.normal(ks[2], (dim, hidden), dtype=jnp.float32)
        u = 0.02 * jax.random.normal(ks[3], (hidden, rank), dtype=jnp.float32)
        v = 0.02 * jax.random.normal(ks[4], (rank, dim), dtype=jnp.float32)
        fast_b = jax.random.normal(ks[5], (rank, rank), dtype=jnp.float32)
        gate = jnp.float32(0.05)
        return {'x': x, 'fast_b': fast_b, 'w_fc': w_fc, 'w_proj': w_proj, 'u': u, 'v': v, 'gate': gate}
    _L3_ffn_in = _L3_ffn_setup()
    _d = {'L0_attn_x': _L0_attn_in['x'], 'L0_attn_Wq': _L0_attn_in['Wq'], 'L0_attn_Wv': _L0_attn_in['Wv'], 'L0_attn_Wg': _L0_attn_in['Wg'], 'L0_attn_Wo': _L0_attn_in['Wo'], 'L0_attn_beta': _L0_attn_in['beta'], 'L0_attn_ln_gamma': _L0_attn_in['ln_gamma'], 'L0_attn_ln_beta': _L0_attn_in['ln_beta'], 'L0_ffn_W_r': _L0_ffn_in['W_r'], 'L0_ffn_W_k': _L0_ffn_in['W_k'], 'L0_ffn_W_v': _L0_ffn_in['W_v'], 'L0_ffn_mu_r': _L0_ffn_in['mu_r'], 'L0_ffn_mu_k': _L0_ffn_in['mu_k'], 'L1_attn_W_in': _L1_attn_in['W_in'], 'L1_attn_b_in': _L1_attn_in['b_in'], 'L1_attn_Wg_x': _L1_attn_in['Wg_x'], 'L1_attn_bg_x': _L1_attn_in['bg_x'], 'L1_attn_Wg_a': _L1_attn_in['Wg_a'], 'L1_attn_bg_a': _L1_attn_in['bg_a'], 'L1_attn_a_real_param': _L1_attn_in['a_real_param'], 'L1_attn_a_imag_param': _L1_attn_in['a_imag_param'], 'L1_attn_W_out': _L1_attn_in['W_out'], 'L1_attn_b_out': _L1_attn_in['b_out'], 'L1_ffn_theta': _L1_ffn_in['theta'], 'L1_ffn_phi': _L1_ffn_in['phi'], 'L1_ffn_theta_noise': _L1_ffn_in['theta_noise'], 'L1_ffn_phi_noise': _L1_ffn_in['phi_noise'], 'L2_attn_Wq': _L2_attn_in['Wq'], 'L2_attn_Wk': _L2_attn_in['Wk'], 'L2_attn_Wv': _L2_attn_in['Wv'], 'L2_ffn_router_w': _L2_ffn_in['router_w'], 'L2_ffn_w_gate': _L2_ffn_in['w_gate'], 'L2_ffn_w_up': _L2_ffn_in['w_up'], 'L2_ffn_w_down': _L2_ffn_in['w_down'], 'L3_attn_phazor_init_re': _L3_attn_in['phazor_init_re'], 'L3_attn_phazor_init_im': _L3_attn_in['phazor_init_im'], 'L3_attn_phazor_angle': _L3_attn_in['phazor_angle'], 'L3_attn_ln_minus_ln_phazor_abs': _L3_attn_in['ln_minus_ln_phazor_abs'], 'L3_attn_last_conv_re': _L3_attn_in['last_conv_re'], 'L3_attn_last_conv_im': _L3_attn_in['last_conv_im'], 'L3_attn_ln_phazor_scale': _L3_attn_in['ln_phazor_scale'], 'L3_ffn_fast_b': _L3_ffn_in['fast_b'], 'L3_ffn_w_fc': _L3_ffn_in['w_fc'], 'L3_ffn_w_proj': _L3_ffn_in['w_proj'], 'L3_ffn_u': _L3_ffn_in['u'], 'L3_ffn_v': _L3_ffn_in['v'], 'L3_ffn_gate': _L3_ffn_in['gate']}
    _x0 = _d['L0_attn_x']
    _d['L0_attn_x'] = jax.random.normal(jax.random.fold_in(jax.random.key(seed), 1), (4, 512, 128), dtype=_x0.dtype)
    del _x0
    return _d

def reference(L0_attn_x, L0_attn_Wq, L0_attn_Wv, L0_attn_Wg, L0_attn_Wo, L0_attn_beta, L0_attn_ln_gamma, L0_attn_ln_beta, L0_ffn_W_r, L0_ffn_W_k, L0_ffn_W_v, L0_ffn_mu_r, L0_ffn_mu_k, L1_attn_W_in, L1_attn_b_in, L1_attn_Wg_x, L1_attn_bg_x, L1_attn_Wg_a, L1_attn_bg_a, L1_attn_a_real_param, L1_attn_a_imag_param, L1_attn_W_out, L1_attn_b_out, L1_ffn_theta, L1_ffn_phi, L1_ffn_theta_noise, L1_ffn_phi_noise, L2_attn_Wq, L2_attn_Wk, L2_attn_Wv, L2_ffn_router_w, L2_ffn_w_gate, L2_ffn_w_up, L2_ffn_w_down, L3_attn_phazor_init_re, L3_attn_phazor_init_im, L3_attn_phazor_angle, L3_attn_ln_minus_ln_phazor_abs, L3_attn_last_conv_re, L3_attn_last_conv_im, L3_attn_ln_phazor_scale, L3_ffn_fast_b, L3_ffn_w_fc, L3_ffn_w_proj, L3_ffn_u, L3_ffn_v, L3_ffn_gate):

    def _L0_attn_ref(x, Wq, Wv, Wg, Wo, beta, ln_gamma, ln_beta):
        import jax, jax.numpy as jnp
        import numpy as np
        D_MODEL = 128
        NHEAD = 16
        HEAD_DIM = D_MODEL // NHEAD
        LN_EPS = 1e-05

        def _retention_scan(v, lam_h):
            B, L, H, DH = v.shape
            a = jnp.broadcast_to(lam_h[None, None, :, None], v.shape)

            def combine(x, y):
                a1, b1 = x
                a2, b2 = y
                return (a1 * a2, a2 * b1 + b2)
            _, states = jax.lax.associative_scan(combine, (a, v), axis=1)
            return states
        B, L, D = x.shape
        H, DH = (NHEAD, HEAD_DIM)
        q = (x @ Wq.T).reshape(B, L, H, DH)
        v = (x @ Wv.T).reshape(B, L, H, DH)
        lam_h = jax.nn.sigmoid(beta)
        state = _retention_scan(v, lam_h)
        y = (q * state).reshape(B, L, D)
        mu = jnp.mean(y, axis=-1, keepdims=True)
        var = jnp.mean((y - mu) ** 2, axis=-1, keepdims=True)
        y = (y - mu) * jax.lax.rsqrt(var + LN_EPS) * ln_gamma + ln_beta
        gate = jax.nn.silu(x @ Wg.T)
        y = y * gate
        return y @ Wo.T

    def _L0_ffn_ref(x, W_r, W_k, W_v, mu_r, mu_k):
        import jax, jax.numpy as jnp
        import numpy as np
        DIM = 128

        def _reference_tuple_inner(x, W_r, W_k, W_v, mu_r, mu_k):
            B, T, C = x.shape
            x_prev = jnp.concatenate([jnp.zeros((B, 1, C), x.dtype), x[:, :-1, :]], axis=1)
            xr = mu_r * x + (1.0 - mu_r) * x_prev
            xk = mu_k * x + (1.0 - mu_k) * x_prev
            r = jax.nn.sigmoid(jnp.einsum('btc,dc->btd', xr, W_r))
            k = jnp.einsum('btc,dc->btd', xk, W_k)
            k_act = jnp.square(jax.nn.relu(k))
            out = r * jnp.einsum('btc,dc->btd', k_act, W_v)
            new_state = x[:, -1, :]
            return (out, new_state)
        return _reference_tuple_inner(x, W_r, W_k, W_v, mu_r, mu_k)[0]

    def _L1_attn_ref(x, W_in, b_in, Wg_x, bg_x, Wg_a, bg_a, a_real_param, a_imag_param, W_out, b_out):
        import jax, jax.numpy as jnp
        from jax import lax
        import numpy as np
        B, S, D_IN = (4, 512, 128)
        D_HIDDEN = 256
        N_BLOCKS = 16
        D_INNER = D_HIDDEN // 2
        R_MIN, R_MAX = (0.9, 0.999)
        MAX_IMAG = 0.1

        def _block_diag(x, W, b):
            xb = x.reshape(x.shape[0], x.shape[1], N_BLOCKS, -1)
            y = jnp.einsum('bsnh,nhk->bsnk', xb, W)
            return y.reshape(x.shape[0], x.shape[1], -1) + b

        def _reference_tuple_inner(x, W_in, b_in, Wg_x, bg_x, Wg_a, bg_a, a_real_param, a_imag_param, W_out, b_out):
            xh = x @ W_in + b_in
            gate_x = jax.nn.sigmoid(_block_diag(xh, Wg_x, bg_x))
            gate_a = jax.nn.sigmoid(_block_diag(xh, Wg_a, bg_a))
            magn_a = jnp.power(jax.nn.softplus(a_real_param), gate_a)
            theta = a_imag_param * gate_a * jnp.pi
            a = (magn_a * jnp.exp(1j * theta)).astype(jnp.complex64)
            xc = (xh[..., :D_INNER] + 1j * xh[..., D_INNER:]).astype(jnp.complex64)
            xc = gate_x * xc
            norm = jnp.sqrt(jnp.maximum(1.0 - jnp.square(magn_a), 1e-06))
            xc = norm * xc
            a_t = jnp.swapaxes(a, 0, 1)
            x_t = jnp.swapaxes(xc, 0, 1)

            def step(h, inp):
                a_i, x_i = inp
                h = a_i * h + x_i
                return (h, h)
            h0 = jnp.zeros((x.shape[0], D_INNER), jnp.complex64)
            h_last, hs = lax.scan(step, h0, (a_t, x_t), unroll=8)
            h = jnp.swapaxes(hs, 0, 1)
            h_merged = jnp.concatenate([h.real, h.imag], axis=-1)
            out = h_merged @ W_out + b_out
            h_last_merged = jnp.concatenate([h_last.real, h_last.imag], axis=-1)
            return (out, h_last_merged)
        return _reference_tuple_inner(x, W_in, b_in, Wg_x, bg_x, Wg_a, bg_a, a_real_param, a_imag_param, W_out, b_out)[0]

    def _L1_ffn_ref(x, theta, phi, theta_noise, phi_noise):
        import jax, jax.numpy as jnp
        import numpy as np
        INPUT_SIZE = 128
        OUTPUT_SIZE = 128
        real = jnp.einsum('bti,io->bto', x, jnp.cos(theta + theta_noise))
        imag = jnp.einsum('bti,io->bto', x, jnp.sin(phi + phi_noise))
        return jnp.sqrt(real * real + imag * imag)

    def _L2_attn_ref(x, Wq, Wk, Wv):
        import jax, jax.numpy as jnp
        import numpy as np
        NUM_HEADS = 16
        N, S, D = x.shape
        H = NUM_HEADS
        hd = D // H
        q = (x @ Wq.T).reshape(N, S, H, hd).transpose(0, 2, 1, 3)
        k = (x @ Wk.T).reshape(N, S, H, hd).transpose(0, 2, 1, 3)
        v = (x @ Wv.T).reshape(N, S, H, hd).transpose(0, 2, 1, 3)
        energy = jnp.einsum('nhqd,nhkd->nhqk', q, k)
        attn = jax.nn.softmax(energy / jnp.sqrt(jnp.float32(hd)), axis=3)
        out = jnp.einsum('nhql,nhld->nhqd', attn, v)
        return out.transpose(0, 2, 1, 3).reshape(N, S, D)

    def _L2_ffn_ref(x, router_w, w_gate, w_up, w_down):
        import jax, jax.numpy as jnp
        import numpy as np
        B, S, D = (4, 256, 128)
        E, K, I = (8, 2, 344)
        orig_shape = x.shape
        d = orig_shape[-1]
        xf = x.reshape(-1, d)
        T = xf.shape[0]
        n_experts = router_w.shape[1]
        probs = jax.nn.softmax(xf @ router_w, axis=-1)
        w, idx = jax.lax.top_k(probs, K)
        w = w / (jnp.sum(w, axis=-1, keepdims=True) + 1e-06)
        combine = jnp.zeros((T, n_experts), xf.dtype).at[jnp.arange(T)[:, None], idx].add(w)
        out = jnp.zeros_like(xf)
        for e in range(n_experts):
            h = jax.nn.silu(xf @ w_gate[e]) * (xf @ w_up[e])
            out = out + combine[:, e:e + 1] * (h @ w_down[e])
        return out.reshape(orig_shape)

    def _L3_attn_ref(x, phazor_init_re, phazor_init_im, phazor_angle, ln_minus_ln_phazor_abs, last_conv_re, last_conv_im, ln_phazor_scale):
        import jax, jax.numpy as jnp
        import numpy as np
        B, L, D = (4, 512, 128)
        PHAZOR_SCALE_START = 32.0
        PHAZOR_SCALE_END = 2048.0
        b, length, d = x.shape
        dtype = x.dtype
        xc = x.astype(jnp.complex64)
        decay = jnp.exp(ln_minus_ln_phazor_abs)
        phazor = jnp.exp((phazor_angle * 1j - decay) * ln_phazor_scale)
        t = jnp.arange(length, dtype=jnp.float32)[:, None]
        phazor_progression = phazor[None, :] ** t
        phazor_init = phazor_init_re + 1j * phazor_init_im
        filt = phazor_progression * phazor_init[None, :]
        filter_fft = jnp.fft.fft(filt, n=2 * length, axis=0)
        x_fft = jnp.fft.fft(xc, n=2 * length, axis=1)
        conv_filter_x = jnp.fft.ifft(filter_fft[None] * x_fft, axis=1)[:, :length]
        last_conv = (last_conv_re + 1j * last_conv_im)[None, None, :]
        conv_with_past = conv_filter_x + last_conv * phazor_progression[None] * phazor[None, None, :]
        gate = 1.0 - jnp.exp(-decay * ln_phazor_scale)
        y = conv_with_past * gate
        return y.real.astype(dtype)

    def _L3_ffn_ref(x, fast_b, w_fc, w_proj, u, v, gate):
        import jax, jax.numpy as jnp
        import numpy as np

        def _bitlinear(x, w_latent):
            scale = jax.lax.stop_gradient(jnp.clip(jnp.mean(jnp.abs(w_latent), axis=1, keepdims=True), 1e-05, None))
            tern = jnp.clip(jnp.round(w_latent / scale), -1.0, 1.0)
            w = w_latent + jax.lax.stop_gradient(tern - w_latent)
            return x @ (w * scale).T
        h = _bitlinear(x, w_fc) + gate * (x @ v.T @ fast_b.T @ u.T)
        r = jnp.maximum(h, 0.0)
        return _bitlinear(r * r, w_proj)
    x = L0_attn_x
    x = _layernorm(x + _L0_attn_ref(x, L0_attn_Wq, L0_attn_Wv, L0_attn_Wg, L0_attn_Wo, L0_attn_beta, L0_attn_ln_gamma, L0_attn_ln_beta), axis=-1)
    x = _layernorm(x + _L0_ffn_ref(x, L0_ffn_W_r, L0_ffn_W_k, L0_ffn_W_v, L0_ffn_mu_r, L0_ffn_mu_k), axis=-1)
    x = _layernorm(x + _L1_attn_ref(x, L1_attn_W_in, L1_attn_b_in, L1_attn_Wg_x, L1_attn_bg_x, L1_attn_Wg_a, L1_attn_bg_a, L1_attn_a_real_param, L1_attn_a_imag_param, L1_attn_W_out, L1_attn_b_out), axis=-1)
    x = _layernorm(x + _L1_ffn_ref(x, L1_ffn_theta, L1_ffn_phi, L1_ffn_theta_noise, L1_ffn_phi_noise), axis=-1)
    x = _layernorm(x + _L2_attn_ref(x, L2_attn_Wq, L2_attn_Wk, L2_attn_Wv), axis=-1)
    x = _layernorm(x + _L2_ffn_ref(x, L2_ffn_router_w, L2_ffn_w_gate, L2_ffn_w_up, L2_ffn_w_down), axis=-1)
    x = _layernorm(x + _L3_attn_ref(x, L3_attn_phazor_init_re, L3_attn_phazor_init_im, L3_attn_phazor_angle, L3_attn_ln_minus_ln_phazor_abs, L3_attn_last_conv_re, L3_attn_last_conv_im, L3_attn_ln_phazor_scale), axis=-1)
    x = _layernorm(x + _L3_ffn_ref(x, L3_ffn_fast_b, L3_ffn_w_fc, L3_ffn_w_proj, L3_ffn_u, L3_ffn_v, L3_ffn_gate), axis=-1)
    return x

_drawn_inputs = setup_inputs


def setup_inputs(seed=0):
    import zlib

    import numpy as np

    out = dict(_drawn_inputs(seed))
    spreads = {'L0_attn_beta': (-0.20000000298023224, 0.6),
     'L0_attn_ln_gamma': (1.0, 0.2),
     'L0_attn_ln_beta': (0.0, 0.1),
     'L1_attn_b_in': (0.0, 0.1),
     'L1_attn_bg_x': (0.0, 0.347),
     'L1_attn_bg_a': (0.0, 0.1),
     'L1_attn_b_out': (0.0, 0.1)}
    factors = {'L0_ffn_W_r': 3.098,
     'L0_ffn_mu_r': 6.302,
     'L1_ffn_theta': 8.0,
     'L1_ffn_theta_noise': 8.0,
     'L2_ffn_router_w': 8.0,
     'L2_ffn_w_gate': 8.0,
     'L2_ffn_w_up': 8.0,
     'L2_ffn_w_down': 8.0,
     'L3_attn_last_conv_re': 8.0,
     'L3_attn_last_conv_im': 44.647,
     'L3_ffn_fast_b': 8.0,
     'L3_ffn_w_fc': 6.021,
     'L3_ffn_w_proj': 4.974,
     'L3_ffn_u': 8.0,
     'L3_ffn_v': 8.0}
    for name, (base, spread) in spreads.items():
        noise = np.random.default_rng([zlib.crc32(name.encode()), seed]).standard_normal(out[name].shape)
        drawn = base * np.exp(spread * noise) if base else spread * noise
        out[name] = jnp.asarray(drawn.astype(out[name].dtype))
    for name, factor in factors.items():
        out[name] = (out[name] * factor).astype(out[name].dtype)
    return out
```

```python
import concourse.bass as bass
from concourse import mybir
from contextlib import ExitStack

B, L, D = 4, 512, 128
NT = L // 128
PAIRS = 2
NH, HD = 16, 8
NG = 4
E_MOE, I_MOE = 8, 344
MT = [(0, 128), (128, 128), (256, 88)]
HID = 512
RANK = 16
VW = HD + 1
NLN = 9
EPS = 1e-5
MAGIC = 1.5 * 2.0 ** 23
MAGIC14 = 1.5 * 2.0 ** 9
TURN = 6.283185
PI_2 = 1.5707962

VEC = ["beta", "gamma", "lnb", "mu_r", "mu_k", "b_re", "b_im", "bg_x", "bg_a", "a_re", "a_im",
       "ph_re", "ph_im", "ph_ang", "ph_ln", "lc_re", "lc_im", "ph_sc", "gate"]
V = {n: i for i, n in enumerate(VEC)}
WA = ["l0_q", "l0_v", "l0_g", "l0_o", "ident"]
WB = ["f0_r", "f0_k", "f0_v", "in_re", "in_im", "inT0", "inT1", "bdx0", "bdx1", "bda0", "bda1",
      "out0", "out1", "b_out", "th", "thn", "phi", "phin", "a_q", "a_k", "a_v"]
WC = ["fc0", "fc1", "fc2", "fc3", "pj0", "pj1", "pj2", "pj3"]


def build(nc, xt_d, xf_d, vec_d, wa_d, wb_d, wc_d, small_d, rt_d, gu_d, dn_d, iota_d, tri_d, out_d,
          LAST=8):
    F32, BF16, FP16 = mybir.dt.float32, mybir.dt.bfloat16, mybir.dt.float16
    ALU, ACT, AX = mybir.AluOpType, mybir.ActivationFunctionType, mybir.AxisListType
    ADD, SUB, MUL, MAX = ALU.add, ALU.subtract, ALU.mult, ALU.max

    ctx = ExitStack()
    with ctx:
        def sb(name, shape, dt=F32):
            return ctx.enter_context(nc.sbuf_tensor(name, shape, dt))

        def sem(name):
            return ctx.enter_context(nc.semaphore(name))

        xT = [sb(f"xT{p}", [128, L]) for p in range(2)]
        xF = [sb(f"xF{p}", [128, 1 + L]) for p in range(2)]
        Y = [sb(f"Y{p}", [128, L]) for p in range(2)]
        NTMP = 10
        tmp = [[sb(f"tmp{p}_{i}", [128, 1 + L]) for i in range(NTMP)] for p in range(2)]
        vec = sb("vec", [128, len(VEC)])
        wa = sb("wa", [128, len(WA), 128])
        wb = sb("wb", [128, len(WB), 128])
        wc = sb("wc", [128, len(WC), 128])
        small = sb("small", [RANK, HID + 128 + RANK])
        router = sb("router", [128, E_MOE])
        gu = sb("gu", [128, 2, E_MOE, I_MOE])
        dn = sb("dn", [128, E_MOE * 3, 128])
        tri = sb("tri", [128, E_MOE, E_MOE])
        st6 = sb("st6", [128, 2, NT, 6])
        mv = sb("mv", [128, 2, NT, 2])
        rstd = sb("rstd", [128, 2, NT])
        kc = sb("kc", [128, 8])
        sv = sb("sv", [128, 64])
        wgx = sb("wgx", [128, 128])
        wga = sb("wga", [128, 128])
        w_cos = sb("w_cos", [128, 128])
        w_sin = sb("w_sin", [128, 128])
        stmp = sb("stmp", [128, 2, 128])
        tab = sb("tab", [128, 4, L])
        iota = tab[:, 3, :]
        tt = [tmp[1][5][:, 0:L], tmp[0][6][:, 0:L]]
        x0F = [tmp[p][9][:, 0:L] for p in range(2)]
        fcT = sb("fcT", [128, HID])
        pjT = sb("pjT", [128, HID])
        wq_s = [tmp[1][6 + i][:, 0:L] for i in range(3)]
        fsc = sb("fsc", [128, 5, 3])
        uT_m = sb("uT_m", [RANK, 128])
        QS = [sb(f"QS{p}", [128, NH, L], BF16) for p in range(2)]
        KS = [sb(f"KS{p}", [128, NH, L], BF16) for p in range(2)]
        parts = sb("parts", [128, 2, 3, L], BF16)
        VA = [sb(f"VA{p}", [128, NT * NH * VW + 32 - VW]) for p in range(2)]
        PT = [[tmp[i][2 + j][:, 0:L] for j in range(4)] for i in range(2)]
        OS = tmp[0][9][:, 0:L]
        ones_zeros = sb("ones_zeros", [56, L], BF16)
        ones, zero3 = ones_zeros[0:24, :], ones_zeros[32:56, :]
        mx = sb("mx", [128, 2, 16])
        mrow = sb("mrow", [16, 2, 128])
        mres = sb("mres", [16, 2, 128])
        mneg = sb("mneg", [16, 2, 3, 128], BF16)
        rden = sb("rden", [128, 2, NT * 4])
        rt = sb("rt", [128, 2, 3, NT, E_MOE])
        rs = sb("rs", [128, 2, 4, NT])
        cmb = sb("cmb", [128, 2, NT, E_MOE])
        hm = [tmp[0][i][:, 0:L] for i in range(6)]
        sg = [tmp[1][i][:, 0:L] for i in range(3)]
        ye = [tmp[1][3 + i][:, 0:L] for i in range(2)]
        two = [ctx.enter_context(nc.psum_tensor(f"two{i}", [128, 2, L], F32)) for i in range(2)]
        bank = [two[i // 2][:, i % 2, :] for i in range(4)]
        bank += [ctx.enter_context(nc.psum_tensor(f"bank{i}", [128, L], F32))[:, :] for i in range(4, 8)]

        def P(p, i):
            return bank[4 * p + i]

        KHALF, KE, KM1, KPI2, KEPS, KLN = range(6)
        NAMES = ["lam", "one_r", "one_k", "hbx", "hba", "Lh", "ai4", "m", "w", "u1", "dd", "t0", "t1", "t2",
                 "t3", "soft", "y", "gateC", "ir", "om", "z"]
        S_ = {n: i for i, n in enumerate(NAMES)}

        def C(n):
            return sv[:, S_[n]:S_[n] + 1]

        def vc(n):
            return vec[:, V[n]:V[n] + 1]

        def k(i):
            return kc[:, i:i + 1]

        ident = wa[:, WA.index("ident"), :]

        def W(n):
            return wa[:, WA.index(n), :] if n in WA else wb[:, WB.index(n), :]

        def r3(ap):
            return ap.rearrange("p (t c) -> p t c", t=NT)

        ld_t = [sem(f"ld_t{b}") for b in range(B)]
        ld_x = [sem(f"ld_x{b}") for b in range(B)]
        names = """ld_a ld_b ld_c ld_m ld_o ones_row zeroed ones_set consts lam_set mix_set bias_half gates_set soft_u soft_ln soft_s
        log_s decay_set ph_arg ph_trig tab_set th_arg th_trig stats_mv rstd_set ln_done x_turned xf_set
        l0_v l0_q l0_g l0_sg l0_yq l0_yt l0_nt l0_ng l0_z l0_o
        f0_mix f0_xrk f0_k f0_r f0_kk f0_tr f0_v
        g_pre g_xh g_ta g_tx g_mag g_t g_w g_arg g_trig g_xr g_rot g_scan g_hr g_hi g_o g_xb
        f1_ri f1_sq f1_ss f1_rt
        wc_bias wc_set at_qkv at_hi at_mid at_r1 at_parts at_qs at_ks at_mz at_v at_va at_s at_max at_mt at_mrow at_mneg
        at_e at_p at_pv at_os at_ot at_res at_y
        rt_l rt_s rt_e rt_c mo_gu mo_sg mo_h mo_y mo_t mo_acc
        c_in c_g c_t2 c_y c_t
        q_fc q_uv q_um q_uc q_ft q_fe h_pre h_relu h_sqd h_sqp h_o
        dchain achain pchain""".split()
        S = {n: sem(n) for n in names}
        out_dma = [sem(f"out_dma{b}") for b in range(B)]
        at_m = [sem(f"at_m{i}") for i in range(2)]

        def at(b, steps=1):
            return steps * (b + 1)

        def ln_at(n, b):
            return 2 * (LAST + 1) * (b // 2) + 2 * n + b % 2 + 1

        def xf_at(n, b):
            return 2 * (LAST - 1) * (b // 2) + 2 * (n - 1) + b % 2 + 1

        def heads(a):
            return a[:, 0:L].rearrange("p (t h d) -> p t h d", t=NT, h=NH)

        def values(p):
            return VA[p][:, 0:NT * NH * VW].rearrange("p (t h c) -> p t h c", t=NT, h=NH)

        def ids(q):
            return (2 * q, 2 * q + 1)

        block = ctx.enter_context(nc.Block())

        @block.sync
        def _(sp):
            sp.dma_start(x0F[0], xf_d[:, 0, :]).then_inc(ld_x[0], 16)
            sp.dma_start(wa[:, :, :], wa_d).then_inc(S["ld_a"], 16)
            sp.dma_start(vec[:, :], vec_d).then_inc(S["ld_a"], 16)
            sp.dma_start(x0F[1], xf_d[:, 1, :]).then_inc(ld_x[1], 16)
            for b in range(2):
                sp.dma_start(xT[b][:, :], xt_d[:, b, :]).then_inc(ld_t[b], 16)
            sp.dma_start(iota, iota_d).then_inc(S["ld_b"], 16)
            sp.dma_start(wb[:, :, :], wb_d).then_inc(S["ld_b"], 16)
            sp.dma_start(wc[:, :, :], wc_d).then_inc(S["ld_c"], 16)
            sp.dma_start(small[:, :], small_d).then_inc(S["ld_c"], 16)
            sp.dma_start(gu[:, 0, :, :], gu_d[:, 0, :, :]).then_inc(S["ld_m"], 16)
            sp.dma_start(gu[:, 1, :, :], gu_d[:, 1, :, :]).then_inc(S["ld_m"], 16)
            sp.dma_start(dn[:, :, :], dn_d).then_inc(S["ld_m"], 16)
            sp.dma_start(router[:, :], rt_d).then_inc(S["ld_m"], 16)
            sp.dma_start(tri[:, :, :], tri_d).then_inc(S["ld_m"], 16)
            sp.wait_ge(S["ones_row"], 1)
            for p in range(2):
                for hh in range(2):
                    sp.dma_start(KS[p][64 * hh + 48:64 * hh + 51, 8 * hh:8 * hh + 8, :], ones).then_inc(S["ld_o"], 16)
            for q in range(PAIRS):
                if LAST >= 5:
                    if q:
                        for p in range(2):
                            sp.wait_ge(S["at_pv"], NT * (2 * NG * (q - 1) + NG * (p + 1)))
                            for hh in range(2):
                                sp.dma_start(QS[p][64 * hh + 48:64 * hh + 51, 8 * hh:8 * hh + 8, :],
                                             zero3).then_inc(S["at_mz"], 16)
                    for p, b in enumerate(ids(q)):
                        sp.wait_ge(S["at_parts"], at(b))
                        for r, part in enumerate((0, 0, 1, 1, 0, 2)):
                            for hh in range(2):
                                sp.dma_start(QS[p][64 * hh + 8 * r:64 * hh + 8 * r + 8, 8 * hh:8 * hh + 8, :],
                                             parts[64 * hh:64 * hh + 64, 0, part, :]).then_inc(S["at_qs"], 16)
                    for v in range(2 * NG):
                        u = 2 * NG * q + v
                        p, g = v // NG, v % NG
                        sp.wait_ge(S["at_mneg"], u + 1)
                        for hh in range(2):
                            for r in range(3):
                                sp.dma_start(QS[p][64 * hh + 48 + r:64 * hh + 49 + r,
                                                   8 * hh + 2 * g:8 * hh + 2 * g + 2, :],
                                             mneg[8 * hh:8 * hh + 8, v % 2, r, :]).then_inc(at_m[u % 2], 16)
                    for p, b in enumerate(ids(q)):
                        if b + 2 < B:
                            sp.wait_ge(S["stats_mv"], ln_at(5, b))
                            sp.dma_start(x0F[p], xf_d[:, b + 2, :]).then_inc(ld_x[b + 2], 16)
                elif q == 0:
                    for p, b in enumerate(ids(q)):
                        sp.wait_ge(S["ln_done"], ln_at(LAST, b))
                        sp.dma_start(x0F[p], xf_d[:, b + 2, :]).then_inc(ld_x[b + 2], 16)
                for p, b in enumerate(ids(q)):
                    sp.wait_ge(S["ln_done"], ln_at(LAST, b))
                    sp.dma_start(out_d[:, b, :], xT[p][:, :]).then_inc(out_dma[b], 16)
                    if b + 2 < B:
                        sp.wait_ge(out_dma[b], 16)
                        sp.dma_start(xT[p][:, :], xt_d[:, b + 2, :]).then_inc(ld_t[b + 2], 16)
            for n, v in (("ld_a", 32), ("ld_b", 32), ("ld_c", 32), ("ld_m", 80), ("ld_o", 64)):
                sp.wait_ge(S[n], v)
            for b in range(B):
                sp.wait_ge(out_dma[b], 16)

        @block.tensor
        def _(pe):
            def token_major(out, act, w, first=True, last=True, tiles=range(NT)):
                for t in tiles:
                    mm = pe.matmul(out[:, t * 128:(t + 1) * 128], act[:, t * 128:(t + 1) * 128], w,
                                   start=first, stop=last)
                return mm

            def turn(out, src):
                for t in range(NT):
                    mm = pe.transpose(out[:, t * 128:(t + 1) * 128], src[:, t * 128:(t + 1) * 128], ident)
                return mm

            def turn_x(n, q):
                for p, b in enumerate(ids(q) if n < LAST else ()):
                    pe.wait_ge(S["ln_done"], ln_at(n, b))
                    turn(P(p, 3), xT[p]).then_inc(S["x_turned"], 1)

            def l0_attn(q):
                for p, b in enumerate(ids(q)):
                    pe.wait_ge(ld_x[b], 16)
                    if b == 0:
                        pe.wait_ge(S["ld_a"], 32)
                    if q:
                        pe.wait_ge(S["stats_mv"], ln_at(LAST, b - 2))
                    pe.matmul(P(p, 1)[:, :], W("l0_v"), x0F[p], start=True, stop=True).then_inc(S["l0_v"], 1)
                    pe.matmul(P(p, 0)[:, :], W("l0_q"), x0F[p], start=True, stop=True).then_inc(S["l0_q"], 1)
                    pe.matmul(P(p, 2)[:, :], W("l0_g"), x0F[p], start=True, stop=True).then_inc(S["l0_g"], 1)
                for p, b in enumerate(ids(q)):
                    pe.wait_ge(S["l0_yq"], at(b))
                    turn(P(p, 3), tmp[p][1]).then_inc(S["l0_yt"], 1)
                for p, b in enumerate(ids(q)):
                    pe.wait_ge(S["ln_done"], ln_at(0, b))
                    turn(P(p, 0), tmp[p][3]).then_inc(S["l0_nt"], 1)
                for p, b in enumerate(ids(q)):
                    pe.wait_ge(S["l0_z"], at(b))
                    token_major(P(p, 1), tmp[p][5], W("l0_o")).then_inc(S["l0_o"], 1)

            def l0_ffn(q):
                for p, b in enumerate(ids(q)):
                    if b == 0:
                        pe.wait_ge(S["ld_b"], 32)
                    pe.wait_ge(S["f0_xrk"], at(b))
                    pe.matmul(P(p, 1)[:, :], W("f0_k"), tmp[p][3][:, 0:L], start=True, stop=True).then_inc(S["f0_k"], 1)
                    token_major(P(p, 0), tmp[p][2], W("f0_r")).then_inc(S["f0_r"], 1)
                for p, b in enumerate(ids(q)):
                    pe.wait_ge(S["f0_kk"], at(b))
                    token_major(P(p, 2), tmp[p][5], W("f0_v")).then_inc(S["f0_v"], 1)

            def gate_weights():
                pe.wait_ge(S["ld_b"], 32)
                for i, (w0, w1) in enumerate((("bdx0", "bdx1"), ("bda0", "bda1"))):
                    pe.matmul(P(0, 3)[:, i * 128:(i + 1) * 128], W("inT0"), W(w0), start=True, stop=False)
                    pe.matmul(P(0, 3)[:, i * 128:(i + 1) * 128], W("inT1"), W(w1), start=False, stop=True)
                    pe.matmul(P(0, 3)[:, 256 + i:257 + i], W(w0), vc("b_re"), start=True, stop=False)
                    mm = pe.matmul(P(0, 3)[:, 256 + i:257 + i], W(w1), vc("b_im"), start=False, stop=True)
                mm.then_inc(S["wc_bias"], 1)

            def l1_attn(q):
                for p, b in enumerate(ids(q)):
                    pe.wait_ge(S["xf_set"], xf_at(2, b))
                    if b == 0:
                        pe.wait_ge(S["wc_set"], 2)
                    x = xF[p][:, 1:1 + L]
                    pe.matmul(P(p, 3)[:, :], wga[:, :], x, start=True, stop=True).then_inc(S["g_pre"], 1)
                    pe.matmul(P(p, 2)[:, :], wgx[:, :], x, start=True, stop=True).then_inc(S["g_pre"], 1)
                    pe.matmul(P(p, 0)[:, :], W("in_re"), x, start=True, stop=True)
                    pe.matmul(P(p, 1)[:, :], W("in_im"), x, start=True, stop=True).then_inc(S["g_xh"], 1)
                for p, b in enumerate(ids(q)):
                    pe.wait_ge(S["g_hr"], at(b))
                    pe.wait_ge(S["g_hi"], at(b))
                    for t in range(NT):
                        token_major(P(p, 2), tmp[p][5], W("out0"), last=False, tiles=[t])
                        mm = token_major(P(p, 2), tmp[p][8], W("out1"), first=False, tiles=[t])
                    mm.then_inc(S["g_o"], 1)

            def l1_ffn(q):
                for p, b in enumerate(ids(q)):
                    pe.wait_ge(S["xf_set"], xf_at(3, b))
                    if b == 0:
                        pe.wait_ge(S["th_trig"], 2)
                    x = xF[p][:, 1:1 + L]
                    token_major(P(p, 0), x, w_cos[:, :])
                    token_major(P(p, 1), x, w_sin[:, :]).then_inc(S["f1_ri"], 1)

            def l2_attn(q):
                for p, b in enumerate(ids(q)):
                    pe.wait_ge(S["xf_set"], xf_at(4, b))
                    x = xF[p][:, 1:1 + L]
                    pe.matmul(P(p, 0)[:, :], W("a_q"), x, start=True, stop=True)
                    pe.matmul(P(p, 1)[:, :], W("a_k"), x, start=True, stop=True).then_inc(S["at_qkv"], 1)
                    token_major(P(p, 2), x, W("a_v")).then_inc(S["at_v"], 1)

                u0 = 2 * NG * q

                def stack(arr, j, g):
                    return arr[:, 8 * (j % 2) + 2 * g + j // 2, :]

                def score_tile(u, i):
                    v = u - u0
                    p, g = v // NG, v % NG
                    n = 8 * u + i
                    jj, qt = i % 2, i // 2
                    if i == 0 and u == 0:
                        pe.wait_ge(S["ld_o"], 64)
                    if i == 0 and v == 0 and q:
                        pe.wait_ge(S["at_mz"], 64)
                    if i == 0 and g == 0:
                        pe.wait_ge(S["at_qs"], 16 * 12 * (2 * q + p + 1))
                        pe.wait_ge(S["at_ks"], 16 * 12 * (2 * q + p + 1))
                    if n >= 2:
                        pe.wait_ge(S["at_max"], n - 1)
                    for s in range(2):
                        j = 2 * jj + s
                        mm = pe.matmul(bank[2 * (i % 2) + s][:, :],
                                       stack(QS[p], j, g)[:, qt * 128:(qt + 1) * 128],
                                       stack(KS[p], j, g), start=True, stop=True)
                    mm.then_inc(S["at_s"], 1)

                def turn_max(u):
                    pe.wait_ge(S["at_max"], 8 * (u + 1))
                    if u > 2:
                        pe.wait_ge(S["at_res"], max(u - 2, u0))
                    pe.transpose(bank[7][0:16, 0:128], mx[:, u % 2, :], ident).then_inc(S["at_mt"], 1)

                def exp_tile(u, i):
                    v = u - u0
                    p, g = v // NG, v % NG
                    kt, j = i // 4, i % 4
                    n = 16 * u + i
                    if i == 0:
                        pe.wait_ge(at_m[u % 2], 16 * 6 * (u // 2 + 1))
                    if n >= 2:
                        pe.wait_ge(S["at_p"], n - 1)
                    pe.matmul(bank[4 + i % 2][:, :], stack(KS[p], j, g)[:, kt * 128:(kt + 1) * 128],
                              stack(QS[p], j, g), start=True, stop=True).then_inc(S["at_e"], 1)

                def weigh(u, kt):
                    v = u - u0
                    p, g = v // NG, v % NG
                    if kt == 0:
                        if u:
                            pe.wait_ge(S["at_os"], u)
                        if g == 0:
                            pe.wait_ge(S["at_va"], 2 * q + p + 1)
                    pe.wait_ge(S["at_p"], 16 * u + 4 * kt + 4)
                    for j in range(4):
                        c = (kt * NH + 4 * g + j) * VW
                        mm = pe.matmul(bank[6][32 * j:32 * j + 32, :], VA[p][:, c:c + 32], PT[kt % 2][j],
                                       start=(kt == 0), stop=(kt == NT - 1))
                    mm.then_inc(S["at_pv"], 1)

                def turn_out(u):
                    pe.wait_ge(S["at_os"], u + 1)
                    pe.wait_ge(S["at_mrow"], min(u + 3, u0 + 2 * NG))
                    if u > u0:
                        pe.wait_ge(S["at_res"], u)
                    turn(bank[7], OS).then_inc(S["at_ot"], 1)

                pe.wait_ge(S["at_r1"], at(2 * q + 1, 2))
                pe.wait_ge(S["at_va"], 2 * q + 2)
                for i in range(8):
                    score_tile(u0, i)
                for i in range(8):
                    score_tile(u0 + 1, i)
                    if i == 1:
                        turn_max(u0)
                for v in range(2 * NG):
                    u = u0 + v
                    for i in range(8):
                        if v + 2 < 2 * NG:
                            score_tile(u + 2, i)
                        exp_tile(u, 2 * i)
                        exp_tile(u, 2 * i + 1)
                        if i in (2, 4, 6):
                            weigh(u, i // 2 - 1)
                        elif i == 0 and v:
                            weigh(u - 1, 3)
                        if i == 1 and v + 1 < 2 * NG:
                            turn_max(u + 1)
                        if i == 4 and v:
                            turn_out(u - 1)
                weigh(u0 + 2 * NG - 1, 3)
                turn_out(u0 + 2 * NG - 1)

            def moe(q):
                if q == 0:
                    pe.wait_ge(S["ld_m"], 80)
                for p, b in enumerate(ids(q)):
                    pe.wait_ge(S["xf_set"], xf_at(5, b))
                    for t in range(NT):
                        mm = pe.matmul(bank[6 + p][:, t * E_MOE:(t + 1) * E_MOE],
                                       xF[p][:, 1 + t * 128:1 + (t + 1) * 128], router[:, :], start=True, stop=True)
                    mm.then_inc(S["rt_l"], 1)

                def up(p, b, e):
                    for m, (c0, cn) in enumerate(MT):
                        n = 3 * (E_MOE * b + e) + m
                        if n >= 3:
                            pe.wait_ge(S["mo_h"], n - 2)
                        for s in range(2):
                            mm = pe.matmul(bank[2 * (n % 3) + s][0:cn, :], gu[:, s, e, c0:c0 + cn],
                                           xF[p][:, 1:1 + L], start=True, stop=True)
                        mm.then_inc(S["mo_gu"], 1)

                def down(p, b, e):
                    n = E_MOE * b + e
                    pe.wait_ge(S["mo_h"], 3 * n + 3)
                    if n >= 2:
                        pe.wait_ge(S["mo_t"], n - 1)
                    for t in range(NT):
                        for m, (c0, cn) in enumerate(MT):
                            mm = pe.matmul(bank[6 + e % 2][:, t * 128:(t + 1) * 128],
                                           hm[3 * (e % 2) + m][0:cn, t * 128:(t + 1) * 128],
                                           dn[0:cn, 3 * e + m, :], start=(m == 0), stop=(m == 2))
                    mm.then_inc(S["mo_y"], 1)

                work = [(p, b, e) for p, b in enumerate(ids(q)) for e in range(E_MOE)]
                for i, w in enumerate(work):
                    up(*w)
                    if i == 0:
                        pe.wait_ge(S["rt_s"], at(2 * q + 1))
                    if i:
                        down(*work[i - 1])
                down(*work[-1])

            def l3_attn(q):
                for p, b in enumerate(ids(q)):
                    pe.wait_ge(S["c_y"], at(b))
                    turn(P(p, 0), tmp[p][4]).then_inc(S["c_t"], 1)

            def last_weights():
                pe.wait_ge(S["ld_c"], 32)
                pe.matmul(P(0, 0)[0:RANK, 0:128], small[:, HID + 128:HID + 128 + RANK],
                          small[:, HID:HID + 128], start=True, stop=True).then_inc(S["q_um"], 1)
                pe.wait_ge(S["q_uc"], 1)
                pe.matmul(P(0, 1)[:, :], uT_m[:, :], small[:, 0:HID], start=True, stop=True).then_inc(S["q_uv"], 1)
                pe.wait_ge(S["q_fc"], 2)
                turn(P(0, 2), wq_s[0])
                turn(P(0, 3), wq_s[1]).then_inc(S["q_ft"], 1)

            def l3_ffn(q):
                for p, b in enumerate(ids(q)):
                    pe.wait_ge(S["xf_set"], xf_at(7, b))
                    if b == 0:
                        pe.wait_ge(S["q_fe"], 1)
                    for m in range(4):
                        pe.matmul(P(p, m)[:, :], fcT[:, m * 128:(m + 1) * 128], xF[p][:, 1:1 + L],
                                  start=True, stop=True).then_inc(S["h_pre"], 1)
                for p, b in enumerate(ids(q)):
                    pe.wait_ge(S["h_sqd"], at(b, 2))
                    pe.wait_ge(S["h_sqp"], at(b, 2))
                    for t in range(NT):
                        for m in range(4):
                            mm = token_major(P(p, 0), tmp[p][4 + m], pjT[:, m * 128:(m + 1) * 128],
                                             first=(m == 0), last=(m == 3), tiles=[t])
                    mm.then_inc(S["h_o"], 1)

            for q in range(PAIRS):
                l0_attn(q)
                if q == 0 and LAST >= 3:
                    pass
                turn_x(1, q)
                if LAST >= 2:
                    l0_ffn(q)
                    turn_x(2, q)
                if LAST >= 3:
                    if q == 0:
                        pe.wait_ge(S["xf_set"], xf_at(2, 0))
                        gate_weights()
                    l1_attn(q)
                    turn_x(3, q)
                if LAST >= 4:
                    l1_ffn(q)
                    turn_x(4, q)
                if LAST >= 5:
                    l2_attn(q)
                    turn_x(5, q)
                if LAST >= 6:
                    moe(q)
                    turn_x(6, q)
                if LAST >= 7:
                    l3_attn(q)
                    turn_x(7, q)
                if LAST >= 8:
                    if q == 0:
                        pe.wait_ge(S["xf_set"], xf_at(7, 0))
                        last_weights()
                    l3_ffn(q)

        @block.scalar
        def _(act):
            n_chain = [0]

            def link(ins):
                n_chain[0] += 1
                ins.then_inc(S["achain"], 1)
                act.wait_ge(S["achain"], n_chain[0])

            def put_x(n, q):
                for p, b in enumerate(ids(q) if n < LAST else ()):
                    act.wait_ge(S["x_turned"], xf_at(n, b))
                    if n == 1 and b == 0:
                        act.wait_ge(S["zeroed"], 1)
                    act.activation(xF[p][:, 1:1 + L], P(p, 3)[:, :], ACT.Copy).then_inc(S["xf_set"], 1)

            act.wait_ge(S["consts"], 1)
            act.wait_ge(S["th_arg"], 1)
            act.activation(w_cos[:, :], stmp[:, 0, :], ACT.Sin, scale=-TURN, bias=k(KPI2)).then_inc(S["th_trig"], 1)
            act.activation(w_sin[:, :], stmp[:, 1, :], ACT.Sin, scale=-TURN).then_inc(S["th_trig"], 1)

            for q in range(PAIRS):
                for p, b in enumerate(ids(q)):
                    act.wait_ge(S["l0_g"], at(b))
                    act.activation(tmp[p][2][:, 0:L], P(p, 2)[:, :], ACT.Silu).then_inc(S["l0_sg"], 1)
                for p, b in enumerate(ids(q)):
                    act.wait_ge(S["l0_nt"], at(b))
                    act.activation(tmp[p][4][:, 0:L], P(p, 0)[:, :], ACT.Identity, scale=vc("gamma"),
                                   bias=vc("lnb")).then_inc(S["l0_ng"], 1)
                put_x(1, q)
                if LAST >= 2:
                    for p, b in enumerate(ids(q)):
                        if b == 0:
                            act.wait_ge(S["mix_set"], 1)
                        act.wait_ge(S["xf_set"], xf_at(1, b))
                        act.activation(tmp[p][0][:, :], xF[p][:, :], ACT.Copy, scale=C("one_k"))
                        act.activation(tmp[p][1][:, :], xF[p][:, :], ACT.Copy, scale=C("one_r")).then_inc(S["f0_mix"], 1)
                    for p, b in enumerate(ids(q)):
                        act.wait_ge(S["f0_k"], at(b))
                        link(act.activation(tmp[p][4][:, 0:L], P(p, 1)[:, :], ACT.Relu))
                        act.activation(tmp[p][5][:, 0:L], tmp[p][4][:, 0:L], ACT.Square).then_inc(S["f0_kk"], 1)
                    for p, b in enumerate(ids(q)):
                        act.wait_ge(S["f0_r"], at(b))
                        act.activation(tmp[p][6][:, 0:L], P(p, 0)[:, :], ACT.Tanh, scale=0.5).then_inc(S["f0_tr"], 1)
                    put_x(2, q)
                if LAST >= 3:
                    if q == 0:
                        act.wait_ge(S["bias_half"], 1)
                        act.activation(wgx[:, :], P(0, 3)[:, 0:128], ACT.Copy).then_inc(S["wc_set"], 1)
                        act.activation(wga[:, :], P(0, 3)[:, 128:256], ACT.Copy).then_inc(S["wc_set"], 1)
                    for p, b in enumerate(ids(q)):
                        act.wait_ge(S["g_pre"], at(b, 2))
                        act.activation(tmp[p][0][:, 0:L], P(p, 3)[:, :], ACT.Tanh, scale=0.5,
                                       bias=C("hba")).then_inc(S["g_ta"], 1)
                        act.activation(tmp[p][1][:, 0:L], P(p, 2)[:, :], ACT.Tanh, scale=0.5,
                                       bias=C("hbx")).then_inc(S["g_tx"], 1)
                    act.preload_act_table_set("natural_log_exp_and_others")
                    if q == 0:
                        act.wait_ge(S["soft_u"], 1)
                        act.activation(C("t0"), C("u1"), ACT.Ln).then_inc(S["soft_ln"], 1)
                        act.wait_ge(S["soft_s"], 1)
                        act.activation(C("y"), C("t3"), ACT.Ln).then_inc(S["log_s"], 1)
                        act.wait_ge(S["gates_set"], 1)
                    for p, b in enumerate(ids(q)):
                        act.wait_ge(S["g_ta"], at(b))
                        act.activation(tmp[p][2][:, 0:L], tmp[p][0][:, 0:L], ACT.Exp, scale=C("Lh"),
                                       bias=C("Lh")).then_inc(S["g_mag"], 1)
                    for p, b in enumerate(ids(q)):
                        act.wait_ge(S["g_t"], at(b))
                        link(act.activation(tmp[p][3][:, 0:L], tmp[p][3][:, 0:L], ACT.Ln))
                        act.activation(tmp[p][3][:, 0:L], tmp[p][3][:, 0:L], ACT.Exp, scale=0.5,
                                       bias=k(KLN)).then_inc(S["g_w"], 1)
                    for p, b in enumerate(ids(q)):
                        act.wait_ge(S["g_arg"], at(b))
                        act.activation(tmp[p][7][:, 0:L], tmp[p][5][:, 0:L], ACT.Sin, scale=-TURN)
                        act.activation(tmp[p][8][:, 0:L], tmp[p][6][:, 0:L], ACT.Sin, scale=-TURN,
                                       bias=k(KPI2)).then_inc(S["g_trig"], 1)
                    put_x(3, q)
                if LAST >= 4:
                    for p, b in enumerate(ids(q)):
                        act.wait_ge(S["f1_ri"], at(b))
                        act.activation(tmp[p][0][:, 0:L], P(p, 0)[:, :], ACT.Square)
                        act.activation(tmp[p][1][:, 0:L], P(p, 1)[:, :], ACT.Square).then_inc(S["f1_sq"], 1)
                    for p, b in enumerate(ids(q)):
                        act.wait_ge(S["f1_ss"], at(b))
                        act.activation(tmp[p][3][:, 0:L], tmp[p][2][:, 0:L], ACT.Sqrt).then_inc(S["f1_rt"], 1)
                    put_x(4, q)
                if LAST >= 5:
                    for p, b in enumerate(ids(q)):
                        act.wait_ge(S["at_qkv"], at(b))
                        if b:
                            act.wait_ge(S["at_qs"], 16 * 12 * b)
                            act.wait_ge(S["at_ks"], 16 * 12 * b)
                        for side in range(2):
                            act.activation(parts[:, side, 0, :], P(p, side)[:, :], ACT.Copy).then_inc(S["at_hi"], 1)
                        for side in range(2):
                            act.wait_ge(S["at_r1"], at(b, 2) - 1 + side)
                            act.activation(parts[:, side, 1, :], tmp[p][side][:, 0:L], ACT.Copy).then_inc(S["at_mid"], 1)
                        act.wait_ge(S["at_v"], at(b))
                        if b == 0:
                            act.wait_ge(S["ones_set"], 1)
                        act.activation(values(p)[:, :, :, 0:HD], heads(P(p, 2)), ACT.Copy).then_inc(S["at_va"], 1)
                    u0 = 2 * NG * q

                    def take_out(u):
                        act.wait_ge(S["at_pv"], NT * (u + 1))
                        if u:
                            act.wait_ge(S["at_ot"], u)
                        act.activation(OS, bank[6][:, :], ACT.Copy).then_inc(S["at_os"], 1)

                    act.preload_act_table_set("exp_and_others")
                    for u in range(u0, u0 + 2 * NG):
                        for i in range(16):
                            n = 16 * u + i
                            act.wait_ge(S["at_e"], n + 1)
                            if n >= 8 and i % 4 == 0:
                                act.wait_ge(S["at_pv"], n // 4 - 1)
                            act.activation(PT[(i // 4) % 2][i % 4], bank[4 + i % 2][:, :], ACT.Exp,
                                           scale=float(HD) ** -0.5).then_inc(S["at_p"], 1)
                            if i == 2 and u > u0:
                                take_out(u - 1)
                    take_out(u0 + 2 * NG - 1)
                    put_x(5, q)
                if LAST >= 6:
                    for p, b in enumerate(ids(q)):
                        act.wait_ge(S["rt_s"], at(b))
                        act.activation(rt[:, p, 1, :, :], rt[:, p, 0, :, :], ACT.Exp).then_inc(S["rt_e"], 1)
                    for p, b in enumerate(ids(q)):
                        for e in range(E_MOE):
                            for m, (c0, cn) in enumerate(MT):
                                n = 3 * (E_MOE * b + e) + m
                                if n == 6:
                                    act.wait_ge(S["ph_arg"], 1)
                                    act.activation(tt[0], tab[:, 0, :], ACT.Sin, scale=-TURN)
                                    act.activation(tt[1], tab[:, 1, :], ACT.Sin, scale=-TURN,
                                                   bias=k(KPI2)).then_inc(S["ph_trig"], 1)
                                act.wait_ge(S["mo_gu"], n + 1)
                                if n >= 3:
                                    act.wait_ge(S["mo_h"], n - 2)
                                act.activation(sg[n % 3][0:cn, :], bank[2 * (n % 3)][0:cn, :],
                                               ACT.Silu).then_inc(S["mo_sg"], 1)
                    put_x(6, q)
                if LAST >= 7:
                    put_x(7, q)
                if LAST >= 8:
                    if q == 0:
                        act.wait_ge(S["q_um"], 1)
                        act.activation(uT_m[:, :], P(0, 0)[0:RANK, 0:128], ACT.Copy).then_inc(S["q_uc"], 1)
                        act.wait_ge(S["q_ft"], 1)
                        act.activation(pjT[:, :], P(0, 3)[:, :], ACT.Copy).then_inc(S["q_ft"], 1)
                    for p, b in enumerate(ids(q)):
                        for m in range(4):
                            act.wait_ge(S["h_pre"], 4 * b + m + 1)
                            act.activation(tmp[p][m][:, 0:L], P(p, m)[:, :], ACT.Relu).then_inc(S["h_relu"], 1)

        @block.gpsimd
        def _(pool):
            n_chain = [0]

            def link(ins):
                n_chain[0] += 1
                ins.then_inc(S["pchain"], 1)
                pool.wait_ge(S["pchain"], n_chain[0])

            def ts(out, a, s1, op0, s2=None, op1=None):
                if op1 is None:
                    return pool.tensor_scalar(out, a, s1, None, op0)
                return pool.tensor_scalar(out, a, s1, s2, op0, op1)

            def tten(out, a, b_, op):
                return pool.tensor_tensor(out, a, b_, op)

            def norm_scale(n, q):
                for p, b in enumerate(ids(q)):
                    pool.wait_ge(S["stats_mv"], ln_at(n, b))
                    link(ts(rstd[:, p, :], mv[:, p, :, 1], EPS, ADD))
                    tten(rstd[:, p, :], rstd[:, p, :], k(KHALF).to_broadcast([128, NT]), ALU.pow).then_inc(S["rstd_set"], 1)

            for i, v in ((KHALF, -0.5), (KE, 2.718281828459045), (KM1, -1.0), (KPI2, PI_2),
                         (KEPS, EPS), (KLN, -0.6931471805599453)):
                last = pool.memset(k(i), v)
            link(last)
            pool.wait_ge(S["ld_a"], 32)
            link(ts(C("lam"), vc("beta"), -1.0, MUL))
            link(tten(C("lam"), k(KE), C("lam"), ALU.pow))
            link(ts(C("lam"), C("lam"), 1.0, ADD))
            tten(C("lam"), C("lam"), k(KM1), ALU.pow).then_inc(S["lam_set"], 1)
            pool.memset(xF[0][:, 0:1], 0.0)
            pool.memset(xF[1][:, 0:1], 0.0).then_inc(S["zeroed"], 1)
            ts(C("one_r"), vc("mu_r"), -1.0, MUL, 1.0, ADD)
            ts(C("one_k"), vc("mu_k"), -1.0, MUL, 1.0, ADD).then_inc(S["mix_set"], 1)
            ts(C("ai4"), vc("a_im"), 0.25, MUL)
            pool.memset(C("t3"), 0.0).then_inc(S["consts"], 1)
            pool.wait_ge(S["ld_b"], 32)
            tten(stmp[:, 0, :], W("th"), W("thn"), ADD)
            link(tten(stmp[:, 1, :], W("phi"), W("phin"), ADD))
            link(ts(stmp[:, :, :], stmp[:, :, :], 1.0 / 6.283185307179586, MUL))
            ts(w_cos[:, :], stmp[:, 0, :], 0.25, ADD, MAGIC, ADD)
            link(ts(w_sin[:, :], stmp[:, 1, :], MAGIC, ADD))
            ts(w_cos[:, :], w_cos[:, :], MAGIC, SUB)
            link(ts(w_sin[:, :], w_sin[:, :], MAGIC, SUB))
            tten(stmp[:, 0, :], w_cos[:, :], stmp[:, 0, :], SUB)
            tten(stmp[:, 1, :], w_sin[:, :], stmp[:, 1, :], SUB).then_inc(S["th_arg"], 1)

            def ones_columns():
                link(pool.memset(QS[0][:, :, :].bitcast(F32), 0.0))
                link(pool.memset(ones_zeros[:, :], 0.0))
                link(pool.memset(ones, 1.0))
                for rows in (QS[1], KS[0], KS[1]):
                    last = pool.memset(rows[:, :, :].bitcast(F32), 0.0)
                last.then_inc(S["ones_row"], 1)
                for p in range(2):
                    pool.memset(VA[p][:, NT * NH * VW:], 0.0)
                    last = pool.memset(values(p)[:, :, :, HD:VW], 1.0)
                last.then_inc(S["ones_set"], 1)

            def soft():
                a = vc("a_re")
                link(ts(C("w"), a, -1.0, MUL))
                link(ts(C("w"), C("w"), a, ALU.min))
                link(tten(C("w"), k(KE), C("w"), ALU.pow))
                link(ts(C("u1"), C("w"), 1.0, ADD))
                ts(C("dd"), C("u1"), -1.0, ADD).then_inc(S["soft_u"], 1)
                pool.wait_ge(S["soft_u"], 1)
                link(ts(C("t1"), C("dd"), 0.0, ALU.is_equal))
                pool.wait_ge(S["soft_ln"], 1)
                link(ts(C("t2"), C("t0"), -1.0, MUL))
                link(tten(C("t2"), k(KE), C("t2"), ALU.pow))
                link(tten(C("t2"), C("t2"), C("u1"), MUL))
                link(ts(C("t2"), C("t2"), -1.0, ADD))
                link(tten(C("t0"), C("t0"), C("t2"), ADD))
                link(tten(C("t0"), C("t0"), C("t1"), ADD))
                link(tten(C("t0"), C("t0"), C("w"), MUL))
                link(tten(C("dd"), C("dd"), C("t1"), ADD))
                link(tten(C("dd"), C("dd"), k(KM1), ALU.pow))
                link(tten(C("t0"), C("t0"), C("dd"), MUL))
                link(ts(C("soft"), a, 0.0, MAX))
                link(tten(C("soft"), C("soft"), C("t0"), ADD))
                link(ts(C("t3"), C("soft"), 1e-19, MAX))
                pool.memset(C("z"), 0.0).then_inc(S["soft_s"], 1)
                pool.wait_ge(S["log_s"], 1)
                link(ts(C("t2"), C("y"), -1.0, MUL))
                link(tten(C("t2"), k(KE), C("t2"), ALU.pow))
                link(tten(C("t2"), C("t2"), C("t3"), MUL))
                link(ts(C("t2"), C("t2"), -1.0, ADD))
                link(tten(C("y"), C("y"), C("t2"), ADD))
                link(ts(C("t1"), a, -40.0, ALU.is_lt))
                link(tten(C("t2"), a, C("y"), SUB))
                link(tten(C("t2"), C("t2"), C("t1"), MUL))
                link(tten(C("y"), C("y"), C("t2"), ADD))
                ts(C("Lh"), C("y"), 0.5, MUL).then_inc(S["gates_set"], 1)

            def tables_arg():
                link(tten(C("z"), k(KE), vc("ph_ln"), ALU.pow))
                link(tten(C("z"), C("z"), vc("ph_sc"), MUL))
                link(ts(C("z"), C("z"), -1.0, MUL))
                link(tten(C("m"), k(KE), C("z"), ALU.pow))
                link(ts(C("gateC"), C("m"), -1.0, MUL, 1.0, ADD))
                link(tten(C("om"), vc("ph_ang"), vc("ph_sc"), MUL))
                link(ts(C("om"), C("om"), 1.0 / 6.283185307179586, MUL))
                link(ts(tt[0], iota, C("om"), MUL))
                ts(tab[:, 0, :], tt[0], MAGIC, ADD)
                link(ts(tab[:, 1, :], tt[0], 0.25, ADD, MAGIC, ADD))
                link(ts(tab[:, 0:2, :], tab[:, 0:2, :], MAGIC, SUB))
                tten(tab[:, 0, :], tab[:, 0, :], tt[0], SUB)
                link(tten(tab[:, 1, :], tab[:, 1, :], tt[0], SUB))
                ts(C("ir"), vc("ph_im"), -1.0, MUL).then_inc(S["ph_arg"], 1)

            def tables():
                pool.wait_ge(S["ph_trig"], 1)
                sn, cs = tt[0], tt[1]
                ts(tab[:, 0, :], sn, vc("ph_im"), MUL)
                ts(tab[:, 1, :], cs, vc("ph_im"), MUL)
                ts(tab[:, 2, :], cs, vc("ph_re"), MUL)
                link(ts(tab[:, 3, :], sn, vc("ph_re"), MUL))
                tten(tab[:, 0, :], tab[:, 0, :], tab[:, 2, :], ADD)
                link(tten(tab[:, 1, :], tab[:, 1, :], tab[:, 3, :], SUB))
                ts(tab[:, 2, :], cs, C("gateC"), MUL)
                ts(tab[:, 3, :], sn, C("gateC"), MUL).then_inc(S["tab_set"], 1)

            ones_columns()
            for q in range(PAIRS):
                norm_scale(0, q)
                norm_scale(1, q)
                if LAST >= 2:
                    norm_scale(2, q)
                if LAST >= 3:
                    if q == 0:
                        soft()
                    for p, b in enumerate(ids(q)):
                        pool.wait_ge(S["ln_done"], ln_at(2, b))
                        tten(r3(tmp[p][9][:, 0:L]), r3(xT[p][:, :]),
                             W("b_out").unsqueeze(1).broadcast_to([128, NT, 128]), ADD).then_inc(S["g_xb"], 1)
                    for p, b in enumerate(ids(q)):
                        pool.wait_ge(S["g_mag"], at(b))
                        t = tmp[p][3][:, 0:L]
                        link(tten(t, tmp[p][2][:, 0:L], tmp[p][2][:, 0:L], MUL))
                        link(ts(t, t, -1.0, MUL, 1.0, ADD))
                        ts(t, t, 1e-6, MAX).then_inc(S["g_t"], 1)
                    for p, b in enumerate(ids(q)):
                        pool.wait_ge(S["g_xr"], at(b))
                        a_, b_ = tmp[p][5][:, 0:L], tmp[p][6][:, 0:L]
                        tten(a_, tmp[p][1][:, 0:L], tmp[p][8][:, 0:L], MUL)
                        link(tten(b_, tmp[p][0][:, 0:L], tmp[p][7][:, 0:L], MUL))
                        tten(a_, a_, b_, SUB).then_inc(S["g_rot"], 1)
                    for p, b in enumerate(ids(q)):
                        pool.wait_ge(S["g_scan"], at(b))
                        a_, b_ = tmp[p][1][:, 0:L], tmp[p][6][:, 0:L]
                        tten(a_, tmp[p][7][:, 0:L], tmp[p][3][:, 0:L], MUL)
                        link(tten(b_, tmp[p][8][:, 0:L], tmp[p][4][:, 0:L], MUL))
                        pool.wait_ge(S["g_hr"], at(b))
                        tten(tmp[p][8][:, 0:L], a_, b_, ADD).then_inc(S["g_hi"], 1)
                    norm_scale(3, q)
                if LAST >= 4:
                    for p, b in enumerate(ids(q)):
                        pool.wait_ge(S["f1_sq"], at(b))
                        tten(tmp[p][2][:, 0:L], tmp[p][0][:, 0:L], tmp[p][1][:, 0:L], ADD).then_inc(S["f1_ss"], 1)
                    norm_scale(4, q)
                if LAST >= 5:
                    for p, b in enumerate(ids(q)):
                        pool.wait_ge(S["at_parts"], at(b))
                        for r, part in enumerate((0, 1, 0, 1, 2, 0)):
                            for hh in range(2):
                                pool.dma_start(KS[p][64 * hh + 8 * r:64 * hh + 8 * r + 8, 8 * hh:8 * hh + 8, :],
                                               parts[64 * hh:64 * hh + 64, 1, part, :]).then_inc(S["at_ks"], 16)
                    u0 = 2 * NG * q

                    def negate(u):
                        v = u % 2
                        pool.wait_ge(S["at_mrow"], u + 1)
                        if u >= 2:
                            pool.wait_ge(at_m[v], 16 * 6 * (u // 2))
                        ts(mneg[:, v, 0, :], mrow[:, v, :], -1.0, MUL)
                        link(ts(mres[:, v, :], mrow[:, v, :], -1.0, MUL))
                        link(tten(mres[:, v, :], mres[:, v, :], mneg[:, v, 0, :], SUB))
                        link(pool.tensor_copy(mneg[:, v, 1, :], mres[:, v, :]))
                        tten(mneg[:, v, 2, :], mres[:, v, :], mneg[:, v, 1, :], SUB).then_inc(S["at_mneg"], 1)

                    for u in range(u0, u0 + 2 * NG):
                        negate(u)
                    norm_scale(5, q)
                if LAST >= 6:
                    if q == 0:
                        pool.wait_ge(S["ln_done"], ln_at(5, 1))
                        tables_arg()
                    for p, b in enumerate(ids(q)):
                        for e in range(E_MOE):
                            n = E_MOE * b + e
                            if q == 0 and n == 4:
                                tables()
                            pool.wait_ge(S["mo_t"], n + 1)
                            other = xT[p] if e == 0 else Y[p]
                            if e:
                                pool.wait_ge(S["mo_acc"], n)
                            tten(Y[p][:, :], ye[e % 2], other[:, :], ADD).then_inc(S["mo_acc"], 1)
                    norm_scale(6, q)
                if LAST >= 7:
                    for p, b in enumerate(ids(q)):
                        pool.wait_ge(S["xf_set"], xf_at(6, b))
                        tten(tmp[p][0][:, 0:L], xF[p][:, 1:1 + L], tab[:, 0, :], MUL).then_inc(S["c_in"], 1)
                    for p, b in enumerate(ids(q)):
                        pool.wait_ge(S["c_g"], at(b, 2))
                        tten(tmp[p][5][:, 0:L], tmp[p][3][:, 0:L], tab[:, 3, :], MUL).then_inc(S["c_t2"], 1)
                    norm_scale(7, q)
                if LAST >= 8:
                    for p, b in enumerate(ids(q)):
                        for m in (1, 3):
                            pool.wait_ge(S["h_relu"], 4 * b + m + 1)
                            tten(tmp[p][4 + m][:, 0:L], tmp[p][m][:, 0:L], tmp[p][m][:, 0:L], MUL).then_inc(S["h_sqp"], 1)
                    norm_scale(8, q)

        @block.vector
        def _(dve):
            n_chain = [0]

            def link(ins):
                n_chain[0] += 1
                ins.then_inc(S["dchain"], 1)
                dve.wait_ge(S["dchain"], n_chain[0])

            def stt(out, a, s, b_, op0, op1):
                return dve.scalar_tensor_tensor(out, a, s, b_, op0, op1)

            def tt_(out, a, b_, op):
                return dve.tensor_tensor(out, a, b_, op)

            def ts(out, a, s1, op0, s2=None, op1=None):
                if op1 is None:
                    return dve.tensor_scalar(out, a, s1, None, op0)
                return dve.tensor_scalar(out, a, s1, s2, op0, op1)

            def stats(p, src):
                for t in range(NT):
                    last = dve.bn_stats(st6[:, p, t, :], src[:, t * 128:(t + 1) * 128])
                link(last)
                for t in range(NT):
                    last = dve.bn_aggr(mv[:, p, t, :], st6[:, p, t, :])
                last.then_inc(S["stats_mv"], 1)

            def scale_rows(n, p, b, dst, src):
                dve.wait_ge(S["rstd_set"], ln_at(n, b))
                for t in range(NT):
                    last = ts(dst[:, t * 128:(t + 1) * 128], src[:, t * 128:(t + 1) * 128],
                              mv[:, p, t, 0:1], SUB, rstd[:, p, t:t + 1], MUL)
                last.then_inc(S["ln_done"], 1)

            def norm(n, q):
                for p, b in enumerate(ids(q)):
                    scale_rows(n, p, b, xT[p], Y[p])

            def l0_attn(q):
                for p, b in enumerate(ids(q)):
                    if b == 0:
                        dve.wait_ge(S["lam_set"], 1)
                    dve.wait_ge(S["l0_v"], at(b))
                    link(dve.tensor_tensor_scan(tmp[p][0][:, 0:L], C("lam").to_broadcast([128, L]),
                                                P(p, 1)[:, :], 0.0, MUL, ADD))
                    dve.wait_ge(S["l0_q"], at(b))
                    tt_(tmp[p][1][:, 0:L], tmp[p][0][:, 0:L], P(p, 0)[:, :], MUL).then_inc(S["l0_yq"], 1)
                for p, b in enumerate(ids(q)):
                    dve.wait_ge(S["l0_yt"], at(b))
                    stats(p, P(p, 3))
                for p, b in enumerate(ids(q)):
                    scale_rows(0, p, b, tmp[p][3], P(p, 3))
                for p, b in enumerate(ids(q)):
                    dve.wait_ge(S["l0_ng"], at(b))
                    dve.wait_ge(S["l0_sg"], at(b))
                    tt_(tmp[p][5][:, 0:L], tmp[p][4][:, 0:L], tmp[p][2][:, 0:L], MUL).then_inc(S["l0_z"], 1)
                for p, b in enumerate(ids(q)):
                    dve.wait_ge(S["l0_o"], at(b))
                    dve.wait_ge(ld_t[b], 16)
                    link(tt_(Y[p][:, :], P(p, 1)[:, :], xT[p][:, :], ADD))
                    stats(p, Y[p])
                norm(1, q)

            def l0_ffn(q):
                for p, b in enumerate(ids(q)):
                    dve.wait_ge(S["f0_mix"], at(b))
                    x = xF[p][:, 1:1 + L]
                    stt(tmp[p][3][:, 0:L], x, vc("mu_k"), tmp[p][0][:, 0:L], MUL, ADD)
                    stt(tmp[p][2][:, 0:L], x, vc("mu_r"), tmp[p][1][:, 0:L], MUL, ADD).then_inc(S["f0_xrk"], 1)
                for p, b in enumerate(ids(q)):
                    dve.wait_ge(S["f0_v"], at(b))
                    dve.wait_ge(S["f0_tr"], at(b))
                    link(stt(tmp[p][7][:, 0:L], tmp[p][6][:, 0:L], 1.0, P(p, 2)[:, :], ADD, MUL))
                    link(stt(Y[p][:, :], tmp[p][7][:, 0:L], 0.5, xT[p][:, :], MUL, ADD))
                    stats(p, Y[p])
                norm(2, q)

            def l1_attn(q):
                if q == 0:
                    dve.wait_ge(S["wc_bias"], 1)
                    link(tt_(sv[:, S_["hbx"]:S_["hba"] + 1], P(0, 3)[:, 256:258],
                             vec[:, V["bg_x"]:V["bg_a"] + 1], ADD))
                    ts(sv[:, S_["hbx"]:S_["hba"] + 1], sv[:, S_["hbx"]:S_["hba"] + 1], 0.5, MUL).then_inc(S["bias_half"], 1)
                    dve.wait_ge(S["mix_set"], 1)
                for p, b in enumerate(ids(q)):
                    u, f, g = tmp[p][4][:, 0:L], tmp[p][5][:, 0:L], tmp[p][6][:, 0:L]
                    hi, lo = tmp[p][7][:, 0:L], tmp[p][8][:, 0:L]
                    dve.wait_ge(S["g_ta"], at(b))
                    link(ts(u, tmp[p][0][:, 0:L], C("ai4"), MUL, C("ai4"), ADD))
                    link(ts(f, u, MAGIC, ADD))
                    link(stt(f, f, MAGIC, u, SUB, SUB))
                    link(ts(g, f, MAGIC14, ADD, MAGIC14, SUB))
                    link(tt_(u, f, g, SUB))
                    one = kone.to_broadcast([128, L])
                    dve.tensor_tensor_scan(hi, one, g, 0.0, MUL, ADD)
                    link(dve.tensor_tensor_scan(lo, one, u, 0.0, MUL, ADD))
                    link(ts(f, hi, MAGIC, ADD))
                    link(stt(f, f, MAGIC, hi, SUB, SUB))
                    link(tt_(u, f, lo, SUB))
                    ts(f, u, MAGIC, ADD)
                    link(ts(g, u, 0.25, ADD, MAGIC, ADD))
                    stt(f, f, MAGIC, u, SUB, SUB)
                    stt(g, g, MAGIC, u, SUB, SUB).then_inc(S["g_arg"], 1)
                for p, b in enumerate(ids(q)):
                    dve.wait_ge(S["g_w"], at(b))
                    dve.wait_ge(S["g_tx"], at(b))
                    dve.wait_ge(S["g_xh"], at(b))
                    w, xr, xi = tmp[p][3][:, 0:L], tmp[p][0][:, 0:L], tmp[p][1][:, 0:L]
                    link(stt(w, tmp[p][1][:, 0:L], 1.0, w, ADD, MUL))
                    stt(xr, P(p, 0)[:, :], vc("b_re"), w, ADD, MUL)
                    link(stt(xi, P(p, 1)[:, :], vc("b_im"), w, ADD, MUL))
                    dve.wait_ge(S["g_trig"], at(b))
                    sn, cs = tmp[p][7][:, 0:L], tmp[p][8][:, 0:L]
                    tt_(w, xr, cs, MUL).then_inc(S["g_xr"], 1)
                    link(tt_(tmp[p][4][:, 0:L], xi, sn, MUL))
                    link(tt_(w, w, tmp[p][4][:, 0:L], ADD))
                    mag = tmp[p][2][:, 0:L]
                    dve.tensor_tensor_scan(w, mag, w, 0.0, MUL, ADD)
                    dve.wait_ge(S["g_rot"], at(b))
                    dve.tensor_tensor_scan(tmp[p][4][:, 0:L], mag, tmp[p][5][:, 0:L], 0.0, MUL, ADD).then_inc(S["g_scan"], 1)
                for p, b in enumerate(ids(q)):
                    sn, cs = tmp[p][7][:, 0:L], tmp[p][8][:, 0:L]
                    dve.wait_ge(S["g_scan"], at(b))
                    tt_(tmp[p][5][:, 0:L], cs, tmp[p][3][:, 0:L], MUL)
                    link(tt_(tmp[p][0][:, 0:L], sn, tmp[p][4][:, 0:L], MUL))
                    tt_(tmp[p][5][:, 0:L], tmp[p][5][:, 0:L], tmp[p][0][:, 0:L], SUB).then_inc(S["g_hr"], 1)
                for p, b in enumerate(ids(q)):
                    dve.wait_ge(S["g_o"], at(b))
                    dve.wait_ge(S["g_xb"], at(b))
                    link(tt_(Y[p][:, :], P(p, 2)[:, :], tmp[p][9][:, 0:L], ADD))
                    stats(p, Y[p])
                norm(3, q)

            def l1_ffn(q):
                for p, b in enumerate(ids(q)):
                    dve.wait_ge(S["f1_rt"], at(b))
                    link(tt_(Y[p][:, :], tmp[p][3][:, 0:L], xT[p][:, :], ADD))
                    stats(p, Y[p])
                norm(4, q)

            def l2_attn(q):
                for p, b in enumerate(ids(q)):
                    for side in range(2):
                        dve.wait_ge(S["at_hi"], at(b, 2) - 1 + side)
                        tt_(tmp[p][side][:, 0:L], P(p, side)[:, :], parts[:, side, 0, :], SUB).then_inc(S["at_r1"], 1)
                    for side in range(2):
                        dve.wait_ge(S["at_mid"], at(b, 2) - 1 + side)
                        last = tt_(parts[:, side, 2, :], tmp[p][side][:, 0:L], parts[:, side, 1, :], SUB)
                    last.then_inc(S["at_parts"], 1)
                u0 = 2 * NG * q

                def max_row(u):
                    dve.wait_ge(S["at_mt"], u + 1)
                    if u >= 2:
                        dve.wait_ge(S["at_mneg"], u - 1)
                    dve.tensor_copy(mrow[:, u % 2, :], bank[7][0:16, 0:128]).then_inc(S["at_mrow"], 1)

                def out_rows(u):
                    v = u - u0
                    p, g = v // NG, v % NG
                    dve.wait_ge(S["at_ot"], u + 1)
                    o = bank[7][:, :].rearrange("p (n c) -> p n c", c=32)
                    link(dve.reciprocal(rden[:, u % 2, :], o[:, :, HD]))
                    dst = Y[p][:, :].rearrange("p (t g j d) -> p t g j d", t=NT, g=NG, j=4)[:, :, g, :, :]
                    tt_(dst, o[:, :, 0:HD].rearrange("p (t j) d -> p t j d", t=NT),
                        rden[:, u % 2, :].rearrange("p (t j) -> p t j", t=NT).unsqueeze(3).broadcast_to(
                            [128, NT, 4, HD]), MUL).then_inc(S["at_res"], 1)

                def maxima(u, i):
                    n = 8 * u + i
                    jj, qt = i % 2, i // 2
                    dve.wait_ge(S["at_s"], n + 1)
                    if i == 0 and u >= 2:
                        dve.wait_ge(S["at_mt"], u - 1)
                    dst = mx[:, u % 2, :].rearrange("p (s j t) -> p s j t", s=2, j=2)[:, :, jj, qt]
                    dve.reduce_max(dst, two[i % 2][:, :, :], AX.X).then_inc(S["at_max"], 1)

                for v in range(-2, 2 * NG):
                    u = u0 + v
                    for i in range(8):
                        if v + 2 < 2 * NG:
                            maxima(u + 2, i)
                        if i == 2 and v >= -1 and v + 1 < 2 * NG:
                            max_row(u + 1)
                        if i == 5 and v >= 1:
                            out_rows(u - 1)
                out_rows(u0 + 2 * NG - 1)
                for p, b in enumerate(ids(q)):
                    dve.wait_ge(S["at_res"], NG * (b + 1))
                    link(tt_(Y[p][:, :], Y[p][:, :], xT[p][:, :], ADD))
                    stats(p, Y[p])
                norm(5, q)

            def last_weights():
                dve.wait_ge(S["ld_c"], 32)
                fc, pj = wc[:, 0:4, :], wc[:, 4:8, :].rearrange("p t c -> p (t c)")
                dve.tensor_reduce(fsc[:, 0:4, 0:1], fc, AX.X, ADD, apply_absolute_value=True)
                link(dve.tensor_reduce(fsc[:, 4, 0:1], pj, AX.X, ADD, apply_absolute_value=True))
                ts(fsc[:, 0:4, 0], fsc[:, 0:4, 0], 1.0 / 128, MUL, 1e-5, MAX)
                link(ts(fsc[:, 4:5, 0], fsc[:, 4:5, 0], 1.0 / HID, MUL, 1e-5, MAX))
                ts(fsc[:, :, 1], fsc[:, :, 0], 0.5, MUL)
                link(ts(fsc[:, :, 2], fsc[:, :, 0], -0.5, MUL))
                for s, tiles in ((0, [(t, wc[:, t, :], slice(t * 128, (t + 1) * 128)) for t in range(4)]),
                                 (1, [(4, pj, slice(0, HID))])):
                    for step in range(5):
                        for t, w, c in tiles:
                            d, o = wq_s[s][:, c], wq_s[2][:, c]
                            if step == 0:
                                last = ts(o, w, fsc[:, t, 1:2], ALU.is_gt)
                            elif step == 1:
                                last = stt(d, w, fsc[:, t, 2:3], o, ALU.is_lt, SUB)
                            elif step == 2:
                                last = stt(o, d, -1.0, w, MUL, SUB)
                            elif step == 3:
                                last = tt_(d, w, o, ADD)
                            else:
                                last = ts(o if False else d, d, fsc[:, t, 0:1], MUL)
                        if step < 4:
                            link(last)
                        else:
                            link(last)
                ts(fsc[:, :, 1], fsc[:, :, 1], 1.0, MUL).then_inc(S["q_fc"], 2)

            def moe(q):
                for p, b in enumerate(ids(q)):
                    lg = bank[6 + p][:, 0:NT * E_MOE].rearrange("p (t e) -> p t e", t=NT)
                    dve.wait_ge(S["rt_l"], at(b))
                    link(dve.reduce_max(rs[:, p, 0, :], lg, AX.X))
                    tt_(rt[:, p, 0, :, :], lg, rs[:, p, 0, :].unsqueeze(2).broadcast_to([128, NT, E_MOE]),
                        SUB).then_inc(S["rt_s"], 1)
                for p, b in enumerate(ids(q)):
                    dve.wait_ge(S["rt_e"], at(b))
                    pr = rt[:, p, 2, :, :]
                    link(dve.reduce_sum(rs[:, p, 1, :], rt[:, p, 1, :, :], AX.X))
                    link(dve.reciprocal(rs[:, p, 1, :], rs[:, p, 1, :]))
                    link(tt_(pr, rt[:, p, 1, :, :], rs[:, p, 1, :].unsqueeze(2).broadcast_to([128, NT, E_MOE]), MUL))
                    rk = tmp[p][8][:, 0:256].rearrange("p (t e j) -> p t e j", t=NT, e=E_MOE)
                    for t in range(NT):
                        mine = pr[:, t, :].unsqueeze(2).broadcast_to([128, E_MOE, E_MOE])
                        all_ = pr[:, t, :].unsqueeze(1).broadcast_to([128, E_MOE, E_MOE])
                        last = tt_(rk[:, t, :, :], all_, mine, ALU.is_equal)
                    link(last)
                    for t in range(NT):
                        last = tt_(rk[:, t, :, :], rk[:, t, :, :], tri[:, :, :], MUL)
                    link(last)
                    for t in range(NT):
                        mine = pr[:, t, :].unsqueeze(2).broadcast_to([128, E_MOE, E_MOE])
                        all_ = pr[:, t, :].unsqueeze(1).broadcast_to([128, E_MOE, E_MOE])
                        last = tt_(tmp[p][8][:, 256 + t * 64:256 + (t + 1) * 64].rearrange("p (e j) -> p e j", e=E_MOE), all_, mine, ALU.is_gt)
                    link(last)
                    gt4 = tmp[p][8][:, 256:512].rearrange("p (t e j) -> p t e j", t=NT, e=E_MOE)
                    for t in range(NT):
                        last = tt_(rk[:, t, :, :], rk[:, t, :, :], gt4[:, t, :, :], ADD)
                    link(last)
                    link(dve.reduce_sum(cmb[:, p, :, :], rk, AX.X))
                    link(stt(cmb[:, p, :, :], cmb[:, p, :, :], 2.0, pr, ALU.is_lt, MUL))
                    link(dve.reduce_sum(rs[:, p, 2, :], cmb[:, p, :, :], AX.X))
                    link(ts(rs[:, p, 2, :], rs[:, p, 2, :], 1e-6, ADD))
                    link(dve.reciprocal(rs[:, p, 2, :], rs[:, p, 2, :]))
                    link(tt_(cmb[:, p, :, :], cmb[:, p, :, :],
                             rs[:, p, 2, :].unsqueeze(2).broadcast_to([128, NT, E_MOE]), MUL))

                def weigh(p, b, e):
                    n = E_MOE * b + e
                    dve.wait_ge(S["mo_y"], n + 1)
                    if n >= 2:
                        dve.wait_ge(S["mo_acc"], n - 1)
                    tt_(r3(ye[e % 2]), r3(bank[6 + e % 2][:, :]),
                        cmb[:, p, :, e].unsqueeze(2).broadcast_to([128, NT, 128]), MUL).then_inc(S["mo_t"], 1)

                work = [(p, b, e) for p, b in enumerate(ids(q)) for e in range(E_MOE)]
                for i, (p, b, e) in enumerate(work):
                    for m, (c0, cn) in enumerate(MT):
                        n = 3 * (E_MOE * b + e) + m
                        dve.wait_ge(S["mo_sg"], n + 1)
                        if e >= 2 or b:
                            dve.wait_ge(S["mo_y"], E_MOE * b + e - 1)
                        tt_(hm[3 * (e % 2) + m][0:cn, :], sg[n % 3][0:cn, :],
                            bank[2 * (n % 3) + 1][0:cn, :], MUL).then_inc(S["mo_h"], 1)
                    if i:
                        weigh(*work[i - 1])
                    if LAST >= 8 and q == 0 and i == 2:
                        last_weights()
                weigh(*work[-1])
                for p, b in enumerate(ids(q)):
                    dve.wait_ge(S["mo_acc"], E_MOE * (b + 1))
                    stats(p, Y[p])
                norm(6, q)

            def l3_attn(q):
                if q == 0:
                    dve.wait_ge(S["tab_set"], 1)
                for p, b in enumerate(ids(q)):
                    dve.wait_ge(S["xf_set"], xf_at(6, b))
                    link(tt_(tmp[p][1][:, 0:L], xF[p][:, 1:1 + L], tab[:, 1, :], MUL))
                    m = C("m").to_broadcast([128, L])
                    dve.tensor_tensor_scan(tmp[p][3][:, 0:L], m, tmp[p][1][:, 0:L], vc("lc_im"), MUL, ADD).then_inc(S["c_g"], 1)
                    dve.wait_ge(S["c_in"], at(b))
                    dve.tensor_tensor_scan(tmp[p][2][:, 0:L], m, tmp[p][0][:, 0:L], vc("lc_re"), MUL, ADD).then_inc(S["c_g"], 1)
                for p, b in enumerate(ids(q)):
                    dve.wait_ge(S["c_g"], at(b, 2))
                    link(tt_(tmp[p][4][:, 0:L], tmp[p][2][:, 0:L], tab[:, 2, :], MUL))
                    dve.wait_ge(S["c_t2"], at(b))
                    tt_(tmp[p][4][:, 0:L], tmp[p][4][:, 0:L], tmp[p][5][:, 0:L], SUB).then_inc(S["c_y"], 1)
                for p, b in enumerate(ids(q)):
                    dve.wait_ge(S["c_t"], at(b))
                    link(tt_(Y[p][:, :], P(p, 0)[:, :], xT[p][:, :], ADD))
                    stats(p, Y[p])
                norm(7, q)

            def l3_ffn(q):
                if q == 0:
                    dve.wait_ge(S["q_uv"], 1)
                    dve.wait_ge(S["q_ft"], 2)
                    link(dve.tensor_copy(fcT[:, :], P(0, 2)[:, :]))
                    stt(fcT[:, :], P(0, 1)[:, :], vc("gate"), fcT[:, :], MUL, ADD).then_inc(S["q_fe"], 1)
                for p, b in enumerate(ids(q)):
                    for m in (0, 2):
                        dve.wait_ge(S["h_relu"], 4 * b + m + 1)
                        tt_(tmp[p][4 + m][:, 0:L], tmp[p][m][:, 0:L], tmp[p][m][:, 0:L], MUL).then_inc(S["h_sqd"], 1)
                for p, b in enumerate(ids(q)):
                    dve.wait_ge(S["h_o"], at(b))
                    link(tt_(Y[p][:, :], P(p, 0)[:, :], xT[p][:, :], ADD))
                    stats(p, Y[p])
                norm(8, q)

            kone = kc[:, 6:7]
            dve.memset(kone, 1.0)
            for q in range(PAIRS):
                l0_attn(q)
                for n, layer in enumerate((l0_ffn, l1_attn, l1_ffn, l2_attn, moe, l3_attn, l3_ffn)):
                    if LAST >= n + 2:
                        layer(q)


def _arrays(i):
    import numpy as np
    g = {n: np.asarray(a) for n, a in i.items()}
    x = g["L0_attn_x"]
    f32 = x.dtype

    def T(a):
        return np.asarray(a).T

    def diag(w):
        d = np.zeros((256, 128), f32)
        for n in range(16):
            d[16 * n:16 * n + 16, 8 * n:8 * n + 8] = w[n]
        return d

    def halves(w):
        return w.reshape(128, NH // 2, 2, HD).transpose(0, 2, 3, 1).reshape(128, 128)

    bdx, bda = diag(g["L1_attn_Wg_x"]), diag(g["L1_attn_Wg_a"])
    w_in, w_out = g["L1_attn_W_in"], g["L1_attn_W_out"]
    blocks = {
        "l0_q": T(g["L0_attn_Wq"]), "l0_v": T(g["L0_attn_Wv"]), "l0_g": T(g["L0_attn_Wg"]), "l0_o": T(g["L0_attn_Wo"]),
        "ident": np.eye(128, dtype=f32),
        "f0_r": T(g["L0_ffn_W_r"]), "f0_k": T(g["L0_ffn_W_k"]), "f0_v": T(g["L0_ffn_W_v"]),
        "in_re": w_in[:, :128], "in_im": w_in[:, 128:], "inT0": T(w_in)[:128], "inT1": T(w_in)[128:],
        "bdx0": bdx[:128], "bdx1": bdx[128:], "bda0": bda[:128], "bda1": bda[128:],
        "out0": w_out[:128], "out1": w_out[128:], "b_out": np.broadcast_to(g["L1_attn_b_out"], (128, 128)),
        "th": g["L1_ffn_theta"], "thn": g["L1_ffn_theta_noise"], "phi": g["L1_ffn_phi"], "phin": g["L1_ffn_phi_noise"],
        "a_q": halves(T(g["L2_attn_Wq"])), "a_k": halves(T(g["L2_attn_Wk"])), "a_v": T(g["L2_attn_Wv"]),
    }
    for t in range(4):
        blocks[f"fc{t}"] = g["L3_ffn_w_fc"][t * 128:(t + 1) * 128]
        blocks[f"pj{t}"] = g["L3_ffn_w_proj"][:, t * 128:(t + 1) * 128]
    vecs = {
        "beta": np.repeat(g["L0_attn_beta"], 8), "gamma": g["L0_attn_ln_gamma"], "lnb": g["L0_attn_ln_beta"],
        "mu_r": g["L0_ffn_mu_r"], "mu_k": g["L0_ffn_mu_k"], "b_re": g["L1_attn_b_in"][:128], "b_im": g["L1_attn_b_in"][128:],
        "bg_x": g["L1_attn_bg_x"], "bg_a": g["L1_attn_bg_a"], "a_re": g["L1_attn_a_real_param"],
        "a_im": g["L1_attn_a_imag_param"], "ph_re": g["L3_attn_phazor_init_re"], "ph_im": g["L3_attn_phazor_init_im"],
        "ph_ang": g["L3_attn_phazor_angle"], "ph_ln": g["L3_attn_ln_minus_ln_phazor_abs"],
        "lc_re": g["L3_attn_last_conv_re"], "lc_im": g["L3_attn_last_conv_im"], "ph_sc": g["L3_attn_ln_phazor_scale"],
        "gate": np.broadcast_to(g["L3_ffn_gate"], (128,)),
    }
    dn = np.zeros((128, 8 * 3, 128), f32)
    for e in range(8):
        for m, (c0, cn) in enumerate(MT):
            dn[:cn, 3 * e + m] = g["L2_ffn_w_down"][e, c0:c0 + cn]
    ar = {
        "xt": x.reshape(B, NT, 128, D).transpose(2, 0, 1, 3).reshape(128, B, L),
        "xf": x.transpose(2, 0, 1),
        "vec": np.stack([vecs[n] for n in VEC], axis=1),
        "wa": np.stack([blocks[n] for n in WA], axis=1),
        "wb": np.stack([blocks[n] for n in WB], axis=1),
        "wc": np.stack([blocks[n] for n in WC], axis=1),
        "small": np.concatenate([T(g["L3_ffn_u"]), g["L3_ffn_v"], T(g["L3_ffn_fast_b"])], axis=1),
        "rt": g["L2_ffn_router_w"],
        "gu": np.stack([g["L2_ffn_w_gate"], g["L2_ffn_w_up"]]).transpose(2, 0, 1, 3),
        "dn": dn,
        "iota": np.broadcast_to(np.arange(1, L + 1, dtype=f32), (128, L)),
        "tri": np.broadcast_to(np.tril(np.ones((8, 8), f32), -1), (128, 8, 8)),
    }
    return {n: np.ascontiguousarray(a) for n, a in ar.items()}


def kernel(**inputs):
    import numpy as _np
    import concourse.bacc as _bacc
    from concourse import mybir as _mybir
    from concourse.bass_utils import run_bass_kernel_spmd as _run

    nc = _bacc.Bacc("TRN2", target_bir_lowering=False, num_devices=1)
    arrays = _arrays(inputs)
    args = [nc.dram_tensor("in_" + n, a.shape, _mybir.dt.from_np(a.dtype), kind="ExternalInput").ap() for n, a in arrays.items()]
    out = nc.dram_tensor("out", (128, B, L), _mybir.dt.float32, kind="ExternalOutput").ap()
    build(nc, *args, out)
    r = _run(nc, [{"in_" + n: a for n, a in arrays.items()}], core_ids=[0])
    y = r.results[0]["out"]
    return _np.ascontiguousarray(_np.asarray(y).reshape(128, B, NT, D).transpose(1, 2, 0, 3).reshape(B, L, D))
```

```python
import concourse.bass as bass
from concourse import mybir
from contextlib import ExitStack

B, L, D = 4, 512, 128
NT = L // 128
PAIRS = 2
NH, HD = 16, 8
NG = 4
E_MOE, I_MOE = 8, 344
MT = [(0, 128), (128, 128), (256, 88)]
HID = 512
RANK = 16
VW = HD + 1
NLN = 9
EPS = 1e-5
MAGIC = 1.5 * 2.0 ** 23
MAGIC14 = 1.5 * 2.0 ** 9
TURN = 6.283185
PI_2 = 1.5707962

VEC = ["beta", "gamma", "lnb", "mu_r", "mu_k", "b_re", "b_im", "bg_x", "bg_a", "a_re", "a_im",
       "ph_re", "ph_im", "ph_ang", "ph_ln", "lc_re", "lc_im", "ph_sc", "gate"]
V = {n: i for i, n in enumerate(VEC)}
WA = ["l0_q", "l0_v", "l0_g", "l0_o", "ident"]
WB = ["f0_r", "f0_k", "f0_v", "in_re", "in_im", "inT0", "inT1", "bdx0", "bdx1", "bda0", "bda1",
      "out0", "out1", "b_out", "th", "thn", "phi", "phin", "a_q", "a_k", "a_v"]
WC = ["fc0", "fc1", "fc2", "fc3", "pj0", "pj1", "pj2", "pj3"]


def build(nc, xt_d, xf_d, vec_d, wa_d, wb_d, wc_d, small_d, rt_d, gu_d, dn_d, iota_d, tri_d, out_d,
          LAST=8):
    F32, BF16, FP16 = mybir.dt.float32, mybir.dt.bfloat16, mybir.dt.float16
    ALU, ACT, AX = mybir.AluOpType, mybir.ActivationFunctionType, mybir.AxisListType
    ADD, SUB, MUL, MAX = ALU.add, ALU.subtract, ALU.mult, ALU.max

    ctx = ExitStack()
    with ctx:
        def sb(name, shape, dt=F32):
            return ctx.enter_context(nc.sbuf_tensor(name, shape, dt))

        def sem(name):
            return ctx.enter_context(nc.semaphore(name))

        xT = [sb(f"xT{p}", [128, L]) for p in range(2)]
        xF = [sb(f"xF{p}", [128, 1 + L]) for p in range(2)]
        Y = [sb(f"Y{p}", [128, L]) for p in range(2)]
        NTMP = 10
        tmp = [[sb(f"tmp{p}_{i}", [128, 1 + L]) for i in range(NTMP)] for p in range(2)]
        vec = sb("vec", [128, len(VEC)])
        wa = sb("wa", [128, len(WA), 128])
        wb = sb("wb", [128, len(WB), 128])
        wc = sb("wc", [128, len(WC), 128])
        small = sb("small", [RANK, HID + 128 + RANK])
        router = sb("router", [128, E_MOE])
        gu = sb("gu", [128, 2, E_MOE, I_MOE])
        dn = sb("dn", [128, E_MOE * 3, 128])
        tri = sb("tri", [128, E_MOE, E_MOE])
        st6 = sb("st6", [128, 2, NT, 6])
        mv = sb("mv", [128, 2, NT, 2])
        rstd = sb("rstd", [128, 2, NT])
        kc = sb("kc", [128, 8])
        sv = sb("sv", [128, 64])
        wgx = sb("wgx", [128, 128])
        wga = sb("wga", [128, 128])
        w_cos = sb("w_cos", [128, 128])
        w_sin = sb("w_sin", [128, 128])
        stmp = sb("stmp", [128, 2, 128])
        tab = sb("tab", [128, 4, L])
        iota = tab[:, 3, :]
        tt = [tmp[1][5][:, 0:L], tmp[0][6][:, 0:L]]
        x0F = [tmp[p][9][:, 0:L] for p in range(2)]
        fcT = sb("fcT", [128, HID])
        pjT = sb("pjT", [128, HID])
        wq_s = [tmp[1][6 + i][:, 0:L] for i in range(2)]
        wo_s = [tmp[0][7][:, 0:L], tmp[0][8][:, 0:L]]
        fsc = sb("fsc", [128, 5, 3])
        uT_m = sb("uT_m", [RANK, 128])
        QS = [sb(f"QS{p}", [128, NH, L], BF16) for p in range(2)]
        KS = [sb(f"KS{p}", [128, NH, L], BF16) for p in range(2)]
        parts = [[[tmp[p][6 + (3 * side + i) // 2][:, :].bitcast(BF16)[:, (3 * side + i) % 2 * L:][:, 0:L]
                   for i in range(3)] for side in range(2)] for p in range(2)]
        VA = [sb(f"VA{p}", [128, NT * NH * VW + 32 - VW]) for p in range(2)]
        PT = [[tmp[i][2 + j][:, 0:L] for j in range(4)] for i in range(2)]
        OS = tmp[0][9][:, 0:L]
        ones_zeros = sb("ones_zeros", [56, L], BF16)
        ones, zero3 = ones_zeros[0:24, :], ones_zeros[32:56, :]
        mx = sb("mx", [128, 2, 16])
        mres = sb("mres", [128, 2, 16])
        mp = sb("mp", [128, 2, 48], BF16)
        mrow = sb("mrow", [48, 2, 128], BF16)
        ident_h = sb("ident_h", [128, 128], BF16)
        rden = sb("rden", [128, 2, NT * 4])
        rt = sb("rt", [128, 2, 3, NT, E_MOE])
        rs = sb("rs", [128, 2, 4, NT])
        cmb = sb("cmb", [128, 2, NT, E_MOE])
        hm = [tmp[0][i][:, 0:L] for i in range(6)]
        sg = [tmp[1][i][:, 0:L] for i in range(3)]
        ye = [tmp[1][3 + i][:, 0:L] for i in range(2)]
        two = [ctx.enter_context(nc.psum_tensor(f"two{i}", [128, 2, L], F32)) for i in range(2)]
        bank = [two[i // 2][:, i % 2, :] for i in range(4)]
        bank += [ctx.enter_context(nc.psum_tensor(f"bank{i}", [128, L], F32))[:, :] for i in range(4, 8)]

        def P(p, i):
            return bank[4 * p + i]

        KHALF, KE, KM1, KPI2, KEPS, KLN = range(6)
        NAMES = ["lam", "one_r", "one_k", "hbx", "hba", "Lh", "ai4", "m", "w", "u1", "dd", "t0", "t1", "t2",
                 "t3", "soft", "y", "gateC", "ir", "om", "z"]
        S_ = {n: i for i, n in enumerate(NAMES)}

        def C(n):
            return sv[:, S_[n]:S_[n] + 1]

        def vc(n):
            return vec[:, V[n]:V[n] + 1]

        def k(i):
            return kc[:, i:i + 1]

        ident = wa[:, WA.index("ident"), :]

        def W(n):
            return wa[:, WA.index(n), :] if n in WA else wb[:, WB.index(n), :]

        def r3(ap):
            return ap.rearrange("p (t c) -> p t c", t=NT)

        ld_t = [sem(f"ld_t{b}") for b in range(B)]
        ld_x = [sem(f"ld_x{b}") for b in range(B)]
        names = """ld_a ld_b ld_c ld_m ld_o rows_zero zeroed ones_set consts lam_set mix_set bias_half gates_set soft_u soft_ln soft_s
        log_s decay_set ph_arg ph_trig tab_set th_arg th_trig stats_mv rstd_set ln_done x_turned xf_set
        l0_v l0_q l0_g l0_sg l0_yq l0_yt l0_nt l0_ng l0_z l0_o
        f0_mix f0_xrk f0_k f0_r f0_kk f0_tr f0_v
        g_pre g_xh g_ta g_tx g_mag g_t g_w g_arg g_trig g_xr g_rot g_scan g_hr g_hi g_o g_xb
        f1_ri f1_sq f1_ss f1_rt
        wc_bias wc_set at_qkv at_hi at_mid at_r1 at_parts at_mz at_v at_va at_s at_max at_mp at_mt at_mrow
        at_e at_p at_pv at_os at_ot at_res at_y
        rt_l rt_s rt_e rt_c mo_gu mo_sg mo_h mo_y mo_t mo_acc
        c_in c_g c_t2 c_y c_t
        q_fc q_uv q_um q_uc q_ft q_fe h_pre h_relu h_sqd h_sqp h_o
        dchain achain pchain""".split()
        S = {n: sem(n) for n in names}
        out_dma = [sem(f"out_dma{b}") for b in range(B)]
        at_qs = [sem(f"at_qs{p}") for p in range(2)]
        at_ks = [sem(f"at_ks{p}") for p in range(2)]
        at_m = [sem(f"at_m{i}") for i in range(2)]

        def at(b, steps=1):
            return steps * (b + 1)

        def ln_at(n, b):
            return 2 * (LAST + 1) * (b // 2) + 2 * n + b % 2 + 1

        def xf_at(n, b):
            return 2 * (LAST - 1) * (b // 2) + 2 * (n - 1) + b % 2 + 1

        def heads(a):
            return a[:, 0:L].rearrange("p (t h d) -> p t h d", t=NT, h=NH)

        def values(p):
            return VA[p][:, 0:NT * NH * VW].rearrange("p (t h c) -> p t h c", t=NT, h=NH)

        def ids(q):
            return (2 * q, 2 * q + 1)

        def spread(queue, p, b, landed, shares):
            for (part, side), halves in shares.items():
                if part < 2:
                    queue.wait_ge(S[("at_hi", "at_mid")[part]], 2 * b + 1 + side)
                else:
                    queue.wait_ge(S["at_parts"], at(b))
                rows, order = ((QS, (0, 0, 1, 1, 0, 2)), (KS, (0, 1, 0, 1, 2, 0)))[side]
                for r in (r for r in range(6) if order[r] == part):
                    for hh in halves:
                        queue.dma_start(rows[p][64 * hh + 8 * r:64 * hh + 8 * r + 8, 8 * hh:8 * hh + 8, :],
                                        parts[p][side][part][64 * hh:64 * hh + 64, :]).then_inc(landed, 16)

        block = ctx.enter_context(nc.Block())

        @block.sync
        def _(sp):
            sp.dma_start(x0F[0], xf_d[:, 0, :]).then_inc(ld_x[0], 16)
            sp.dma_start(wa[:, :, :], wa_d).then_inc(S["ld_a"], 16)
            sp.dma_start(vec[:, :], vec_d).then_inc(S["ld_a"], 16)
            sp.dma_start(x0F[1], xf_d[:, 1, :]).then_inc(ld_x[1], 16)
            for b in range(2):
                sp.dma_start(xT[b][:, :], xt_d[:, b, :]).then_inc(ld_t[b], 16)
            sp.dma_start(iota, iota_d).then_inc(S["ld_b"], 16)
            sp.dma_start(wb[:, :, :], wb_d).then_inc(S["ld_b"], 16)
            sp.dma_start(wc[:, :, :], wc_d).then_inc(S["ld_c"], 16)
            sp.dma_start(small[:, :], small_d).then_inc(S["ld_c"], 16)
            sp.dma_start(gu[:, 0, :, :], gu_d[:, 0, :, :]).then_inc(S["ld_m"], 16)
            sp.dma_start(gu[:, 1, :, :], gu_d[:, 1, :, :]).then_inc(S["ld_m"], 16)
            sp.dma_start(dn[:, :, :], dn_d).then_inc(S["ld_m"], 16)
            sp.dma_start(router[:, :], rt_d).then_inc(S["ld_m"], 16)
            sp.dma_start(tri[:, :, :], tri_d).then_inc(S["ld_m"], 16)
            if LAST >= 4:
                sp.wait_ge(S["rows_zero"], 4)
                sp.wait_ge(S["ones_set"], 1)
            for p in range(2):
                for hh in range(2):
                    sp.dma_start(KS[p][64 * hh + 48:64 * hh + 51, 8 * hh:8 * hh + 8, :], ones).then_inc(S["ld_o"], 16)
            for q in range(PAIRS):
                if LAST >= 5:
                    if q:
                        for p in range(2):
                            sp.wait_ge(S["at_pv"], 2 * NT * (2 * NG * (q - 1) + NG * (p + 1)))
                            for hh in range(2):
                                sp.dma_start(QS[p][64 * hh + 48:64 * hh + 51, 8 * hh:8 * hh + 8, :],
                                             zero3).then_inc(S["at_mz"], 16)
                    for p, b in enumerate(ids(q)):
                        spread(sp, p, b, at_qs[p], {(part, side): (1,) if side else (0, 1) for part in range(3)
                                                   for side in range(2) if (part, side) != (1, 1)})
                    for v in range(2 * NG):
                        u = 2 * NG * q + v
                        p, g = v // NG, v % NG
                        sp.wait_ge(S["at_mrow"], u + 1)
                        for hh in range(2):
                            sp.dma_start(QS[p][64 * hh + 48:64 * hh + 51, 8 * hh + 2 * g:8 * hh + 2 * g + 2, :],
                                         mrow[24 * hh:24 * hh + 24, v % 2, :]).then_inc(at_m[u % 2], 16)
                    for p, b in enumerate(ids(q)):
                        if b + 2 < B:
                            sp.wait_ge(S["at_ot"], 2 * NG * (q + 1))
                            sp.dma_start(x0F[p], xf_d[:, b + 2, :]).then_inc(ld_x[b + 2], 16)
                elif q == 0:
                    for p, b in enumerate(ids(q)):
                        sp.wait_ge(S["ln_done"], ln_at(LAST, b))
                        sp.dma_start(x0F[p], xf_d[:, b + 2, :]).then_inc(ld_x[b + 2], 16)
                for p, b in enumerate(ids(q)):
                    sp.wait_ge(S["ln_done"], ln_at(LAST, b))
                    sp.dma_start(out_d[:, b, :], xT[p][:, :]).then_inc(out_dma[b], 16)
                    if b + 2 < B:
                        sp.wait_ge(out_dma[b], 16)
                        sp.dma_start(xT[p][:, :], xt_d[:, b + 2, :]).then_inc(ld_t[b + 2], 16)
            for n, v in (("ld_a", 32), ("ld_b", 32), ("ld_c", 32), ("ld_m", 80), ("ld_o", 64)):
                sp.wait_ge(S[n], v)
            for b in range(B):
                sp.wait_ge(out_dma[b], 16)

        @block.tensor
        def _(pe):
            def token_major(out, act, w, first=True, last=True, tiles=range(NT)):
                for t in tiles:
                    mm = pe.matmul(out[:, t * 128:(t + 1) * 128], act[:, t * 128:(t + 1) * 128], w,
                                   start=first, stop=last)
                return mm

            def turn(out, src):
                for t in range(NT):
                    mm = pe.transpose(out[:, t * 128:(t + 1) * 128], src[:, t * 128:(t + 1) * 128], ident)
                return mm

            def turn_x(n, q):
                for p, b in enumerate(ids(q) if n < LAST else ()):
                    pe.wait_ge(S["ln_done"], ln_at(n, b))
                    if n == 2 and b == 0:
                        pe.wait_ge(S["wc_set"], 2)
                    turn(P(p, 3), xT[p]).then_inc(S["x_turned"], 1)

            def l0_attn(q):
                for p, b in enumerate(ids(q)):
                    pe.wait_ge(ld_x[b], 16)
                    if b == 0:
                        pe.wait_ge(S["ld_a"], 32)
                    if q:
                        pe.wait_ge(S["stats_mv"], ln_at(LAST, b - 2))
                    pe.matmul(P(p, 1)[:, :], W("l0_v"), x0F[p], start=True, stop=True).then_inc(S["l0_v"], 1)
                    pe.matmul(P(p, 0)[:, :], W("l0_q"), x0F[p], start=True, stop=True).then_inc(S["l0_q"], 1)
                    pe.matmul(P(p, 2)[:, :], W("l0_g"), x0F[p], start=True, stop=True).then_inc(S["l0_g"], 1)
                for p, b in enumerate(ids(q)):
                    pe.wait_ge(S["l0_yq"], at(b))
                    turn(P(p, 3), tmp[p][1]).then_inc(S["l0_yt"], 1)
                for p, b in enumerate(ids(q)):
                    pe.wait_ge(S["ln_done"], ln_at(0, b))
                    turn(P(p, 0), tmp[p][3]).then_inc(S["l0_nt"], 1)
                for p, b in enumerate(ids(q)):
                    pe.wait_ge(S["l0_z"], at(b))
                    token_major(P(p, 1), tmp[p][5], W("l0_o")).then_inc(S["l0_o"], 1)

            def l0_ffn(q):
                for p, b in enumerate(ids(q)):
                    if b == 0:
                        pe.wait_ge(S["ld_b"], 32)
                    pe.wait_ge(S["f0_xrk"], at(b))
                    pe.matmul(P(p, 1)[:, :], W("f0_k"), tmp[p][3][:, 0:L], start=True, stop=True).then_inc(S["f0_k"], 1)
                    token_major(P(p, 0), tmp[p][2], W("f0_r")).then_inc(S["f0_r"], 1)
                if q == 0 and LAST >= 3:
                    gate_weights()
                for p, b in enumerate(ids(q)):
                    pe.wait_ge(S["f0_kk"], at(b))
                    token_major(P(p, 2), tmp[p][5], W("f0_v")).then_inc(S["f0_v"], 1)

            def gate_weights():
                pe.wait_ge(S["ld_b"], 32)
                for i, (w0, w1) in enumerate((("bdx0", "bdx1"), ("bda0", "bda1"))):
                    pe.matmul(P(0, 3)[:, i * 128:(i + 1) * 128], W("inT0"), W(w0), start=True, stop=False)
                    pe.matmul(P(0, 3)[:, i * 128:(i + 1) * 128], W("inT1"), W(w1), start=False, stop=True)
                    pe.matmul(P(0, 3)[:, 256 + i:257 + i], W(w0), vc("b_re"), start=True, stop=False)
                    mm = pe.matmul(P(0, 3)[:, 256 + i:257 + i], W(w1), vc("b_im"), start=False, stop=True)
                mm.then_inc(S["wc_bias"], 1)

            def l1_attn(q):
                for p, b in enumerate(ids(q)):
                    pe.wait_ge(S["xf_set"], xf_at(2, b))
                    if b == 0:
                        pe.wait_ge(S["wc_set"], 2)
                    x = xF[p][:, 1:1 + L]
                    pe.matmul(P(p, 3)[:, :], wga[:, :], x, start=True, stop=True).then_inc(S["g_pre"], 1)
                    pe.matmul(P(p, 2)[:, :], wgx[:, :], x, start=True, stop=True).then_inc(S["g_pre"], 1)
                    pe.matmul(P(p, 0)[:, :], W("in_re"), x, start=True, stop=True)
                    pe.matmul(P(p, 1)[:, :], W("in_im"), x, start=True, stop=True).then_inc(S["g_xh"], 1)
                for p, b in enumerate(ids(q)):
                    pe.wait_ge(S["g_hr"], at(b))
                    if p == 0:
                        pe.wait_ge(S["g_hi"], q + 1)
                    for t in range(NT):
                        token_major(P(p, 2), tmp[p][5], W("out0"), last=False, tiles=[t])
                        mm = token_major(P(p, 2), tmp[p][8], W("out1"), first=False, tiles=[t])
                    mm.then_inc(S["g_o"], 1)

            def l1_ffn(q):
                for p, b in enumerate(ids(q)):
                    pe.wait_ge(S["xf_set"], xf_at(3, b))
                    if b == 0:
                        pe.wait_ge(S["th_trig"], 2)
                    x = xF[p][:, 1:1 + L]
                    token_major(P(p, 0), x, w_cos[:, :])
                    token_major(P(p, 1), x, w_sin[:, :]).then_inc(S["f1_ri"], 1)

            def l2_attn(q):
                for p, b in enumerate(ids(q)):
                    pe.wait_ge(S["xf_set"], xf_at(4, b))
                    x = xF[p][:, 1:1 + L]
                    pe.matmul(P(p, 0)[:, :], W("a_q"), x, start=True, stop=True)
                    pe.matmul(P(p, 1)[:, :], W("a_k"), x, start=True, stop=True).then_inc(S["at_qkv"], 1)
                    token_major(P(p, 2), x, W("a_v")).then_inc(S["at_v"], 1)

                u0 = 2 * NG * q

                def stack(arr, j, g):
                    return arr[:, 8 * (j % 2) + 2 * g + j // 2, :]

                def score_tile(u, i):
                    v = u - u0
                    p, g = v // NG, v % NG
                    n = 8 * u + i
                    jj, qt = i % 2, i // 2
                    if i == 0 and u == 0:
                        pe.wait_ge(S["ld_o"], 64)
                    if i == 0 and v == 0 and q:
                        pe.wait_ge(S["at_mz"], 64)
                    if i == 0 and g == 0:
                        pe.wait_ge(at_qs[p], 16 * 16 * (q + 1))
                        pe.wait_ge(at_ks[p], 16 * 8 * (q + 1))
                    if n >= 2:
                        pe.wait_ge(S["at_max"], n - 1)
                    for s in range(2):
                        j = 2 * jj + s
                        mm = pe.matmul(bank[2 * (i % 2) + s][:, :],
                                       stack(QS[p], j, g)[:, qt * 128:(qt + 1) * 128],
                                       stack(KS[p], j, g), start=True, stop=True)
                    mm.then_inc(S["at_s"], 1)

                def turn_max(u):
                    pe.wait_ge(S["at_mp"], u + 1)
                    if u > 2:
                        pe.wait_ge(S["at_res"], max(u - 2, u0))
                    if LAST >= 6 and u == u0 + 2 * NG - 1:
                        pe.wait_ge(S["xf_set"], xf_at(5, 2 * q))
                    pe.transpose(bank[7].bitcast(BF16)[0:48, 0:128], mp[:, u % 2, :],
                                 ident_h[:, :]).then_inc(S["at_mt"], 1)

                def exp_tile(u, i):
                    v = u - u0
                    p, g = v // NG, v % NG
                    kt, j = i // 4, i % 4
                    n = 16 * u + i
                    if i == 0:
                        pe.wait_ge(at_m[u % 2], 16 * 2 * (u // 2 + 1))
                    if n >= 2:
                        pe.wait_ge(S["at_p"], n - 1)
                    pe.matmul(bank[4 + i % 2][:, :], stack(KS[p], j, g)[:, kt * 128:(kt + 1) * 128],
                              stack(QS[p], j, g), start=True, stop=True).then_inc(S["at_e"], 1)

                def weigh(u, kt, half):
                    v = u - u0
                    p, g = v // NG, v % NG
                    q0 = half * (L // 2)
                    if kt == 0 and half == 0:
                        if u:
                            pe.wait_ge(S["at_os"], u)
                        if g == 0:
                            pe.wait_ge(S["at_va"], 2 * q + p + 1)
                    pe.wait_ge(S["at_p"], 16 * u + 4 * kt + 4)
                    for j in range(4):
                        c = (kt * NH + 4 * g + j) * VW
                        mm = pe.matmul(bank[6][32 * j:32 * j + 32, q0:q0 + L // 2], VA[p][:, c:c + 32],
                                       PT[kt % 2][j][:, q0:q0 + L // 2], start=(kt == 0 and half == 0), stop=(kt == NT - 1 and half == 1))
                    mm.then_inc(S["at_pv"], 1)

                def turn_out(u):
                    pe.wait_ge(S["at_os"], u + 1)
                    pe.wait_ge(S["at_mrow"], min(u + 3, u0 + 2 * NG))
                    if u > u0:
                        pe.wait_ge(S["at_res"], u)
                    if LAST >= 6 and u >= u0 + 2 * NG - 2:
                        pe.wait_ge(S["rt_s"], 2 * q + 1)
                    turn(bank[7], OS).then_inc(S["at_ot"], 1)

                pe.wait_ge(S["at_r1"], at(2 * q + 1, 2))
                pe.wait_ge(S["at_va"], 2 * q + 2)
                for i in range(8):
                    score_tile(u0, i)
                for i in range(8):
                    score_tile(u0 + 1, i)
                    if i == 2:
                        turn_max(u0)
                for v in range(2 * NG):
                    u = u0 + v
                    for i in range(8):
                        exp_tile(u, 2 * i)
                        if v + 2 < 2 * NG:
                            score_tile(u + 2, i)
                        exp_tile(u, 2 * i + 1)
                        if i >= 2:
                            weigh(u, i // 2 - 1, i % 2)
                        elif v:
                            weigh(u - 1, 3, i)
                        if i == 2 and v + 1 < 2 * NG:
                            turn_max(u + 1)
                        if i == 5 and v:
                            turn_out(u - 1)
                        if LAST >= 6 and i == 7 and v == 2 * NG - 3:
                            turn_early(q, 0, u)
                        if LAST >= 6 and i == 7 and v == 2 * NG - 2:
                            pe.wait_ge(S["at_res"], u)
                            logits(q, 0)
                for half in range(2):
                    weigh(u0 + 2 * NG - 1, 3, half)
                turn_out(u0 + 2 * NG - 1)

            def turn_early(q, p, u):
                pe.wait_ge(S["at_res"], u)
                pe.wait_ge(S["ln_done"], ln_at(5, 2 * q + p))
                turn(bank[7], xT[p]).then_inc(S["x_turned"], 1)

            def logits(q, p):
                if q == 0 and p == 0:
                    pe.wait_ge(S["ld_m"], 80)
                pe.wait_ge(S["xf_set"], xf_at(5, 2 * q + p))
                for t in range(NT):
                    mm = pe.matmul(bank[7][:, t * E_MOE:(t + 1) * E_MOE],
                                   xF[p][:, 1 + t * 128:1 + (t + 1) * 128], router[:, :], start=True, stop=True)
                mm.then_inc(S["rt_l"], 1)

            def moe(q):
                def up(p, b, e):
                    for m, (c0, cn) in enumerate(MT):
                        n = 3 * (E_MOE * b + e) + m
                        if n >= 3:
                            pe.wait_ge(S["mo_h"], n - 2)
                        for s in range(2):
                            mm = pe.matmul(bank[2 * (n % 3) + s][0:cn, :], gu[:, s, e, c0:c0 + cn],
                                           xF[p][:, 1:1 + L], start=True, stop=True)
                        mm.then_inc(S["mo_gu"], 1)

                def down(p, b, e):
                    n = E_MOE * b + e
                    pe.wait_ge(S["mo_h"], 3 * n + 3)
                    if p == 0 and e == 1:
                        pe.wait_ge(S["rt_s"], 2 * q + 2)
                    if n >= 2:
                        pe.wait_ge(S["mo_t"], n - 1)
                    for t in range(NT):
                        for m, (c0, cn) in enumerate(MT):
                            mm = pe.matmul(bank[6 + e % 2][:, t * 128:(t + 1) * 128],
                                           hm[3 * (e % 2) + m][0:cn, t * 128:(t + 1) * 128],
                                           dn[0:cn, 3 * e + m, :], start=(m == 0), stop=(m == 2))
                    mm.then_inc(S["mo_y"], 1)

                work = [(p, b, e) for p, b in enumerate(ids(q)) for e in range(E_MOE)]
                for i, w in enumerate(work):
                    up(*w)
                    if i == 0:
                        turn_early(q, 1, 2 * NG * (q + 1))
                    if i == 1:
                        logits(q, 1)
                    if i:
                        down(*work[i - 1])
                down(*work[-1])

            def l3_attn(q):
                for p, b in enumerate(ids(q)):
                    pe.wait_ge(S["c_y"], at(b))
                    turn(P(p, 0), tmp[p][4]).then_inc(S["c_t"], 1)

            def last_weights():
                pe.wait_ge(S["ld_c"], 32)
                pe.matmul(P(0, 0)[0:RANK, 0:128], small[:, HID + 128:HID + 128 + RANK],
                          small[:, HID:HID + 128], start=True, stop=True).then_inc(S["q_um"], 1)
                pe.wait_ge(S["q_uc"], 1)
                pe.matmul(P(0, 1)[:, :], uT_m[:, :], small[:, 0:HID], start=True, stop=True).then_inc(S["q_uv"], 1)
                pe.wait_ge(S["q_fc"], 2)
                turn(P(0, 2), wq_s[0])
                turn(P(0, 3), wq_s[1]).then_inc(S["q_ft"], 1)

            def l3_ffn(q):
                for p, b in enumerate(ids(q)):
                    pe.wait_ge(S["xf_set"], xf_at(7, b))
                    if b == 0:
                        pe.wait_ge(S["q_fe"], 1)
                    for m in range(4):
                        pe.matmul(P(p, m)[:, :], fcT[:, m * 128:(m + 1) * 128], xF[p][:, 1:1 + L],
                                  start=True, stop=True).then_inc(S["h_pre"], 1)
                for p, b in enumerate(ids(q)):
                    pe.wait_ge(S["h_sqd"], at(b, 2))
                    pe.wait_ge(S["h_sqp"], at(b, 2))
                    for t in range(NT):
                        for m in range(4):
                            mm = token_major(P(p, 0), tmp[p][4 + m], pjT[:, m * 128:(m + 1) * 128],
                                             first=(m == 0), last=(m == 3), tiles=[t])
                    mm.then_inc(S["h_o"], 1)

            for q in range(PAIRS):
                l0_attn(q)
                turn_x(1, q)
                if LAST >= 2:
                    l0_ffn(q)
                    turn_x(2, q)
                if LAST >= 3:
                    l1_attn(q)
                    turn_x(3, q)
                if LAST >= 4:
                    l1_ffn(q)
                    turn_x(4, q)
                if LAST >= 5:
                    l2_attn(q)
                if LAST >= 6:
                    moe(q)
                    turn_x(6, q)
                if LAST >= 7:
                    l3_attn(q)
                    turn_x(7, q)
                if LAST >= 8:
                    if q == 0:
                        pe.wait_ge(S["xf_set"], xf_at(7, 0))
                        last_weights()
                    l3_ffn(q)

        @block.scalar
        def _(act):
            n_chain = [0]

            def link(ins):
                n_chain[0] += 1
                ins.then_inc(S["achain"], 1)
                act.wait_ge(S["achain"], n_chain[0])

            def put_early(q, p):
                act.wait_ge(S["x_turned"], xf_at(5, 2 * q + p))
                act.activation(xF[p][:, 1:1 + L], bank[7], ACT.Copy).then_inc(S["xf_set"], 1)

            def router_exp(q, p):
                act.wait_ge(S["rt_s"], 2 * q + p + 1)
                act.activation(rt[:, p, 1, :, :], rt[:, p, 0, :, :], ACT.Exp).then_inc(S["rt_e"], 1)

            def put_x(n, q):
                for p, b in enumerate(ids(q) if n < LAST else ()):
                    act.wait_ge(S["x_turned"], xf_at(n, b))
                    if n == 1 and b == 0:
                        act.wait_ge(S["zeroed"], 1)
                    act.activation(xF[p][:, 1:1 + L], P(p, 3)[:, :], ACT.Copy).then_inc(S["xf_set"], 1)

            act.wait_ge(S["consts"], 1)
            act.wait_ge(S["soft_u"], 1)
            act.activation(C("t0"), C("u1"), ACT.Ln).then_inc(S["soft_ln"], 1)

            for q in range(PAIRS):
                for p, b in enumerate(ids(q)):
                    act.wait_ge(S["l0_g"], at(b))
                    act.activation(tmp[p][2][:, 0:L], P(p, 2)[:, :], ACT.Silu).then_inc(S["l0_sg"], 1)
                for p, b in enumerate(ids(q)):
                    act.wait_ge(S["l0_nt"], at(b))
                    act.activation(tmp[p][4][:, 0:L], P(p, 0)[:, :], ACT.Identity, scale=vc("gamma"),
                                   bias=vc("lnb")).then_inc(S["l0_ng"], 1)
                if q == 0:
                    act.wait_ge(S["soft_s"], 1)
                    act.activation(C("y"), C("t3"), ACT.Ln).then_inc(S["log_s"], 1)
                put_x(1, q)
                if LAST >= 2:
                    for p, b in enumerate(ids(q)):
                        if b == 0:
                            act.wait_ge(S["mix_set"], 1)
                        act.wait_ge(S["xf_set"], xf_at(1, b))
                        act.activation(tmp[p][0][:, :], xF[p][:, :], ACT.Copy, scale=C("one_k"))
                        act.activation(tmp[p][1][:, :], xF[p][:, :], ACT.Copy, scale=C("one_r")).then_inc(S["f0_mix"], 1)
                    for p, b in enumerate(ids(q)):
                        act.wait_ge(S["f0_k"], at(b))
                        link(act.activation(tmp[p][4][:, 0:L], P(p, 1)[:, :], ACT.Relu))
                        act.activation(tmp[p][5][:, 0:L], tmp[p][4][:, 0:L], ACT.Square).then_inc(S["f0_kk"], 1)
                    for p, b in enumerate(ids(q)):
                        act.wait_ge(S["f0_r"], at(b))
                        act.activation(tmp[p][6][:, 0:L], P(p, 0)[:, :], ACT.Tanh, scale=0.5).then_inc(S["f0_tr"], 1)
                    if q == 0 and LAST >= 3:
                        act.wait_ge(S["bias_half"], 1)
                        act.activation(wgx[:, :], P(0, 3)[:, 0:128], ACT.Copy).then_inc(S["wc_set"], 1)
                        act.activation(wga[:, :], P(0, 3)[:, 128:256], ACT.Copy).then_inc(S["wc_set"], 1)
                    put_x(2, q)
                if LAST >= 3:
                    for p, b in enumerate(ids(q)):
                        act.wait_ge(S["g_pre"], at(b, 2))
                        act.activation(tmp[p][0][:, 0:L], P(p, 3)[:, :], ACT.Tanh, scale=0.5,
                                       bias=C("hba")).then_inc(S["g_ta"], 1)
                        act.activation(tmp[p][1][:, 0:L], P(p, 2)[:, :], ACT.Tanh, scale=0.5,
                                       bias=C("hbx")).then_inc(S["g_tx"], 1)
                    act.preload_act_table_set("natural_log_exp_and_others")
                    if q == 0:
                        act.wait_ge(S["gates_set"], 1)
                    for p, b in enumerate(ids(q)):
                        act.wait_ge(S["g_ta"], at(b))
                        act.activation(tmp[p][2][:, 0:L], tmp[p][0][:, 0:L], ACT.Exp, scale=C("Lh"),
                                       bias=C("Lh")).then_inc(S["g_mag"], 1)
                    for p, b in enumerate(ids(q)):
                        act.wait_ge(S["g_t"], at(b))
                        link(act.activation(tmp[p][3][:, 0:L], tmp[p][3][:, 0:L], ACT.Ln))
                        act.activation(tmp[p][3][:, 0:L], tmp[p][3][:, 0:L], ACT.Exp, scale=0.5,
                                       bias=k(KLN)).then_inc(S["g_w"], 1)
                    for p, b in enumerate(ids(q)):
                        act.wait_ge(S["g_arg"], at(b))
                        act.activation(tmp[p][7][:, 0:L], tmp[p][5][:, 0:L], ACT.Sin, scale=-TURN)
                        act.activation(tmp[p][8][:, 0:L], tmp[p][6][:, 0:L], ACT.Sin, scale=-TURN,
                                       bias=k(KPI2)).then_inc(S["g_trig"], 1)
                    if q == 0:
                        act.wait_ge(S["th_arg"], 1)
                        act.activation(w_cos[:, :], stmp[:, 0, :], ACT.Sin, scale=-TURN,
                                       bias=k(KPI2)).then_inc(S["th_trig"], 1)
                        act.activation(w_sin[:, :], stmp[:, 1, :], ACT.Sin, scale=-TURN).then_inc(S["th_trig"], 1)
                    put_x(3, q)
                if LAST >= 4:
                    for p, b in enumerate(ids(q)):
                        act.wait_ge(S["f1_ri"], at(b))
                        act.activation(tmp[p][0][:, 0:L], P(p, 0)[:, :], ACT.Square)
                        act.activation(tmp[p][1][:, 0:L], P(p, 1)[:, :], ACT.Square).then_inc(S["f1_sq"], 1)
                    for p, b in enumerate(ids(q)):
                        act.wait_ge(S["f1_ss"], at(b))
                        act.activation(tmp[p][3][:, 0:L], tmp[p][2][:, 0:L], ACT.Sqrt).then_inc(S["f1_rt"], 1)
                    put_x(4, q)
                if LAST >= 5:
                    for p, b in enumerate(ids(q)):
                        act.wait_ge(S["at_qkv"], at(b))
                        for side in range(2):
                            act.activation(parts[p][side][0], P(p, side)[:, :], ACT.Copy).then_inc(S["at_hi"], 1)
                        for side in range(2):
                            act.wait_ge(S["at_r1"], at(b, 2) - 1 + side)
                            act.activation(parts[p][side][1], tmp[p][side][:, 0:L], ACT.Copy).then_inc(S["at_mid"], 1)
                        act.wait_ge(S["at_v"], at(b))
                        if b == 0:
                            act.wait_ge(S["ones_set"], 1)
                        act.activation(values(p)[:, :, :, 0:HD], heads(P(p, 2)), ACT.Copy).then_inc(S["at_va"], 1)
                    u0 = 2 * NG * q

                    def take_out(u):
                        act.wait_ge(S["at_pv"], 2 * NT * (u + 1))
                        if u:
                            act.wait_ge(S["at_ot"], u)
                        act.activation(OS, bank[6][:, :], ACT.Copy).then_inc(S["at_os"], 1)

                    act.preload_act_table_set("exp_and_others")
                    for u in range(u0, u0 + 2 * NG):
                        for i in range(16):
                            n = 16 * u + i
                            act.wait_ge(S["at_e"], n + 1)
                            if n >= 8 and i % 4 == 0:
                                act.wait_ge(S["at_pv"], 2 * (n // 4 - 1))
                            act.activation(PT[(i // 4) % 2][i % 4], bank[4 + i % 2][:, :], ACT.Exp,
                                           scale=float(HD) ** -0.5).then_inc(S["at_p"], 1)
                            if i == 2 and u > u0:
                                take_out(u - 1)
                            if LAST >= 6 and i == 1 and u == u0 + 2 * NG - 2:
                                put_early(q, 0)
                            if LAST >= 6 and i == 6 and u == u0 + 2 * NG - 1:
                                router_exp(q, 0)
                    take_out(u0 + 2 * NG - 1)
                if LAST >= 6:
                    for p, b in enumerate(ids(q)):
                        for e in range(E_MOE):
                            for m, (c0, cn) in enumerate(MT):
                                n = 3 * (E_MOE * b + e) + m
                                if n == 6:
                                    act.wait_ge(S["ph_arg"], 1)
                                    act.activation(tt[0], tab[:, 0, :], ACT.Sin, scale=-TURN)
                                    act.activation(tt[1], tab[:, 1, :], ACT.Sin, scale=-TURN,
                                                   bias=k(KPI2)).then_inc(S["ph_trig"], 1)
                                act.wait_ge(S["mo_gu"], n + 1)
                                if n >= 3:
                                    act.wait_ge(S["mo_h"], n - 2)
                                act.activation(sg[n % 3][0:cn, :], bank[2 * (n % 3)][0:cn, :],
                                               ACT.Silu).then_inc(S["mo_sg"], 1)
                            if p == 0 and e == 0:
                                put_early(q, 1)
                            if p == 0 and e == 1:
                                router_exp(q, 1)
                    put_x(6, q)
                if LAST >= 7:
                    put_x(7, q)
                if LAST >= 8:
                    if q == 0:
                        act.wait_ge(S["q_um"], 1)
                        act.activation(uT_m[:, :], P(0, 0)[0:RANK, 0:128], ACT.Copy).then_inc(S["q_uc"], 1)
                        act.wait_ge(S["q_ft"], 1)
                        act.activation(pjT[:, :], P(0, 3)[:, :], ACT.Copy).then_inc(S["q_ft"], 1)
                    for p, b in enumerate(ids(q)):
                        for m in range(4):
                            act.wait_ge(S["h_pre"], 4 * b + m + 1)
                            act.activation(tmp[p][m][:, 0:L], P(p, m)[:, :], ACT.Relu).then_inc(S["h_relu"], 1)

        @block.gpsimd
        def _(pool):
            n_chain = [0]

            def link(ins):
                n_chain[0] += 1
                ins.then_inc(S["pchain"], 1)
                pool.wait_ge(S["pchain"], n_chain[0])

            def ts(out, a, s1, op0, s2=None, op1=None):
                if op1 is None:
                    return pool.tensor_scalar(out, a, s1, None, op0)
                return pool.tensor_scalar(out, a, s1, s2, op0, op1)

            def tten(out, a, b_, op):
                return pool.tensor_tensor(out, a, b_, op)

            def norm_scale(n, q, batch=None):
                for p, b in enumerate(ids(q)) if batch is None else [(batch, 2 * q + batch)]:
                    pool.wait_ge(S["stats_mv"], ln_at(n, b))
                    link(ts(rstd[:, p, :], mv[:, p, :, 1], EPS, ADD))
                    tten(rstd[:, p, :], rstd[:, p, :], k(KHALF).to_broadcast([128, NT]), ALU.pow).then_inc(S["rstd_set"], 1)

            for i, v in ((KHALF, -0.5), (KE, 2.718281828459045), (KM1, -1.0), (KPI2, PI_2),
                         (KEPS, EPS), (KLN, -0.6931471805599453)):
                last = pool.memset(k(i), v)
            link(last)
            pool.wait_ge(S["ld_a"], 32)
            link(ts(C("lam"), vc("beta"), -1.0, MUL))
            link(tten(C("lam"), k(KE), C("lam"), ALU.pow))
            link(ts(C("lam"), C("lam"), 1.0, ADD))
            tten(C("lam"), C("lam"), k(KM1), ALU.pow).then_inc(S["lam_set"], 1)
            pool.memset(xF[0][:, 0:1], 0.0)
            pool.memset(xF[1][:, 0:1], 0.0).then_inc(S["zeroed"], 1)
            ts(C("one_r"), vc("mu_r"), -1.0, MUL, 1.0, ADD)
            ts(C("one_k"), vc("mu_k"), -1.0, MUL, 1.0, ADD).then_inc(S["mix_set"], 1)
            ts(C("ai4"), vc("a_im"), 0.25, MUL)
            pool.memset(C("t3"), 0.0).then_inc(S["consts"], 1)

            def phases():
                pool.wait_ge(S["ld_b"], 32)
                tten(stmp[:, 0, :], W("th"), W("thn"), ADD)
                link(tten(stmp[:, 1, :], W("phi"), W("phin"), ADD))
                link(ts(stmp[:, :, :], stmp[:, :, :], 1.0 / 6.283185307179586, MUL))
                ts(w_cos[:, :], stmp[:, 0, :], 0.25, ADD, MAGIC, ADD)
                link(ts(w_sin[:, :], stmp[:, 1, :], MAGIC, ADD))
                ts(w_cos[:, :], w_cos[:, :], MAGIC, SUB)
                link(ts(w_sin[:, :], w_sin[:, :], MAGIC, SUB))
                tten(stmp[:, 0, :], w_cos[:, :], stmp[:, 0, :], SUB)
                tten(stmp[:, 1, :], w_sin[:, :], stmp[:, 1, :], SUB).then_inc(S["th_arg"], 1)

            def zero_rows(rows):
                pool.memset(rows[:, :, :].bitcast(F32), 0.0).then_inc(S["rows_zero"], 1)

            def ones_rows():
                link(pool.memset(ones_zeros[:, :], 0.0))
                link(pool.memset(ones, 1.0))
                for p in range(2):
                    pool.memset(VA[p][:, NT * NH * VW:], 0.0)
                    last = pool.memset(values(p)[:, :, :, HD:VW], 1.0)
                pool.tensor_copy(ident_h[:, :], ident).then_inc(S["ones_set"], 1)

            def soft_exp():
                a = vc("a_re")
                link(ts(C("w"), a, -1.0, MUL))
                link(ts(C("w"), C("w"), a, ALU.min))
                link(tten(C("w"), k(KE), C("w"), ALU.pow))
                link(ts(C("u1"), C("w"), 1.0, ADD))
                ts(C("dd"), C("u1"), -1.0, ADD).then_inc(S["soft_u"], 1)
                pool.wait_ge(S["soft_u"], 1)
                ts(C("t1"), C("dd"), 0.0, ALU.is_equal)

            def soft_plus():
                a = vc("a_re")
                pool.wait_ge(S["soft_ln"], 1)
                link(ts(C("t2"), C("t0"), -1.0, MUL))
                link(tten(C("t2"), k(KE), C("t2"), ALU.pow))
                link(tten(C("t2"), C("t2"), C("u1"), MUL))
                link(ts(C("t2"), C("t2"), -1.0, ADD))
                link(tten(C("t0"), C("t0"), C("t2"), ADD))
                link(tten(C("t0"), C("t0"), C("t1"), ADD))
                link(tten(C("t0"), C("t0"), C("w"), MUL))
                link(tten(C("dd"), C("dd"), C("t1"), ADD))
                link(tten(C("dd"), C("dd"), k(KM1), ALU.pow))
                link(tten(C("t0"), C("t0"), C("dd"), MUL))
                link(ts(C("soft"), a, 0.0, MAX))
                link(tten(C("soft"), C("soft"), C("t0"), ADD))
                ts(C("t3"), C("soft"), 1e-19, MAX).then_inc(S["soft_s"], 1)

            def soft_log():
                a = vc("a_re")
                pool.wait_ge(S["log_s"], 1)
                link(ts(C("t2"), C("y"), -1.0, MUL))
                link(tten(C("t2"), k(KE), C("t2"), ALU.pow))
                link(tten(C("t2"), C("t2"), C("t3"), MUL))
                link(ts(C("t2"), C("t2"), -1.0, ADD))
                link(tten(C("y"), C("y"), C("t2"), ADD))
                link(ts(C("t1"), a, -40.0, ALU.is_lt))
                link(tten(C("t2"), a, C("y"), SUB))
                link(tten(C("t2"), C("t2"), C("t1"), MUL))
                link(tten(C("y"), C("y"), C("t2"), ADD))
                ts(C("Lh"), C("y"), 0.5, MUL).then_inc(S["gates_set"], 1)

            def tables_arg():
                link(tten(C("z"), k(KE), vc("ph_ln"), ALU.pow))
                link(tten(C("z"), C("z"), vc("ph_sc"), MUL))
                link(ts(C("z"), C("z"), -1.0, MUL))
                link(tten(C("m"), k(KE), C("z"), ALU.pow))
                link(ts(C("gateC"), C("m"), -1.0, MUL, 1.0, ADD))
                link(tten(C("om"), vc("ph_ang"), vc("ph_sc"), MUL))
                link(ts(C("om"), C("om"), 1.0 / 6.283185307179586, MUL))
                link(ts(tt[0], iota, C("om"), MUL))
                ts(tab[:, 0, :], tt[0], MAGIC, ADD)
                link(ts(tab[:, 1, :], tt[0], 0.25, ADD, MAGIC, ADD))
                link(ts(tab[:, 0:2, :], tab[:, 0:2, :], MAGIC, SUB))
                tten(tab[:, 0, :], tab[:, 0, :], tt[0], SUB)
                link(tten(tab[:, 1, :], tab[:, 1, :], tt[0], SUB))
                ts(C("ir"), vc("ph_im"), -1.0, MUL).then_inc(S["ph_arg"], 1)

            def tables():
                pool.wait_ge(S["ph_trig"], 1)
                sn, cs = tt[0], tt[1]
                ts(tab[:, 0, :], sn, vc("ph_im"), MUL)
                ts(tab[:, 1, :], cs, vc("ph_im"), MUL)
                ts(tab[:, 2, :], cs, vc("ph_re"), MUL)
                link(ts(tab[:, 3, :], sn, vc("ph_re"), MUL))
                tten(tab[:, 0, :], tab[:, 0, :], tab[:, 2, :], ADD)
                link(tten(tab[:, 1, :], tab[:, 1, :], tab[:, 3, :], SUB))
                ts(tab[:, 2, :], cs, C("gateC"), MUL)
                ts(tab[:, 3, :], sn, C("gateC"), MUL).then_inc(S["tab_set"], 1)

            soft_exp()
            for q in range(PAIRS):
                norm_scale(0, q)
                if q == 0:
                    soft_plus()
                norm_scale(1, q)
                if q == 0:
                    soft_log()
                    phases()
                    ones_rows()
                    zero_rows(KS[0])
                if LAST >= 2:
                    norm_scale(2, q)
                if LAST >= 3:
                    for p, b in enumerate(ids(q)):
                        pool.wait_ge(S["ln_done"], ln_at(2, b))
                        tten(r3(tmp[p][9][:, 0:L]), r3(xT[p][:, :]),
                             W("b_out").unsqueeze(1).broadcast_to([128, NT, 128]), ADD).then_inc(S["g_xb"], 1)
                    for p, b in enumerate(ids(q)):
                        pool.wait_ge(S["g_mag"], at(b))
                        t = tmp[p][3][:, 0:L]
                        link(tten(t, tmp[p][2][:, 0:L], tmp[p][2][:, 0:L], MUL))
                        link(ts(t, t, -1.0, MUL, 1.0, ADD))
                        ts(t, t, 1e-6, MAX).then_inc(S["g_t"], 1)
                    for p, b in enumerate(ids(q)):
                        pool.wait_ge(S["g_xr"], at(b))
                        pool.wait_ge(S["g_trig"], at(b))
                        a_, b_ = tmp[p][5][:, 0:L], tmp[p][6][:, 0:L]
                        tten(a_, tmp[p][1][:, 0:L], tmp[p][8][:, 0:L], MUL)
                        link(tten(b_, tmp[p][0][:, 0:L], tmp[p][7][:, 0:L], MUL))
                        tten(a_, a_, b_, SUB).then_inc(S["g_rot"], 1)
                    b = 2 * q
                    pool.wait_ge(S["g_scan"], at(b))
                    a_, b_ = tmp[0][1][:, 0:L], tmp[0][6][:, 0:L]
                    tten(a_, tmp[0][7][:, 0:L], tmp[0][3][:, 0:L], MUL)
                    link(tten(b_, tmp[0][8][:, 0:L], tmp[0][4][:, 0:L], MUL))
                    pool.wait_ge(S["g_hr"], at(b))
                    tten(tmp[0][8][:, 0:L], a_, b_, ADD).then_inc(S["g_hi"], 1)
                    if q == 0:
                        zero_rows(QS[1])
                    norm_scale(3, q)
                    if q == 0:
                        zero_rows(KS[1])
                if LAST >= 4:
                    for p, b in enumerate(ids(q)):
                        pool.wait_ge(S["f1_sq"], at(b))
                        tten(tmp[p][2][:, 0:L], tmp[p][0][:, 0:L], tmp[p][1][:, 0:L], ADD).then_inc(S["f1_ss"], 1)
                    norm_scale(4, q)
                if LAST >= 5:
                    for p, b in enumerate(ids(q)):
                        spread(pool, p, b, at_ks[p], {(0, 1): (0,), (1, 1): (0, 1), (2, 1): (0,)})
                    u0 = 2 * NG * q

                    def negate(u):
                        v = u % 2
                        m = mx[:, v, :].rearrange("p (s x) -> p s x", s=2)
                        part = [mp[:, v, :].rearrange("p (s r x) -> p s r x", s=2, r=3)[:, :, r, :] for r in range(3)]
                        res = mres[:, v, :].rearrange("p (s x) -> p s x", s=2)
                        pool.wait_ge(S["at_max"], 8 * (u + 1))
                        if u >= 2:
                            pool.wait_ge(S["at_mt"], u - 1)
                        ts(part[0], m, -1.0, MUL)
                        link(ts(res, m, -1.0, MUL))
                        link(tten(res, res, part[0], SUB))
                        link(pool.tensor_copy(part[1], res))
                        tten(part[2], res, part[1], SUB).then_inc(S["at_mp"], 1)

                    for u in range(u0, u0 + 2 * NG):
                        negate(u)
                        if u == u0 + 2 * NG - 2:
                            norm_scale(5, q, 0)
                    norm_scale(5, q, 1)
                if LAST >= 6:
                    if q == 0:
                        pool.wait_ge(S["ln_done"], ln_at(5, 1))
                        tables_arg()
                    for p, b in enumerate(ids(q)):
                        for e in range(E_MOE):
                            n = E_MOE * b + e
                            if q == 0 and n == 4:
                                tables()
                            pool.wait_ge(S["mo_t"], n + 1)
                            other = xT[p] if e == 0 else Y[p]
                            if e:
                                pool.wait_ge(S["mo_acc"], n)
                            tten(Y[p][:, :], ye[e % 2], other[:, :], ADD).then_inc(S["mo_acc"], 1)
                    norm_scale(6, q)
                if LAST >= 7:
                    for p, b in enumerate(ids(q)):
                        pool.wait_ge(S["xf_set"], xf_at(6, b))
                        tten(tmp[p][0][:, 0:L], xF[p][:, 1:1 + L], tab[:, 0, :], MUL).then_inc(S["c_in"], 1)
                    for p, b in enumerate(ids(q)):
                        pool.wait_ge(S["c_g"], at(b, 2))
                        tten(tmp[p][5][:, 0:L], tmp[p][3][:, 0:L], tab[:, 3, :], MUL).then_inc(S["c_t2"], 1)
                    norm_scale(7, q)
                if LAST >= 8:
                    for p, b in enumerate(ids(q)):
                        for m in (1, 3):
                            pool.wait_ge(S["h_relu"], 4 * b + m + 1)
                            tten(tmp[p][4 + m][:, 0:L], tmp[p][m][:, 0:L], tmp[p][m][:, 0:L], MUL).then_inc(S["h_sqp"], 1)
                    norm_scale(8, q)

        @block.vector
        def _(dve):
            n_chain = [0]

            def link(ins):
                n_chain[0] += 1
                ins.then_inc(S["dchain"], 1)
                dve.wait_ge(S["dchain"], n_chain[0])

            def stt(out, a, s, b_, op0, op1):
                return dve.scalar_tensor_tensor(out, a, s, b_, op0, op1)

            def tt_(out, a, b_, op):
                return dve.tensor_tensor(out, a, b_, op)

            def ts(out, a, s1, op0, s2=None, op1=None):
                if op1 is None:
                    return dve.tensor_scalar(out, a, s1, None, op0)
                return dve.tensor_scalar(out, a, s1, s2, op0, op1)

            def stats(p, src):
                for t in range(NT):
                    last = dve.bn_stats(st6[:, p, t, :], src[:, t * 128:(t + 1) * 128])
                link(last)
                for t in range(NT):
                    last = dve.bn_aggr(mv[:, p, t, :], st6[:, p, t, :])
                last.then_inc(S["stats_mv"], 1)

            def scale_rows(n, p, b, dst, src):
                dve.wait_ge(S["rstd_set"], ln_at(n, b))
                for t in range(NT):
                    last = ts(dst[:, t * 128:(t + 1) * 128], src[:, t * 128:(t + 1) * 128],
                              mv[:, p, t, 0:1], SUB, rstd[:, p, t:t + 1], MUL)
                last.then_inc(S["ln_done"], 1)

            def norm(n, q):
                for p, b in enumerate(ids(q)):
                    scale_rows(n, p, b, xT[p], Y[p])

            def l0_attn(q):
                for p, b in enumerate(ids(q)):
                    if b == 0:
                        dve.wait_ge(S["lam_set"], 1)
                    dve.wait_ge(S["l0_v"], at(b))
                    link(dve.tensor_tensor_scan(tmp[p][0][:, 0:L], C("lam").to_broadcast([128, L]),
                                                P(p, 1)[:, :], 0.0, MUL, ADD))
                    dve.wait_ge(S["l0_q"], at(b))
                    tt_(tmp[p][1][:, 0:L], tmp[p][0][:, 0:L], P(p, 0)[:, :], MUL).then_inc(S["l0_yq"], 1)
                for p, b in enumerate(ids(q)):
                    dve.wait_ge(S["l0_yt"], at(b))
                    stats(p, P(p, 3))
                for p, b in enumerate(ids(q)):
                    scale_rows(0, p, b, tmp[p][3], P(p, 3))
                for p, b in enumerate(ids(q)):
                    dve.wait_ge(S["l0_ng"], at(b))
                    dve.wait_ge(S["l0_sg"], at(b))
                    tt_(tmp[p][5][:, 0:L], tmp[p][4][:, 0:L], tmp[p][2][:, 0:L], MUL).then_inc(S["l0_z"], 1)
                for p, b in enumerate(ids(q)):
                    dve.wait_ge(S["l0_o"], at(b))
                    dve.wait_ge(ld_t[b], 16)
                    link(tt_(Y[p][:, :], P(p, 1)[:, :], xT[p][:, :], ADD))
                    stats(p, Y[p])
                norm(1, q)

            def l0_ffn(q):
                for p, b in enumerate(ids(q)):
                    dve.wait_ge(S["f0_mix"], at(b))
                    x = xF[p][:, 1:1 + L]
                    stt(tmp[p][3][:, 0:L], x, vc("mu_k"), tmp[p][0][:, 0:L], MUL, ADD)
                    stt(tmp[p][2][:, 0:L], x, vc("mu_r"), tmp[p][1][:, 0:L], MUL, ADD).then_inc(S["f0_xrk"], 1)
                if q == 0 and LAST >= 3:
                    hb = sv[:, S_["hbx"]:S_["hba"] + 1]
                    dve.wait_ge(S["wc_bias"], 1)
                    dve.wait_ge(S["mix_set"], 1)
                    link(tt_(hb, P(0, 3)[:, 256:258], vec[:, V["bg_x"]:V["bg_a"] + 1], ADD))
                    ts(hb, hb, 0.5, MUL).then_inc(S["bias_half"], 1)
                for p, b in enumerate(ids(q)):
                    dve.wait_ge(S["f0_v"], at(b))
                    dve.wait_ge(S["f0_tr"], at(b))
                    link(stt(tmp[p][7][:, 0:L], tmp[p][6][:, 0:L], 1.0, P(p, 2)[:, :], ADD, MUL))
                    link(stt(Y[p][:, :], tmp[p][7][:, 0:L], 0.5, xT[p][:, :], MUL, ADD))
                    stats(p, Y[p])
                norm(2, q)

            def l1_attn(q):
                for p, b in enumerate(ids(q)):
                    u, f, g = tmp[p][4][:, 0:L], tmp[p][5][:, 0:L], tmp[p][6][:, 0:L]
                    hi, lo = tmp[p][7][:, 0:L], tmp[p][8][:, 0:L]
                    dve.wait_ge(S["g_ta"], at(b))
                    link(ts(u, tmp[p][0][:, 0:L], C("ai4"), MUL, C("ai4"), ADD))
                    link(ts(f, u, MAGIC, ADD))
                    link(stt(f, f, MAGIC, u, SUB, SUB))
                    link(ts(g, f, MAGIC14, ADD, MAGIC14, SUB))
                    link(tt_(u, f, g, SUB))
                    one = kone.to_broadcast([128, L])
                    dve.tensor_tensor_scan(hi, one, g, 0.0, MUL, ADD)
                    link(dve.tensor_tensor_scan(lo, one, u, 0.0, MUL, ADD))
                    link(ts(f, hi, MAGIC, ADD))
                    link(stt(f, f, MAGIC, hi, SUB, SUB))
                    link(tt_(u, f, lo, SUB))
                    ts(f, u, MAGIC, ADD)
                    link(ts(g, u, 0.25, ADD, MAGIC, ADD))
                    stt(f, f, MAGIC, u, SUB, SUB)
                    stt(g, g, MAGIC, u, SUB, SUB).then_inc(S["g_arg"], 1)
                for p, b in enumerate(ids(q)):
                    dve.wait_ge(S["g_w"], at(b))
                    dve.wait_ge(S["g_tx"], at(b))
                    dve.wait_ge(S["g_xh"], at(b))
                    w, xr, xi = tmp[p][3][:, 0:L], tmp[p][0][:, 0:L], tmp[p][1][:, 0:L]
                    link(stt(w, tmp[p][1][:, 0:L], 1.0, w, ADD, MUL))
                    stt(xr, P(p, 0)[:, :], vc("b_re"), w, ADD, MUL)
                    stt(xi, P(p, 1)[:, :], vc("b_im"), w, ADD, MUL).then_inc(S["g_xr"], 1)
                for p, b in enumerate(ids(q)):
                    w, xr, xi, c = [tmp[p][i][:, 0:L] for i in (3, 0, 1, 4)]
                    sn, cs = tmp[p][7][:, 0:L], tmp[p][8][:, 0:L]
                    dve.wait_ge(S["g_trig"], at(b))
                    dve.wait_ge(S["g_xr"], at(b))
                    tt_(w, xr, cs, MUL)
                    link(tt_(c, xi, sn, MUL))
                    link(tt_(w, w, c, ADD))
                    dve.tensor_tensor_scan(w, tmp[p][2][:, 0:L], w, 0.0, MUL, ADD)
                for p, b in enumerate(ids(q)):
                    dve.wait_ge(S["g_rot"], at(b))
                    dve.tensor_tensor_scan(tmp[p][4][:, 0:L], tmp[p][2][:, 0:L], tmp[p][5][:, 0:L], 0.0,
                                           MUL, ADD).then_inc(S["g_scan"], 1)
                for p, b in enumerate(ids(q)):
                    sn, cs = tmp[p][7][:, 0:L], tmp[p][8][:, 0:L]
                    re, im = tmp[p][3][:, 0:L], tmp[p][4][:, 0:L]
                    dve.wait_ge(S["g_scan"], at(b))
                    tt_(tmp[p][5][:, 0:L], cs, re, MUL)
                    if p:
                        tt_(tmp[p][1][:, 0:L], sn, re, MUL)
                        tt_(tmp[p][6][:, 0:L], cs, im, MUL)
                    link(tt_(tmp[p][0][:, 0:L], sn, im, MUL))
                    last = tt_(tmp[p][5][:, 0:L], tmp[p][5][:, 0:L], tmp[p][0][:, 0:L], SUB)
                    if p:
                        last = tt_(tmp[p][8][:, 0:L], tmp[p][1][:, 0:L], tmp[p][6][:, 0:L], ADD)
                    last.then_inc(S["g_hr"], 1)
                for p, b in enumerate(ids(q)):
                    dve.wait_ge(S["g_o"], at(b))
                    dve.wait_ge(S["g_xb"], at(b))
                    link(tt_(Y[p][:, :], P(p, 2)[:, :], tmp[p][9][:, 0:L], ADD))
                    stats(p, Y[p])
                norm(3, q)

            def l1_ffn(q):
                for p, b in enumerate(ids(q)):
                    dve.wait_ge(S["f1_rt"], at(b))
                    link(tt_(Y[p][:, :], tmp[p][3][:, 0:L], xT[p][:, :], ADD))
                    stats(p, Y[p])
                norm(4, q)

            def l2_attn(q):
                for p, b in enumerate(ids(q)):
                    for side in range(2):
                        dve.wait_ge(S["at_hi"], at(b, 2) - 1 + side)
                        tt_(tmp[p][side][:, 0:L], P(p, side)[:, :], parts[p][side][0], SUB).then_inc(S["at_r1"], 1)
                    for side in range(2):
                        dve.wait_ge(S["at_mid"], at(b, 2) - 1 + side)
                        last = tt_(parts[p][side][2], tmp[p][side][:, 0:L], parts[p][side][1], SUB)
                    last.then_inc(S["at_parts"], 1)
                u0 = 2 * NG * q

                def max_row(u):
                    dve.wait_ge(S["at_mt"], u + 1)
                    if u >= 2:
                        dve.wait_ge(at_m[u % 2], 16 * 2 * (u // 2))
                    dve.tensor_copy(mrow[:, u % 2, :], bank[7].bitcast(BF16)[0:48, 0:128]).then_inc(S["at_mrow"], 1)

                def out_rows(u):
                    v = u - u0
                    p, g = v // NG, v % NG
                    dve.wait_ge(S["at_ot"], u + 1)
                    o = bank[7][:, :].rearrange("p (n c) -> p n c", c=32)
                    link(dve.reciprocal(rden[:, u % 2, :], o[:, :, HD]))
                    dst = Y[p][:, :].rearrange("p (t g j d) -> p t g j d", t=NT, g=NG, j=4)[:, :, g, :, :]
                    tt_(dst, o[:, :, 0:HD].rearrange("p (t j) d -> p t j d", t=NT),
                        rden[:, u % 2, :].rearrange("p (t j) -> p t j", t=NT).unsqueeze(3).broadcast_to(
                            [128, NT, 4, HD]), MUL).then_inc(S["at_res"], 1)

                def maxima(u, i):
                    n = 8 * u + i
                    jj, qt = i % 2, i // 2
                    dve.wait_ge(S["at_s"], n + 1)
                    if i == 0 and u >= 2:
                        dve.wait_ge(S["at_mp"], u - 1)
                    dst = mx[:, u % 2, :].rearrange("p (s j t) -> p s j t", s=2, j=2)[:, :, jj, qt]
                    dve.reduce_max(dst, two[i % 2][:, :, :], AX.X).then_inc(S["at_max"], 1)

                def residual(p):
                    dve.wait_ge(S["at_res"], NG * (2 * q + p + 1))
                    link(tt_(Y[p][:, :], Y[p][:, :], xT[p][:, :], ADD))
                    stats(p, Y[p])

                for v in range(-2, 2 * NG):
                    u = u0 + v
                    for i in range(8):
                        if v + 2 < 2 * NG:
                            maxima(u + 2, i)
                        if i == 3 and v >= -1 and v + 1 < 2 * NG:
                            max_row(u + 1)
                        if i == 6 and v >= 1:
                            out_rows(u - 1)
                        if i == 1 and v == 2 * NG - 3:
                            residual(0)
                        if i == 4 and v == 2 * NG - 3:
                            scale_rows(5, 0, 2 * q, xT[0], Y[0])
                        if LAST >= 6 and i == 0 and v == 2 * NG - 1:
                            route_scores(q, 0)
                        if LAST >= 6 and i == 2 and v == 2 * NG - 1:
                            route(q, 0)
                out_rows(u0 + 2 * NG - 1)
                residual(1)
                scale_rows(5, 1, 2 * q + 1, xT[1], Y[1])

            def last_scales():
                dve.wait_ge(S["ld_c"], 32)
                fc, pj = wc[:, 0:4, :], wc[:, 4:8, :].rearrange("p t c -> p (t c)")
                dve.tensor_reduce(fsc[:, 0:4, 0:1], fc, AX.X, ADD, apply_absolute_value=True)
                link(dve.tensor_reduce(fsc[:, 4, 0:1], pj, AX.X, ADD, apply_absolute_value=True))
                ts(fsc[:, 0:4, 0], fsc[:, 0:4, 0], 1.0 / 128, MUL, 1e-5, MAX)
                link(ts(fsc[:, 4:5, 0], fsc[:, 4:5, 0], 1.0 / HID, MUL, 1e-5, MAX))
                ts(fsc[:, :, 1], fsc[:, :, 0], 0.5, MUL)
                link(ts(fsc[:, :, 2], fsc[:, :, 0], -0.5, MUL))

            def last_weights(step):
                pj = wc[:, 4:8, :].rearrange("p t c -> p (t c)")
                tiles = [(0, t, wc[:, t, :], slice(t * 128, (t + 1) * 128)) for t in range(4)]
                for s, t, w, c in tiles + [(1, 4, pj, slice(0, HID))]:
                    d, o = wq_s[s][:, c], wo_s[s][:, c]
                    if step == 0:
                        last = ts(o, w, fsc[:, t, 1:2], ALU.is_gt)
                    elif step == 1:
                        last = stt(d, w, fsc[:, t, 2:3], o, ALU.is_lt, SUB)
                    elif step == 2:
                        last = stt(o, d, -1.0, w, MUL, SUB)
                    elif step == 3:
                        last = tt_(d, w, o, ADD)
                    else:
                        last = ts(d, d, fsc[:, t, 0:1], MUL)
                link(last)
                if step == 4:
                    ts(fsc[:, :, 1], fsc[:, :, 1], 1.0, MUL).then_inc(S["q_fc"], 2)

            def route_scores(q, p):
                lg = bank[7][:, 0:NT * E_MOE].rearrange("p (t e) -> p t e", t=NT)
                dve.wait_ge(S["rt_l"], 2 * q + p + 1)
                link(dve.reduce_max(rs[:, p, 0, :], lg, AX.X))
                tt_(rt[:, p, 0, :, :], lg, rs[:, p, 0, :].unsqueeze(2).broadcast_to([128, NT, E_MOE]),
                    SUB).then_inc(S["rt_s"], 1)

            def route(q, p):
                b = 2 * q + p
                dve.wait_ge(S["rt_e"], at(b))
                pr = rt[:, p, 2, :, :]
                link(dve.reduce_sum(rs[:, p, 1, :], rt[:, p, 1, :, :], AX.X))
                link(dve.reciprocal(rs[:, p, 1, :], rs[:, p, 1, :]))
                link(tt_(pr, rt[:, p, 1, :, :], rs[:, p, 1, :].unsqueeze(2).broadcast_to([128, NT, E_MOE]), MUL))
                rk = tmp[p][8][:, 0:256].rearrange("p (t e j) -> p t e j", t=NT, e=E_MOE)
                for t in range(NT):
                    mine = pr[:, t, :].unsqueeze(2).broadcast_to([128, E_MOE, E_MOE])
                    all_ = pr[:, t, :].unsqueeze(1).broadcast_to([128, E_MOE, E_MOE])
                    last = tt_(rk[:, t, :, :], all_, mine, ALU.is_equal)
                link(last)
                for t in range(NT):
                    last = tt_(rk[:, t, :, :], rk[:, t, :, :], tri[:, :, :], MUL)
                link(last)
                for t in range(NT):
                    mine = pr[:, t, :].unsqueeze(2).broadcast_to([128, E_MOE, E_MOE])
                    all_ = pr[:, t, :].unsqueeze(1).broadcast_to([128, E_MOE, E_MOE])
                    last = tt_(tmp[p][8][:, 256 + t * 64:256 + (t + 1) * 64].rearrange("p (e j) -> p e j", e=E_MOE), all_, mine, ALU.is_gt)
                link(last)
                gt4 = tmp[p][8][:, 256:512].rearrange("p (t e j) -> p t e j", t=NT, e=E_MOE)
                for t in range(NT):
                    last = tt_(rk[:, t, :, :], rk[:, t, :, :], gt4[:, t, :, :], ADD)
                link(last)
                link(dve.reduce_sum(cmb[:, p, :, :], rk, AX.X))
                link(stt(cmb[:, p, :, :], cmb[:, p, :, :], 2.0, pr, ALU.is_lt, MUL))
                link(dve.reduce_sum(rs[:, p, 2, :], cmb[:, p, :, :], AX.X))
                link(ts(rs[:, p, 2, :], rs[:, p, 2, :], 1e-6, ADD))
                link(dve.reciprocal(rs[:, p, 2, :], rs[:, p, 2, :]))
                link(tt_(cmb[:, p, :, :], cmb[:, p, :, :],
                         rs[:, p, 2, :].unsqueeze(2).broadcast_to([128, NT, E_MOE]), MUL))

            def moe(q):
                def weigh(p, b, e):
                    n = E_MOE * b + e
                    dve.wait_ge(S["mo_y"], n + 1)
                    if n >= 2:
                        dve.wait_ge(S["mo_acc"], n - 1)
                    tt_(r3(ye[e % 2]), r3(bank[6 + e % 2][:, :]),
                        cmb[:, p, :, e].unsqueeze(2).broadcast_to([128, NT, 128]), MUL).then_inc(S["mo_t"], 1)

                work = [(p, b, e) for p, b in enumerate(ids(q)) for e in range(E_MOE)]
                for i, (p, b, e) in enumerate(work):
                    for m, (c0, cn) in enumerate(MT):
                        n = 3 * (E_MOE * b + e) + m
                        dve.wait_ge(S["mo_sg"], n + 1)
                        if e >= 2 or b:
                            dve.wait_ge(S["mo_y"], E_MOE * b + e - 1)
                        tt_(hm[3 * (e % 2) + m][0:cn, :], sg[n % 3][0:cn, :],
                            bank[2 * (n % 3) + 1][0:cn, :], MUL).then_inc(S["mo_h"], 1)
                    if i == 1:
                        route_scores(q, 1)
                    if i:
                        weigh(*work[i - 1])
                    if i == 2:
                        route(q, 1)
                    if LAST >= 8 and q == 0 and i == 2:
                        last_scales()
                    if LAST >= 8 and q == 0 and 3 <= i < 8:
                        last_weights(i - 3)
                weigh(*work[-1])
                for p, b in enumerate(ids(q)):
                    dve.wait_ge(S["mo_acc"], E_MOE * (b + 1))
                    stats(p, Y[p])
                norm(6, q)

            def l3_attn(q):
                if q == 0:
                    dve.wait_ge(S["tab_set"], 1)
                for p, b in enumerate(ids(q)):
                    dve.wait_ge(S["xf_set"], xf_at(6, b))
                    link(tt_(tmp[p][1][:, 0:L], xF[p][:, 1:1 + L], tab[:, 1, :], MUL))
                    m = C("m").to_broadcast([128, L])
                    dve.tensor_tensor_scan(tmp[p][3][:, 0:L], m, tmp[p][1][:, 0:L], vc("lc_im"), MUL, ADD).then_inc(S["c_g"], 1)
                    dve.wait_ge(S["c_in"], at(b))
                    dve.tensor_tensor_scan(tmp[p][2][:, 0:L], m, tmp[p][0][:, 0:L], vc("lc_re"), MUL, ADD).then_inc(S["c_g"], 1)
                for p, b in enumerate(ids(q)):
                    dve.wait_ge(S["c_g"], at(b, 2))
                    link(tt_(tmp[p][4][:, 0:L], tmp[p][2][:, 0:L], tab[:, 2, :], MUL))
                    dve.wait_ge(S["c_t2"], at(b))
                    tt_(tmp[p][4][:, 0:L], tmp[p][4][:, 0:L], tmp[p][5][:, 0:L], SUB).then_inc(S["c_y"], 1)
                for p, b in enumerate(ids(q)):
                    dve.wait_ge(S["c_t"], at(b))
                    link(tt_(Y[p][:, :], P(p, 0)[:, :], xT[p][:, :], ADD))
                    stats(p, Y[p])
                norm(7, q)

            def l3_ffn(q):
                if q == 0:
                    dve.wait_ge(S["q_uv"], 1)
                    dve.wait_ge(S["q_ft"], 2)
                    link(dve.tensor_copy(fcT[:, :], P(0, 2)[:, :]))
                    stt(fcT[:, :], P(0, 1)[:, :], vc("gate"), fcT[:, :], MUL, ADD).then_inc(S["q_fe"], 1)
                for p, b in enumerate(ids(q)):
                    for m in (0, 2):
                        dve.wait_ge(S["h_relu"], 4 * b + m + 1)
                        tt_(tmp[p][4 + m][:, 0:L], tmp[p][m][:, 0:L], tmp[p][m][:, 0:L], MUL).then_inc(S["h_sqd"], 1)
                for p, b in enumerate(ids(q)):
                    dve.wait_ge(S["h_o"], at(b))
                    link(tt_(Y[p][:, :], P(p, 0)[:, :], xT[p][:, :], ADD))
                    stats(p, Y[p])
                norm(8, q)

            dve.memset(QS[0][:, :, :].bitcast(F32), 0.0).then_inc(S["rows_zero"], 1)
            kone = kc[:, 6:7]
            dve.memset(kone, 1.0)
            for q in range(PAIRS):
                l0_attn(q)
                for n, layer in enumerate((l0_ffn, l1_attn, l1_ffn, l2_attn, moe, l3_attn, l3_ffn)):
                    if LAST >= n + 2:
                        layer(q)


def _arrays(i):
    import numpy as np
    g = {n: np.asarray(a) for n, a in i.items()}
    x = g["L0_attn_x"]
    f32 = x.dtype

    def T(a):
        return np.asarray(a).T

    def diag(w):
        d = np.zeros((256, 128), f32)
        for n in range(16):
            d[16 * n:16 * n + 16, 8 * n:8 * n + 8] = w[n]
        return d

    def halves(w):
        return w.reshape(128, NH // 2, 2, HD).transpose(0, 2, 3, 1).reshape(128, 128)

    bdx, bda = diag(g["L1_attn_Wg_x"]), diag(g["L1_attn_Wg_a"])
    w_in, w_out = g["L1_attn_W_in"], g["L1_attn_W_out"]
    blocks = {
        "l0_q": T(g["L0_attn_Wq"]), "l0_v": T(g["L0_attn_Wv"]), "l0_g": T(g["L0_attn_Wg"]), "l0_o": T(g["L0_attn_Wo"]),
        "ident": np.eye(128, dtype=f32),
        "f0_r": T(g["L0_ffn_W_r"]), "f0_k": T(g["L0_ffn_W_k"]), "f0_v": T(g["L0_ffn_W_v"]),
        "in_re": w_in[:, :128], "in_im": w_in[:, 128:], "inT0": T(w_in)[:128], "inT1": T(w_in)[128:],
        "bdx0": bdx[:128], "bdx1": bdx[128:], "bda0": bda[:128], "bda1": bda[128:],
        "out0": w_out[:128], "out1": w_out[128:], "b_out": np.broadcast_to(g["L1_attn_b_out"], (128, 128)),
        "th": g["L1_ffn_theta"], "thn": g["L1_ffn_theta_noise"], "phi": g["L1_ffn_phi"], "phin": g["L1_ffn_phi_noise"],
        "a_q": halves(T(g["L2_attn_Wq"])), "a_k": halves(T(g["L2_attn_Wk"])), "a_v": T(g["L2_attn_Wv"]),
    }
    for t in range(4):
        blocks[f"fc{t}"] = g["L3_ffn_w_fc"][t * 128:(t + 1) * 128]
        blocks[f"pj{t}"] = g["L3_ffn_w_proj"][:, t * 128:(t + 1) * 128]
    vecs = {
        "beta": np.repeat(g["L0_attn_beta"], 8), "gamma": g["L0_attn_ln_gamma"], "lnb": g["L0_attn_ln_beta"],
        "mu_r": g["L0_ffn_mu_r"], "mu_k": g["L0_ffn_mu_k"], "b_re": g["L1_attn_b_in"][:128], "b_im": g["L1_attn_b_in"][128:],
        "bg_x": g["L1_attn_bg_x"], "bg_a": g["L1_attn_bg_a"], "a_re": g["L1_attn_a_real_param"],
        "a_im": g["L1_attn_a_imag_param"], "ph_re": g["L3_attn_phazor_init_re"], "ph_im": g["L3_attn_phazor_init_im"],
        "ph_ang": g["L3_attn_phazor_angle"], "ph_ln": g["L3_attn_ln_minus_ln_phazor_abs"],
        "lc_re": g["L3_attn_last_conv_re"], "lc_im": g["L3_attn_last_conv_im"], "ph_sc": g["L3_attn_ln_phazor_scale"],
        "gate": np.broadcast_to(g["L3_ffn_gate"], (128,)),
    }
    dn = np.zeros((128, 8 * 3, 128), f32)
    for e in range(8):
        for m, (c0, cn) in enumerate(MT):
            dn[:cn, 3 * e + m] = g["L2_ffn_w_down"][e, c0:c0 + cn]
    ar = {
        "xt": x.reshape(B, NT, 128, D).transpose(2, 0, 1, 3).reshape(128, B, L),
        "xf": x.transpose(2, 0, 1),
        "vec": np.stack([vecs[n] for n in VEC], axis=1),
        "wa": np.stack([blocks[n] for n in WA], axis=1),
        "wb": np.stack([blocks[n] for n in WB], axis=1),
        "wc": np.stack([blocks[n] for n in WC], axis=1),
        "small": np.concatenate([T(g["L3_ffn_u"]), g["L3_ffn_v"], T(g["L3_ffn_fast_b"])], axis=1),
        "rt": g["L2_ffn_router_w"],
        "gu": np.stack([g["L2_ffn_w_gate"], g["L2_ffn_w_up"]]).transpose(2, 0, 1, 3),
        "dn": dn,
        "iota": np.broadcast_to(np.arange(1, L + 1, dtype=f32), (128, L)),
        "tri": np.broadcast_to(np.tril(np.ones((8, 8), f32), -1), (128, 8, 8)),
    }
    return {n: np.ascontiguousarray(a) for n, a in ar.items()}


def kernel(**inputs):
    import numpy as _np
    import concourse.bacc as _bacc
    from concourse import mybir as _mybir
    from concourse.bass_utils import run_bass_kernel_spmd as _run

    nc = _bacc.Bacc("TRN2", target_bir_lowering=False, num_devices=1)
    arrays = _arrays(inputs)
    args = [nc.dram_tensor("in_" + n, a.shape, _mybir.dt.from_np(a.dtype), kind="ExternalInput").ap() for n, a in arrays.items()]
    out = nc.dram_tensor("out", (128, B, L), _mybir.dt.float32, kind="ExternalOutput").ap()
    build(nc, *args, out)
    r = _run(nc, [{"in_" + n: a for n, a in arrays.items()}], core_ids=[0])
    y = r.results[0]["out"]
    return _np.ascontiguousarray(_np.asarray(y).reshape(128, B, NT, D).transpose(1, 2, 0, 3).reshape(B, L, D))
```

```python
import concourse.bass as bass
from concourse import mybir
from contextlib import ExitStack

B, L, D = 4, 512, 128
NT = L // 128
PAIRS = 2
NH, HD = 16, 8
NG = 4
E_MOE, I_MOE = 8, 344
EARLY = {2: ("v", 2), 3: ("v", 3), 4: ("q", 2), 5: ("q", 3), 6: ("turn", 2), 7: ("turn", 3),
         8: ("back", 2), 9: ("back", 3), 11: ("g", 2), 12: ("g", 3)}
MT = [(0, 128), (128, 128), (256, 88)]
HID = 512
RANK = 16
VW = HD + 1
LAST = 8
EPS = 1e-5
MAGIC = 1.5 * 2.0 ** 23
MAGIC14 = 1.5 * 2.0 ** 9
TURN = 6.283185
PI_2 = 1.5707962

VEC = ["beta", "gamma", "lnb", "mu_r", "mu_k", "b_re", "b_im", "bg_x", "bg_a", "a_re", "a_im",
       "ph_re", "ph_im", "ph_ang", "ph_ln", "lc_re", "lc_im", "ph_sc", "gate"]
V = {n: i for i, n in enumerate(VEC)}
WA = ["l0_q", "l0_v", "l0_g", "l0_o", "ident"]
WB = ["f0_r", "f0_k", "f0_v", "in_re", "in_im", "inT0", "inT1", "bdx0", "bdx1", "bda0", "bda1",
      "out0", "out1", "b_out", "th", "thn", "phi", "phin", "a_q", "a_k", "a_v"]
WC = ["fc0", "fc1", "fc2", "fc3", "pj0", "pj1", "pj2", "pj3"]


def build(nc, xt_d, xf_d, vec_d, wa_d, wb_d, wc_d, small_d, rt_d, gu_d, dn_d, iota_d, tri_d, out_d):
    F32, BF16, FP16 = mybir.dt.float32, mybir.dt.bfloat16, mybir.dt.float16
    ALU, ACT, AX = mybir.AluOpType, mybir.ActivationFunctionType, mybir.AxisListType
    ADD, SUB, MUL, MAX = ALU.add, ALU.subtract, ALU.mult, ALU.max

    ctx = ExitStack()
    with ctx:
        def sb(name, shape, dt=F32):
            return ctx.enter_context(nc.sbuf_tensor(name, shape, dt))

        def sem(name):
            return ctx.enter_context(nc.semaphore(name))

        xT = [sb(f"xT{p}", [128, L]) for p in range(2)]
        xF = [sb(f"xF{p}", [128, 1 + L]) for p in range(2)]
        Y = [sb(f"Y{p}", [128, L]) for p in range(2)]
        NTMP = 10
        tmp = [[sb(f"tmp{p}_{i}", [128, 1 + L]) for i in range(NTMP)] for p in range(2)]
        vec = sb("vec", [128, len(VEC)])
        wa = sb("wa", [128, len(WA), 128])
        wb = sb("wb", [128, len(WB), 128])
        wc = sb("wc", [128, len(WC), 128])
        small = sb("small", [RANK, HID + 128 + RANK])
        router = sb("router", [128, E_MOE])
        gu = sb("gu", [128, 2, E_MOE, I_MOE])
        dn = sb("dn", [128, E_MOE * 3, 128])
        tri = sb("tri", [128, E_MOE, E_MOE])
        st6 = sb("st6", [128, 3, NT, 6])
        mv = sb("mv", [128, 3, NT, 2])
        rstd = sb("rstd", [128, 3, NT])
        kc = sb("kc", [128, 8])
        sv = sb("sv", [128, 64])
        wgx = sb("wgx", [128, 128])
        wga = sb("wga", [128, 128])
        w_cos = sb("w_cos", [128, 128])
        w_sin = sb("w_sin", [128, 128])
        stmp = sb("stmp", [128, 2, 128])
        tab = sb("tab", [128, 4, L])
        iota = tab[:, 3, :]
        tt = [tmp[1][5][:, 0:L], tmp[0][6][:, 0:L]]
        x0F = [tmp[p][9][:, 0:L] for p in range(2)]
        fcT = sb("fcT", [128, HID])
        pjT = sb("pjT", [128, HID])
        wq_s = [tmp[1][6 + i][:, 0:L] for i in range(2)]
        wo_s = [tmp[0][7][:, 0:L], tmp[0][8][:, 0:L]]
        fsc = sb("fsc", [128, 5, 3])
        uT_m = sb("uT_m", [RANK, 128])
        QS = [sb(f"QS{p}", [128, NH, L], BF16) for p in range(2)]
        KS = [sb(f"KS{p}", [128, NH, L], BF16) for p in range(2)]
        parts = [[[tmp[p][6 + (3 * side + i) // 2][:, :].bitcast(BF16)[:, (3 * side + i) % 2 * L:][:, 0:L]
                   for i in range(3)] for side in range(2)] for p in range(2)]
        VA = [sb(f"VA{p}", [128, NT * NH * VW + 32 - VW]) for p in range(2)]
        PT = [[tmp[i][2 + j][:, 0:L] for j in range(4)] for i in range(2)]
        RC = [[tmp[0][6][:, 0:L], tmp[0][7][:, 0:L], tmp[0][8][:, 0:L], tmp[1][5][:, 0:L]],
              [tmp[1][i][:, 0:L] for i in range(4)]]
        QF = [QS[0][:, 2 * i:2 * i + 2, :].rearrange("p a b -> p (a b)").bitcast(F32) for i in range(8)]
        L0 = [dict(zip(("state", "yq", "sg", "n", "ng", "z"), [tmp[p][i][:, 0:L] for i in range(6)]))
              for p in range(2)]
        L0 += [dict(state=QF[4 * p], yq=QF[4 * p], sg=QF[4 * p + 2], n=QF[4 * p + 1], ng=QF[4 * p],
                    z=QF[4 * p + 2]) for p in range(2)]
        XR = [xT[0][:, :], xT[1][:, :], QF[3], QF[7]]
        YR = [Y[0][:, :], Y[1][:, :], QF[1], QF[5]]
        STAT = [0, 1, 0, 2]
        OS = tmp[0][9][:, 0:L]
        ones_zeros = sb("ones_zeros", [56, L], BF16)
        ones, zeros = ones_zeros[0:24, :], ones_zeros[32:56, :]
        mx = sb("mx", [128, 2, 16])
        mres = sb("mres", [128, 2, 16])
        mp = sb("mp", [128, 2, 48], BF16)
        mrow = sb("mrow", [48, 2, 128], BF16)
        ident_h = sb("ident_h", [128, 128], BF16)
        rden = sb("rden", [128, 2, NT * 4])
        rt = sb("rt", [128, 2, 3, NT, E_MOE])
        rs = sb("rs", [128, 2, 4, NT])
        cmb = sb("cmb", [128, 2, NT, E_MOE])
        hm = [tmp[0][i][:, 0:L] for i in range(6)]
        sg = [tmp[1][i][:, 0:L] for i in range(3)]
        ye = [tmp[1][3 + i][:, 0:L] for i in range(2)]
        two = [ctx.enter_context(nc.psum_tensor(f"two{i}", [128, 2, L], F32)) for i in range(2)]
        bank = [two[i // 2][:, i % 2, :] for i in range(4)]
        bank += [ctx.enter_context(nc.psum_tensor(f"bank{i}", [128, L], F32))[:, :] for i in range(4, 8)]

        def P(p, i):
            return bank[4 * p + i]

        l0_bank = [dict(v=P(p, 1), q=P(p, 0), g=P(p, 2), turn=P(p, 3), back=P(p, 0)) for p in range(2)]
        l0_bank += [{what: bank[6 + i % 2] for i, (what, b2) in EARLY.items() if b2 == b} for b in (2, 3)]

        KHALF, KE, KM1, KPI2, KLN = range(5)
        NAMES = ["lam", "one_r", "one_k", "hbx", "hba", "Lh", "ai4", "m", "w", "u1", "dd", "t0", "t1", "t2",
                 "t3", "soft", "y", "gateC", "ir", "om", "z"]
        S_ = {n: i for i, n in enumerate(NAMES)}

        def C(n):
            return sv[:, S_[n]:S_[n] + 1]

        def vc(n):
            return vec[:, V[n]:V[n] + 1]

        def k(i):
            return kc[:, i:i + 1]

        ident = wa[:, WA.index("ident"), :]

        def W(n):
            return wa[:, WA.index(n), :] if n in WA else wb[:, WB.index(n), :]

        def r3(ap):
            return ap.rearrange("p (t c) -> p t c", t=NT)

        ld_t = [sem(f"ld_t{b}") for b in range(B)]
        ld_x = [sem(f"ld_x{b}") for b in range(B)]
        S = {}
        for line in (
            "ld_a ld_b ld_c ld_m ld_o rows_zero zeroed ones_set consts lam_set mix_set bias_half gates_set",
            "soft_u soft_ln soft_s log_s ph_arg ph_trig tab_set th_arg th_trig wc_bias wc_set",
            "stats_mv rstd_set ln_done x_turned xf_set",
            "l0_v l0_state l0_q l0_g l0_sg l0_yq l0_yt l0_nt l0_ng l0_z l0_o f0_mix f0_xrk f0_k f0_r f0_kk f0_tr f0_v",
            "g_pre g_xh g_ta g_tx g_mag g_t g_w g_arg g_trig g_xr g_rot g_scan g_hr g_hi g_o g_xb f1_ri",
            "f1_sq f1_ss f1_rt",
            "at_qkv at_hi at_mid at_r1 at_parts at_mz at_v at_va at_s at_max at_mp at_mt at_mrow at_e at_p",
            "at_pv at_os at_ot at_res",
            "rt_l rt_s rt_e mo_gu mo_sg mo_h mo_y mo_t mo_acc",
            "c_in c_g c_t2 c_y c_t q_fc q_uv q_um q_uc q_ft q_fe h_pre h_relu h_sqd h_sqp h_o",
            "dchain achain pchain",
        ):
            S.update((n, sem(n)) for n in line.split())
        out_dma = [sem(f"out_dma{b}") for b in range(B)]
        at_qs = [sem(f"at_qs{p}") for p in range(2)]
        at_ks = [sem(f"at_ks{p}") for p in range(2)]
        at_m = [sem(f"at_m{i}") for i in range(2)]

        def at(b, steps=1):
            return steps * (b + 1)

        ln_order = []
        for q in range(PAIRS):
            b0, b1 = 2 * q, 2 * q + 1
            ln_order += [(n, b) for n in range(2 * q, 6) for b in (b0, b1)]
            ln_order += [(0, b0 + 2), (0, b1 + 2)] if q == 0 else []
            ln_order += [(6, b0), (7, b0), (6, b1), (7, b1), (8, b0)]
            ln_order += [(1, b0 + 2), (1, b1 + 2)] if q == 0 else []
            ln_order += [(8, b1)]

        def ln_at(n, b):
            return ln_order.index((n, b)) + 1

        def xf_at(n, b):
            turn = 10 + 2 * (b % 2) + n - 6 if n in (6, 7) else 2 * (n - 1) + b % 2
            return 2 * (LAST - 1) * (b // 2) + turn + 1

        def heads(a):
            return a[:, 0:L].rearrange("p (t h d) -> p t h d", t=NT, h=NH)

        def values(p):
            return VA[p][:, 0:NT * NH * VW].rearrange("p (t h c) -> p t h c", t=NT, h=NH)

        def ids(q):
            return (2 * q, 2 * q + 1)

        def spread(queue, p, b, landed, shares):
            for (part, side), halves in shares.items():
                if part < 2:
                    queue.wait_ge(S[("at_hi", "at_mid")[part]], 2 * b + 1 + side)
                else:
                    queue.wait_ge(S["at_parts"], at(b))
                rows, order = ((QS, (0, 0, 1, 1, 0, 2)), (KS, (0, 1, 0, 1, 2, 0)))[side]
                for r in (r for r in range(6) if order[r] == part):
                    for hh in halves:
                        queue.dma_start(rows[p][64 * hh + 8 * r:64 * hh + 8 * r + 8, 8 * hh:8 * hh + 8, :],
                                        parts[p][side][part][64 * hh:64 * hh + 64, :]).then_inc(landed, 16)

        block = ctx.enter_context(nc.Block())

        @block.sync
        def _(sp):
            sp.dma_start(x0F[0], xf_d[:, 0, :]).then_inc(ld_x[0], 16)
            sp.dma_start(wa[:, :, :], wa_d).then_inc(S["ld_a"], 16)
            sp.dma_start(vec[:, :], vec_d).then_inc(S["ld_a"], 16)
            sp.dma_start(x0F[1], xf_d[:, 1, :]).then_inc(ld_x[1], 16)
            for b in range(2):
                sp.dma_start(xT[b][:, :], xt_d[:, b, :]).then_inc(ld_t[b], 16)
            sp.dma_start(iota, iota_d).then_inc(S["ld_b"], 16)
            sp.dma_start(wb[:, :, :], wb_d).then_inc(S["ld_b"], 16)
            sp.dma_start(wc[:, :, :], wc_d).then_inc(S["ld_c"], 16)
            sp.dma_start(small[:, :], small_d).then_inc(S["ld_c"], 16)
            sp.dma_start(gu[:, 0, :, :], gu_d[:, 0, :, :]).then_inc(S["ld_m"], 16)
            sp.dma_start(gu[:, 1, :, :], gu_d[:, 1, :, :]).then_inc(S["ld_m"], 16)
            sp.dma_start(dn[:, :, :], dn_d).then_inc(S["ld_m"], 16)
            sp.dma_start(router[:, :], rt_d).then_inc(S["ld_m"], 16)
            sp.dma_start(tri[:, :, :], tri_d).then_inc(S["ld_m"], 16)
            sp.wait_ge(S["rows_zero"], 4)
            sp.wait_ge(S["ones_set"], 1)
            for p in range(2):
                for hh in range(2):
                    sp.dma_start(KS[p][64 * hh + 48:64 * hh + 51, 8 * hh:8 * hh + 8, :], ones).then_inc(S["ld_o"], 16)
            for q in range(PAIRS):
                if q:
                    sp.wait_ge(S["at_pv"], 2 * NT * 2 * NG * q)
                    for hh in range(2):
                        sp.dma_start(QS[1][64 * hh + 48:64 * hh + 51, 8 * hh:8 * hh + 8, :],
                                     zeros).then_inc(S["at_mz"], 16)
                    sp.wait_ge(S["rows_zero"], 5)
                for p, b in enumerate(ids(q)):
                    spread(sp, p, b, at_qs[p], {(part, side): (1,) if side else (0, 1) for part in range(3)
                                               for side in range(2) if (part, side) not in ((1, 1), (2, 1))})
                for v in range(2 * NG):
                    u = 2 * NG * q + v
                    p, g = v // NG, v % NG
                    sp.wait_ge(S["at_mrow"], u + 1)
                    for hh in range(2):
                        sp.dma_start(QS[p][64 * hh + 48:64 * hh + 51, 8 * hh + 2 * g:8 * hh + 2 * g + 2, :],
                                     mrow[24 * hh:24 * hh + 24, v % 2, :]).then_inc(at_m[u % 2], 16)
                for p, b in enumerate(ids(q)):
                    if b + 2 < B:
                        sp.wait_ge(S["at_ot"], 2 * NG * (q + 1))
                        sp.dma_start(x0F[p], xf_d[:, b + 2, :]).then_inc(ld_x[b + 2], 16)
                        sp.dma_start(XR[b + 2], xt_d[:, b + 2, :]).then_inc(ld_t[b + 2], 16)
                for p, b in enumerate(ids(q)):
                    sp.wait_ge(S["ln_done"], ln_at(LAST, b))
                    sp.dma_start(out_d[:, b, :], Y[p][:, :]).then_inc(out_dma[b], 16)
            for n, v in (("ld_a", 32), ("ld_b", 32), ("ld_c", 32), ("ld_m", 80), ("ld_o", 64)):
                sp.wait_ge(S[n], v)
            for b in range(B):
                sp.wait_ge(out_dma[b], 16)

        @block.tensor
        def _(pe):
            def token_major(out, act, w, first=True, last=True, tiles=range(NT)):
                for t in tiles:
                    mm = pe.matmul(out[:, t * 128:(t + 1) * 128], act[:, t * 128:(t + 1) * 128], w,
                                   start=first, stop=last)
                return mm

            def turn(out, src):
                for t in range(NT):
                    mm = pe.transpose(out[:, t * 128:(t + 1) * 128], src[:, t * 128:(t + 1) * 128], ident)
                return mm

            def turn_x(n, q):
                for p, b in enumerate(ids(q)):
                    pe.wait_ge(S["ln_done"], ln_at(n, b))
                    if n == 2 and b == 0:
                        pe.wait_ge(S["wc_set"], 2)
                    turn(P(p, 3), xT[p]).then_inc(S["x_turned"], 1)

            def l0_step(what, b):
                out = l0_bank[b][what]
                if what == "turn":
                    pe.wait_ge(S["l0_yq"], at(b))
                    turn(out, L0[b]["yq"]).then_inc(S["l0_yt"], 1)
                elif what == "back":
                    pe.wait_ge(S["ln_done"], ln_at(0, b))
                    turn(out, L0[b]["n"]).then_inc(S["l0_nt"], 1)
                else:
                    pe.wait_ge(ld_x[b], 16)
                    if b == 0:
                        pe.wait_ge(S["ld_a"], 32)
                    pe.matmul(out, W("l0_" + what), x0F[b % 2], start=True, stop=True).then_inc(S["l0_" + what], 1)

            def l0_taken(what, b):
                if what == "v":
                    pe.wait_ge(S["l0_state"], at(b))
                elif what == "q":
                    pe.wait_ge(S["l0_yq"], at(b))
                elif what == "g":
                    pe.wait_ge(S["l0_sg"], at(b))
                elif what == "turn":
                    pe.wait_ge(S["ln_done"], ln_at(0, b))
                else:
                    pe.wait_ge(S["l0_ng"], at(b))

            def l0_attn(q):
                if q == 0:
                    for b in ids(q):
                        for what in ("v", "q", "g"):
                            l0_step(what, b)
                    for what in ("turn", "back"):
                        for b in ids(q):
                            l0_step(what, b)
                    for b in ids(q):
                        l0_out(b)

            def l0_out(b):
                pe.wait_ge(S["l0_z"], at(b))
                if b >= 2:
                    pe.wait_ge(S["h_relu"], 4 * (b - 2) + 2)
                token_major(P(b % 2, 1), L0[b]["z"], W("l0_o")).then_inc(S["l0_o"], 1)

            def l0_ffn(q):
                for p, b in enumerate(ids(q)):
                    if b == 0:
                        pe.wait_ge(S["ld_b"], 32)
                    pe.wait_ge(S["f0_xrk"], at(b))
                    pe.matmul(P(p, 1)[:, :], W("f0_k"), tmp[p][3][:, 0:L], start=True, stop=True).then_inc(S["f0_k"], 1)
                    token_major(P(p, 0), tmp[p][2], W("f0_r")).then_inc(S["f0_r"], 1)
                if q == 0:
                    gate_weights()
                for p, b in enumerate(ids(q)):
                    pe.wait_ge(S["f0_kk"], at(b))
                    token_major(P(p, 2), tmp[p][5], W("f0_v")).then_inc(S["f0_v"], 1)

            def gate_weights():
                pe.wait_ge(S["ld_b"], 32)
                for i, (w0, w1) in enumerate((("bdx0", "bdx1"), ("bda0", "bda1"))):
                    pe.matmul(P(0, 3)[:, i * 128:(i + 1) * 128], W("inT0"), W(w0), start=True, stop=False)
                    pe.matmul(P(0, 3)[:, i * 128:(i + 1) * 128], W("inT1"), W(w1), start=False, stop=True)
                    pe.matmul(P(0, 3)[:, 256 + i:257 + i], W(w0), vc("b_re"), start=True, stop=False)
                    mm = pe.matmul(P(0, 3)[:, 256 + i:257 + i], W(w1), vc("b_im"), start=False, stop=True)
                mm.then_inc(S["wc_bias"], 1)

            def l1_attn(q):
                for p, b in enumerate(ids(q)):
                    pe.wait_ge(S["xf_set"], xf_at(2, b))
                    if b == 0:
                        pe.wait_ge(S["wc_set"], 2)
                    pe.matmul(P(p, 3)[:, :], wga[:, :], xF[p][:, 1:1 + L], start=True,
                              stop=True).then_inc(S["g_pre"], 1)
                for p, b in enumerate(ids(q)):
                    pe.matmul(P(p, 2)[:, :], wgx[:, :], xF[p][:, 1:1 + L], start=True,
                              stop=True).then_inc(S["g_pre"], 1)
                for p, b in enumerate(ids(q)):
                    x = xF[p][:, 1:1 + L]
                    pe.matmul(P(p, 0)[:, :], W("in_re"), x, start=True, stop=True)
                    pe.matmul(P(p, 1)[:, :], W("in_im"), x, start=True, stop=True).then_inc(S["g_xh"], 1)
                for p, b in enumerate(ids(q)):
                    pe.wait_ge(S["g_hr"], at(b))
                    if p == 0:
                        pe.wait_ge(S["g_hi"], q + 1)
                    for t in range(NT):
                        token_major(P(p, 2), tmp[p][5], W("out0"), last=False, tiles=[t])
                        mm = token_major(P(p, 2), tmp[p][8], W("out1"), first=False, tiles=[t])
                    mm.then_inc(S["g_o"], 1)

            def l1_ffn(q):
                for p, b in enumerate(ids(q)):
                    pe.wait_ge(S["xf_set"], xf_at(3, b))
                    if b == 0:
                        pe.wait_ge(S["th_trig"], 2)
                    x = xF[p][:, 1:1 + L]
                    token_major(P(p, 0), x, w_cos[:, :])
                    token_major(P(p, 1), x, w_sin[:, :]).then_inc(S["f1_ri"], 1)

            def l2_attn(q):
                for p, b in enumerate(ids(q)):
                    pe.wait_ge(S["xf_set"], xf_at(4, b))
                    x = xF[p][:, 1:1 + L]
                    pe.matmul(P(p, 0)[:, :], W("a_q"), x, start=True, stop=True).then_inc(S["at_qkv"], 1)
                    pe.matmul(P(p, 1)[:, :], W("a_k"), x, start=True, stop=True).then_inc(S["at_qkv"], 1)
                    token_major(P(p, 2), x, W("a_v")).then_inc(S["at_v"], 1)

                u0 = 2 * NG * q

                def stack(arr, j, g):
                    return arr[:, 8 * (j % 2) + 2 * g + j // 2, :]

                def score_tile(u, i):
                    v = u - u0
                    p, g = v // NG, v % NG
                    n = 8 * u + i
                    jj, qt = i % 2, i // 2
                    if i == 0 and u == 0:
                        pe.wait_ge(S["ld_o"], 64)
                    if i == 0 and v == 0 and q:
                        pe.wait_ge(S["at_mz"], 32)
                    if i == 0 and g == 0:
                        pe.wait_ge(at_qs[p], 16 * 15 * (q + 1))
                        pe.wait_ge(at_ks[p], 16 * 9 * (q + 1))
                    if n >= 2:
                        pe.wait_ge(S["at_max"], n - 1)
                    for s in range(2):
                        j = 2 * jj + s
                        mm = pe.matmul(bank[2 * (i % 2) + s][:, :],
                                       stack(QS[p], j, g)[:, qt * 128:(qt + 1) * 128],
                                       stack(KS[p], j, g), start=True, stop=True)
                    mm.then_inc(S["at_s"], 1)

                def turn_max(u):
                    pe.wait_ge(S["at_mp"], u + 1)
                    if u > 2:
                        pe.wait_ge(S["at_res"], max(u - 2, u0))
                    if u == u0 + 2 * NG - 1:
                        pe.wait_ge(S["xf_set"], xf_at(5, 2 * q))
                    pe.transpose(bank[7].bitcast(BF16)[0:48, 0:128], mp[:, u % 2, :],
                                 ident_h[:, :]).then_inc(S["at_mt"], 1)

                def exp_tile(u, i):
                    v = u - u0
                    p, g = v // NG, v % NG
                    kt, j = i // 4, i % 4
                    n = 16 * u + i
                    if i == 0:
                        pe.wait_ge(at_m[u % 2], 16 * 2 * (u // 2 + 1))
                    if n >= 2:
                        pe.wait_ge(S["at_p"], n - 1)
                    pe.matmul(bank[4 + i % 2][:, :], stack(KS[p], j, g)[:, kt * 128:(kt + 1) * 128],
                              stack(QS[p], j, g), start=True, stop=True).then_inc(S["at_e"], 1)

                def weigh(u, kt, half):
                    v = u - u0
                    p, g = v // NG, v % NG
                    q0 = half * (L // 2)
                    if kt == 0 and half == 0:
                        if u:
                            pe.wait_ge(S["at_os"], u)
                        if g == 0:
                            pe.wait_ge(S["at_va"], 2 * q + p + 1)
                    pe.wait_ge(S["at_p"], 16 * u + 4 * kt + 4)
                    for j in range(4):
                        c = (kt * NH + 4 * g + j) * VW
                        mm = pe.matmul(bank[6][32 * j:32 * j + 32, q0:q0 + L // 2], VA[p][:, c:c + 32],
                                       PT[kt % 2][j][:, q0:q0 + L // 2], start=(kt == 0 and half == 0),
                                       stop=(kt == NT - 1 and half == 1))
                    mm.then_inc(S["at_pv"], 1)

                def turn_out(u):
                    pe.wait_ge(S["at_os"], u + 1)
                    pe.wait_ge(S["at_mrow"], min(u + 3, u0 + 2 * NG))
                    if u > u0:
                        pe.wait_ge(S["at_res"], u)
                    if u >= u0 + 2 * NG - 2:
                        pe.wait_ge(S["rt_s"], 2 * q + 1)
                    turn(bank[7], OS).then_inc(S["at_ot"], 1)

                pe.wait_ge(S["at_r1"], at(2 * q + 1, 2))
                pe.wait_ge(S["at_va"], 2 * q + 2)
                for i in range(8):
                    score_tile(u0, i)
                for i in range(8):
                    score_tile(u0 + 1, i)
                    if i == 1:
                        turn_max(u0)
                for v in range(2 * NG):
                    u = u0 + v
                    for i in range(8):
                        exp_tile(u, 2 * i)
                        if v + 2 < 2 * NG:
                            score_tile(u + 2, i)
                        exp_tile(u, 2 * i + 1)
                        if i >= 2:
                            weigh(u, i // 2 - 1, i % 2)
                        elif v:
                            weigh(u - 1, 3, i)
                        if i == 2 and v + 1 < 2 * NG:
                            turn_max(u + 1)
                        if i == 5 and v:
                            turn_out(u - 1)
                        if i == 7 and v == 2 * NG - 3:
                            pe.wait_ge(S["at_res"], u)
                            turn_in(7, 5, q, 0)
                        if i == 7 and v == 2 * NG - 2:
                            pe.wait_ge(S["at_res"], u)
                            logits(q, 0)
                for half in range(2):
                    weigh(u0 + 2 * NG - 1, 3, half)
                turn_out(u0 + 2 * NG - 1)

            def turn_in(bk, n, q, p):
                pe.wait_ge(S["ln_done"], ln_at(n, 2 * q + p))
                turn(bank[bk], xT[p]).then_inc(S["x_turned"], 1)

            def logits(q, p):
                if q == 0 and p == 0:
                    pe.wait_ge(S["ld_m"], 80)
                pe.wait_ge(S["xf_set"], xf_at(5, 2 * q + p))
                for t in range(NT):
                    mm = pe.matmul(bank[7][:, t * E_MOE:(t + 1) * E_MOE],
                                   xF[p][:, 1 + t * 128:1 + (t + 1) * 128], router[:, :], start=True, stop=True)
                mm.then_inc(S["rt_l"], 1)

            def moe(q):
                def up(p, b, e):
                    for m, (c0, cn) in enumerate(MT):
                        n = 3 * (E_MOE * b + e) + m
                        if n >= 3:
                            pe.wait_ge(S["mo_h"], n - 2)
                        for s in range(2):
                            mm = pe.matmul(bank[2 * (n % 3) + s][0:cn, :], gu[:, s, e, c0:c0 + cn],
                                           xF[p][:, 1:1 + L], start=True, stop=True)
                        mm.then_inc(S["mo_gu"], 1)

                def down(p, b, e):
                    n = E_MOE * b + e
                    pe.wait_ge(S["mo_h"], 3 * n + 3)
                    if p == 0 and e == 1:
                        pe.wait_ge(S["rt_s"], 2 * q + 2)
                    if p == 1 and e == 2:
                        pe.wait_ge(S["xf_set"], xf_at(6, 2 * q))
                    if p == 1 and e == 5:
                        pe.wait_ge(S["stats_mv"], ln_at(7, 2 * q))
                    if p == 1 and e == 7:
                        pe.wait_ge(S["xf_set"], xf_at(7, 2 * q))
                    if n in EARLY:
                        l0_taken(*EARLY[n])
                    if n >= 2:
                        pe.wait_ge(S["mo_t"], n - 1)
                    for t in range(NT):
                        for m, (c0, cn) in enumerate(MT):
                            mm = pe.matmul(bank[6 + e % 2][:, t * 128:(t + 1) * 128],
                                           hm[3 * (e % 2) + m][0:cn, t * 128:(t + 1) * 128],
                                           dn[0:cn, 3 * e + m, :], start=(m == 0), stop=(m == 2))
                    mm.then_inc(S["mo_y"], 1)

                work = [(p, b, e) for p, b in enumerate(ids(q)) for e in range(E_MOE)]
                for i, w in enumerate(work):
                    up(*w)
                    if i == 0:
                        pe.wait_ge(S["at_res"], 2 * NG * (q + 1))
                        turn_in(7, 5, q, 1)
                    if i == 1:
                        logits(q, 1)
                    if i:
                        down(*work[i - 1])
                    if q == 0 and i in EARLY:
                        pe.wait_ge(S["mo_t"], i - 1)
                        l0_step(*EARLY[i])
                    if i == 10:
                        pe.wait_ge(S["mo_t"], E_MOE * (2 * q + 1) + 1)
                        turn_in(6, 6, q, 0)
                    if i == 13:
                        pe.wait_ge(S["mo_t"], E_MOE * (2 * q + 1) + 4)
                        turn_rc(7, q, 0)
                    if i == 15:
                        pe.wait_ge(S["mo_t"], E_MOE * (2 * q + 1) + 6)
                        turn_in(7, 7, q, 0)
                down(*work[-1])

            def turn_rc(bk, q, p):
                pe.wait_ge(S["c_y"], 2 * q + p + 1)
                turn(bank[bk], RC[p][0]).then_inc(S["c_t"], 1)

            def last_weights():
                pe.wait_ge(S["ld_c"], 32)
                pe.wait_ge(S["mo_h"], 3 * E_MOE * 2)
                pe.matmul(P(0, 0)[0:RANK, 0:128], small[:, HID + 128:HID + 128 + RANK],
                          small[:, HID:HID + 128], start=True, stop=True).then_inc(S["q_um"], 1)
                pe.wait_ge(S["q_uc"], 1)
                pe.matmul(P(0, 1)[:, :], uT_m[:, :], small[:, 0:HID], start=True, stop=True).then_inc(S["q_uv"], 1)
                pe.wait_ge(S["q_fc"], 2)
                turn(P(0, 2), wq_s[0])
                turn(P(0, 3), wq_s[1]).then_inc(S["q_ft"], 1)

            def hidden(q, p):
                b = 2 * q + p
                pe.wait_ge(S["xf_set"], xf_at(7, b))
                pe.wait_ge(S["mo_h"], 3 * E_MOE * 2 * (q + 1))
                if b == 0:
                    pe.wait_ge(S["q_fe"], 1)
                for m in range(4):
                    pe.matmul(P(p, m)[:, :], fcT[:, m * 128:(m + 1) * 128], xF[p][:, 1:1 + L],
                              start=True, stop=True).then_inc(S["h_pre"], 1)

            def project(q, p):
                b = 2 * q + p
                pe.wait_ge(S["h_sqd"], at(b, 2))
                pe.wait_ge(S["h_sqp"], at(b, 2))
                for t in range(NT):
                    for m in range(4):
                        mm = token_major(P(p, 0), tmp[p][4 + m], pjT[:, m * 128:(m + 1) * 128],
                                         first=(m == 0), last=(m == 3), tiles=[t])
                mm.then_inc(S["h_o"], 1)

            def l3(q):
                if q == 0:
                    last_weights()
                else:
                    hidden(q, 0)
                pe.wait_ge(S["mo_t"], E_MOE * (2 * q + 2))
                turn_in(7, 6, q, 1)
                if q == 0:
                    hidden(q, 0)
                project(q, 0)
                turn_rc(4, q, 1)
                turn_in(7, 7, q, 1)
                pe.wait_ge(S["stats_mv"], ln_at(7, 2 * q + 1))
                hidden(q, 1)
                if q == 0:
                    l0_out(2)
                    l0_out(3)
                project(q, 1)

            for q in range(PAIRS):
                l0_attn(q)
                turn_x(1, q)
                l0_ffn(q)
                turn_x(2, q)
                l1_attn(q)
                turn_x(3, q)
                l1_ffn(q)
                turn_x(4, q)
                l2_attn(q)
                moe(q)
                l3(q)

        @block.scalar
        def _(act):
            n_chain = [0]

            def link(ins):
                n_chain[0] += 1
                ins.then_inc(S["achain"], 1)
                act.wait_ge(S["achain"], n_chain[0])

            def put_in(bk, n, q, p):
                act.wait_ge(S["x_turned"], xf_at(n, 2 * q + p))
                act.activation(xF[p][:, 1:1 + L], bank[bk], ACT.Copy).then_inc(S["xf_set"], 1)

            def l0_gate(b):
                act.wait_ge(S["l0_g"], at(b))
                act.activation(L0[b]["sg"], l0_bank[b]["g"], ACT.Silu).then_inc(S["l0_sg"], 1)

            def l0_scale(b):
                act.wait_ge(S["l0_nt"], at(b))
                act.activation(L0[b]["ng"], l0_bank[b]["back"], ACT.Identity, scale=vc("gamma"),
                               bias=vc("lnb")).then_inc(S["l0_ng"], 1)

            def router_exp(q, p):
                act.wait_ge(S["rt_s"], 2 * q + p + 1)
                act.activation(rt[:, p, 1, :, :], rt[:, p, 0, :, :], ACT.Exp).then_inc(S["rt_e"], 1)

            def put_x(n, q):
                for p, b in enumerate(ids(q)):
                    act.wait_ge(S["x_turned"], xf_at(n, b))
                    if n == 1 and b == 0:
                        act.wait_ge(S["zeroed"], 1)
                    act.activation(xF[p][:, 1:1 + L], P(p, 3)[:, :], ACT.Copy).then_inc(S["xf_set"], 1)

            act.wait_ge(S["consts"], 1)
            act.wait_ge(S["soft_u"], 1)
            act.activation(C("t0"), C("u1"), ACT.Ln).then_inc(S["soft_ln"], 1)

            for q in range(PAIRS):
                if q == 0:
                    for b in ids(q):
                        l0_gate(b)
                    for b in ids(q):
                        l0_scale(b)
                if q == 0:
                    act.wait_ge(S["soft_s"], 1)
                    act.activation(C("y"), C("t3"), ACT.Ln).then_inc(S["log_s"], 1)
                put_x(1, q)
                for p, b in enumerate(ids(q)):
                    if b == 0:
                        act.wait_ge(S["mix_set"], 1)
                    act.wait_ge(S["xf_set"], xf_at(1, b))
                    act.activation(tmp[p][0][:, :], xF[p][:, :], ACT.Copy, scale=C("one_k"))
                    act.activation(tmp[p][1][:, :], xF[p][:, :], ACT.Copy, scale=C("one_r")).then_inc(S["f0_mix"], 1)
                for p, b in enumerate(ids(q)):
                    act.wait_ge(S["f0_k"], at(b))
                    link(act.activation(tmp[p][4][:, 0:L], P(p, 1)[:, :], ACT.Relu))
                    act.activation(tmp[p][5][:, 0:L], tmp[p][4][:, 0:L], ACT.Square).then_inc(S["f0_kk"], 1)
                for p, b in enumerate(ids(q)):
                    act.wait_ge(S["f0_r"], at(b))
                    act.activation(tmp[p][6][:, 0:L], P(p, 0)[:, :], ACT.Tanh, scale=0.5).then_inc(S["f0_tr"], 1)
                if q == 0:
                    act.wait_ge(S["bias_half"], 1)
                    act.activation(wgx[:, :], P(0, 3)[:, 0:128], ACT.Copy).then_inc(S["wc_set"], 1)
                    act.activation(wga[:, :], P(0, 3)[:, 128:256], ACT.Copy).then_inc(S["wc_set"], 1)
                put_x(2, q)
                for p, b in enumerate(ids(q)):
                    act.wait_ge(S["g_pre"], 4 * q + p + 1)
                    link(act.activation(tmp[p][0][:, 0:L], P(p, 3)[:, :], ACT.Tanh, scale=0.5,
                                        bias=C("hba")))
                    act.activation(tmp[p][4][:, 0:L], tmp[p][0][:, 0:L], ACT.Identity, scale=C("ai4"),
                                   bias=C("ai4")).then_inc(S["g_ta"], 1)
                for p, b in enumerate(ids(q)):
                    act.wait_ge(S["g_pre"], 4 * q + p + 3)
                    act.activation(tmp[p][1][:, 0:L], P(p, 2)[:, :], ACT.Tanh, scale=0.5,
                                   bias=C("hbx")).then_inc(S["g_tx"], 1)
                act.preload_act_table_set("natural_log_exp_and_others")
                if q == 0:
                    act.wait_ge(S["gates_set"], 1)
                for p, b in enumerate(ids(q)):
                    act.wait_ge(S["g_ta"], at(b))
                    act.activation(tmp[p][2][:, 0:L], tmp[p][0][:, 0:L], ACT.Exp, scale=C("Lh"),
                                   bias=C("Lh")).then_inc(S["g_mag"], 1)
                for p, b in enumerate(ids(q)):
                    act.wait_ge(S["g_t"], at(b))
                    link(act.activation(tmp[p][3][:, 0:L], tmp[p][3][:, 0:L], ACT.Ln))
                    act.activation(tmp[p][3][:, 0:L], tmp[p][3][:, 0:L], ACT.Exp, scale=0.5,
                                   bias=k(KLN)).then_inc(S["g_w"], 1)
                for p, b in enumerate(ids(q)):
                    act.wait_ge(S["g_arg"], at(b))
                    act.activation(tmp[p][7][:, 0:L], tmp[p][5][:, 0:L], ACT.Sin, scale=-TURN)
                    act.activation(tmp[p][8][:, 0:L], tmp[p][6][:, 0:L], ACT.Sin, scale=-TURN,
                                   bias=k(KPI2)).then_inc(S["g_trig"], 1)
                if q == 0:
                    act.wait_ge(S["th_arg"], 1)
                    act.activation(w_cos[:, :], stmp[:, 0, :], ACT.Sin, scale=-TURN,
                                   bias=k(KPI2)).then_inc(S["th_trig"], 1)
                    act.activation(w_sin[:, :], stmp[:, 1, :], ACT.Sin, scale=-TURN).then_inc(S["th_trig"], 1)
                put_x(3, q)
                for p, b in enumerate(ids(q)):
                    act.wait_ge(S["f1_ri"], at(b))
                    act.activation(tmp[p][0][:, 0:L], P(p, 0)[:, :], ACT.Square)
                    act.activation(tmp[p][1][:, 0:L], P(p, 1)[:, :], ACT.Square).then_inc(S["f1_sq"], 1)
                for p, b in enumerate(ids(q)):
                    act.wait_ge(S["f1_ss"], at(b))
                    act.activation(tmp[p][3][:, 0:L], tmp[p][2][:, 0:L], ACT.Sqrt).then_inc(S["f1_rt"], 1)
                put_x(4, q)
                for p, b in enumerate(ids(q)):
                    for side in range(2):
                        act.wait_ge(S["at_qkv"], at(b, 2) - 1 + side)
                        act.activation(parts[p][side][0], P(p, side)[:, :], ACT.Copy).then_inc(S["at_hi"], 1)
                    for side in range(2):
                        act.wait_ge(S["at_r1"], at(b, 2) - 1 + side)
                        act.activation(parts[p][side][1], tmp[p][side][:, 0:L], ACT.Copy).then_inc(S["at_mid"], 1)
                    act.wait_ge(S["at_v"], at(b))
                    if b == 0:
                        act.wait_ge(S["ones_set"], 1)
                    act.activation(values(p)[:, :, :, 0:HD], heads(P(p, 2)), ACT.Copy).then_inc(S["at_va"], 1)
                u0 = 2 * NG * q

                def take_out(u):
                    act.wait_ge(S["at_pv"], 2 * NT * (u + 1))
                    if u:
                        act.wait_ge(S["at_ot"], u)
                    act.activation(OS, bank[6][:, :], ACT.Copy).then_inc(S["at_os"], 1)

                act.preload_act_table_set("exp_and_others")
                for u in range(u0, u0 + 2 * NG):
                    for i in range(16):
                        n = 16 * u + i
                        act.wait_ge(S["at_e"], n + 1)
                        if n >= 8 and i % 4 == 0:
                            act.wait_ge(S["at_pv"], 2 * (n // 4 - 1))
                        act.activation(PT[(i // 4) % 2][i % 4], bank[4 + i % 2][:, :], ACT.Exp,
                                       scale=float(HD) ** -0.5).then_inc(S["at_p"], 1)
                        if i == 2 and u > u0:
                            take_out(u - 1)
                        if i == 1 and u == u0 + 2 * NG - 2:
                            put_in(7, 5, q, 0)
                        if i == 6 and u == u0 + 2 * NG - 1:
                            router_exp(q, 0)
                take_out(u0 + 2 * NG - 1)
                for p, b in enumerate(ids(q)):
                    for e in range(E_MOE):
                        for m, (c0, cn) in enumerate(MT):
                            n = 3 * (E_MOE * b + e) + m
                            if n == 6:
                                act.wait_ge(S["ph_arg"], 1)
                                act.activation(tt[0], tab[:, 0, :], ACT.Sin, scale=-TURN)
                                act.activation(tt[1], tab[:, 1, :], ACT.Sin, scale=-TURN,
                                               bias=k(KPI2)).then_inc(S["ph_trig"], 1)
                            act.wait_ge(S["mo_gu"], n + 1)
                            if n >= 3:
                                act.wait_ge(S["mo_h"], n - 2)
                            act.activation(sg[n % 3][0:cn, :], bank[2 * (n % 3)][0:cn, :],
                                           ACT.Silu).then_inc(S["mo_sg"], 1)
                        what, b2 = EARLY.get(E_MOE * b + e, ("", 0))
                        if what == "g":
                            l0_gate(b2)
                        if what == "back":
                            l0_scale(b2)
                        if p == 0 and e == 0:
                            put_in(7, 5, q, 1)
                        if p == 0 and e == 1:
                            router_exp(q, 1)
                        if p == 1 and e == 2:
                            put_in(6, 6, q, 0)
                        if p == 1 and e == 7:
                            put_in(7, 7, q, 0)
                if q == 0:
                    act.wait_ge(S["q_um"], 1)
                    act.activation(uT_m[:, :], P(0, 0)[0:RANK, 0:128], ACT.Copy).then_inc(S["q_uc"], 1)
                    act.wait_ge(S["q_ft"], 1)
                    act.activation(pjT[:, :], P(0, 3)[:, :], ACT.Copy).then_inc(S["q_ft"], 1)
                    put_in(7, 6, q, 1)
                for p, b in enumerate(ids(q)):
                    if p:
                        put_in(7, 7, q, 1)
                    for m in range(4):
                        act.wait_ge(S["h_pre"], 4 * b + m + 1)
                        act.activation(tmp[p][m][:, 0:L], P(p, m)[:, :], ACT.Relu).then_inc(S["h_relu"], 1)
                    if p == 0 and q:
                        put_in(7, 6, q, 1)

        @block.gpsimd
        def _(pool):
            n_chain = [0]

            def link(ins):
                n_chain[0] += 1
                ins.then_inc(S["pchain"], 1)
                pool.wait_ge(S["pchain"], n_chain[0])

            def ts(out, a, s1, op0, s2=None, op1=None):
                if op1 is None:
                    return pool.tensor_scalar(out, a, s1, None, op0)
                return pool.tensor_scalar(out, a, s1, s2, op0, op1)

            def tten(out, a, b_, op):
                return pool.tensor_tensor(out, a, b_, op)

            def norm_scale(n, q, batch=None, place=None):
                for p, b in enumerate(ids(q)) if batch is None else [(batch, 2 * q + batch)]:
                    pool.wait_ge(S["stats_mv"], ln_at(n, b))
                    at = p if place is None else place
                    r = rstd[:, at, :]
                    link(ts(r, mv[:, at, :, 1], EPS, ADD))
                    tten(r, r, k(KHALF).to_broadcast([128, NT]), ALU.pow).then_inc(S["rstd_set"], 1)

            for i, v in ((KHALF, -0.5), (KE, 2.718281828459045), (KM1, -1.0), (KPI2, PI_2),
                         (KLN, -0.6931471805599453)):
                last = pool.memset(k(i), v)
            link(last)
            pool.wait_ge(S["ld_a"], 32)
            link(ts(C("lam"), vc("beta"), -1.0, MUL))
            link(tten(C("lam"), k(KE), C("lam"), ALU.pow))
            link(ts(C("lam"), C("lam"), 1.0, ADD))
            tten(C("lam"), C("lam"), k(KM1), ALU.pow).then_inc(S["lam_set"], 1)
            pool.memset(xF[0][:, 0:1], 0.0)
            pool.memset(xF[1][:, 0:1], 0.0).then_inc(S["zeroed"], 1)
            ts(C("one_r"), vc("mu_r"), -1.0, MUL, 1.0, ADD)
            ts(C("one_k"), vc("mu_k"), -1.0, MUL, 1.0, ADD).then_inc(S["mix_set"], 1)
            ts(C("ai4"), vc("a_im"), 0.25, MUL)
            pool.memset(C("t3"), 0.0).then_inc(S["consts"], 1)

            def phases():
                pool.wait_ge(S["ld_b"], 32)
                tten(stmp[:, 0, :], W("th"), W("thn"), ADD)
                link(tten(stmp[:, 1, :], W("phi"), W("phin"), ADD))
                link(ts(stmp[:, :, :], stmp[:, :, :], 1.0 / 6.283185307179586, MUL))
                ts(w_cos[:, :], stmp[:, 0, :], 0.25, ADD, MAGIC, ADD)
                link(ts(w_sin[:, :], stmp[:, 1, :], MAGIC, ADD))
                ts(w_cos[:, :], w_cos[:, :], MAGIC, SUB)
                link(ts(w_sin[:, :], w_sin[:, :], MAGIC, SUB))
                tten(stmp[:, 0, :], w_cos[:, :], stmp[:, 0, :], SUB)
                tten(stmp[:, 1, :], w_sin[:, :], stmp[:, 1, :], SUB).then_inc(S["th_arg"], 1)

            def zero_rows(rows):
                pool.memset(rows[:, :, :].bitcast(F32), 0.0).then_inc(S["rows_zero"], 1)

            def ones_rows():
                link(pool.memset(ones_zeros[:, :], 0.0))
                link(pool.memset(ones, 1.0))
                for p in range(2):
                    pool.memset(VA[p][:, NT * NH * VW:], 0.0)
                    last = pool.memset(values(p)[:, :, :, HD:VW], 1.0)
                pool.tensor_copy(ident_h[:, :], ident).then_inc(S["ones_set"], 1)

            def soft_exp():
                a = vc("a_re")
                link(ts(C("w"), a, -1.0, MUL))
                link(ts(C("w"), C("w"), a, ALU.min))
                link(tten(C("w"), k(KE), C("w"), ALU.pow))
                link(ts(C("u1"), C("w"), 1.0, ADD))
                ts(C("dd"), C("u1"), -1.0, ADD).then_inc(S["soft_u"], 1)
                pool.wait_ge(S["soft_u"], 1)
                ts(C("t1"), C("dd"), 0.0, ALU.is_equal)

            def soft_plus():
                a = vc("a_re")
                pool.wait_ge(S["soft_ln"], 1)
                link(ts(C("t2"), C("t0"), -1.0, MUL))
                link(tten(C("t2"), k(KE), C("t2"), ALU.pow))
                link(tten(C("t2"), C("t2"), C("u1"), MUL))
                link(ts(C("t2"), C("t2"), -1.0, ADD))
                link(tten(C("t0"), C("t0"), C("t2"), ADD))
                link(tten(C("t0"), C("t0"), C("t1"), ADD))
                link(tten(C("t0"), C("t0"), C("w"), MUL))
                link(tten(C("dd"), C("dd"), C("t1"), ADD))
                link(tten(C("dd"), C("dd"), k(KM1), ALU.pow))
                link(tten(C("t0"), C("t0"), C("dd"), MUL))
                link(ts(C("soft"), a, 0.0, MAX))
                link(tten(C("soft"), C("soft"), C("t0"), ADD))
                ts(C("t3"), C("soft"), 1e-19, MAX).then_inc(S["soft_s"], 1)

            def soft_log():
                a = vc("a_re")
                pool.wait_ge(S["log_s"], 1)
                link(ts(C("t2"), C("y"), -1.0, MUL))
                link(tten(C("t2"), k(KE), C("t2"), ALU.pow))
                link(tten(C("t2"), C("t2"), C("t3"), MUL))
                link(ts(C("t2"), C("t2"), -1.0, ADD))
                link(tten(C("y"), C("y"), C("t2"), ADD))
                link(ts(C("t1"), a, -40.0, ALU.is_lt))
                link(tten(C("t2"), a, C("y"), SUB))
                link(tten(C("t2"), C("t2"), C("t1"), MUL))
                link(tten(C("y"), C("y"), C("t2"), ADD))
                ts(C("Lh"), C("y"), 0.5, MUL).then_inc(S["gates_set"], 1)

            def tables_arg():
                link(tten(C("z"), k(KE), vc("ph_ln"), ALU.pow))
                link(tten(C("z"), C("z"), vc("ph_sc"), MUL))
                link(ts(C("z"), C("z"), -1.0, MUL))
                link(tten(C("m"), k(KE), C("z"), ALU.pow))
                link(ts(C("gateC"), C("m"), -1.0, MUL, 1.0, ADD))
                link(tten(C("om"), vc("ph_ang"), vc("ph_sc"), MUL))
                link(ts(C("om"), C("om"), 1.0 / 6.283185307179586, MUL))
                link(ts(tt[0], iota, C("om"), MUL))
                ts(tab[:, 0, :], tt[0], MAGIC, ADD)
                link(ts(tab[:, 1, :], tt[0], 0.25, ADD, MAGIC, ADD))
                link(ts(tab[:, 0:2, :], tab[:, 0:2, :], MAGIC, SUB))
                tten(tab[:, 0, :], tab[:, 0, :], tt[0], SUB)
                link(tten(tab[:, 1, :], tab[:, 1, :], tt[0], SUB))
                ts(C("ir"), vc("ph_im"), -1.0, MUL).then_inc(S["ph_arg"], 1)

            def tables():
                pool.wait_ge(S["ph_trig"], 1)
                sn, cs = tt[0], tt[1]
                ts(tab[:, 0, :], sn, vc("ph_im"), MUL)
                ts(tab[:, 1, :], cs, vc("ph_im"), MUL)
                ts(tab[:, 2, :], cs, vc("ph_re"), MUL)
                link(ts(tab[:, 3, :], sn, vc("ph_re"), MUL))
                tten(tab[:, 0, :], tab[:, 0, :], tab[:, 2, :], ADD)
                link(tten(tab[:, 1, :], tab[:, 1, :], tab[:, 3, :], SUB))
                ts(tab[:, 2, :], cs, C("gateC"), MUL)
                ts(tab[:, 3, :], sn, C("gateC"), MUL).then_inc(S["tab_set"], 1)

            def turn_back(q, p):
                pool.wait_ge(S["xf_set"], xf_at(6, 2 * q + p))
                tten(RC[p][0], xF[p][:, 1:1 + L], tab[:, 0, :], MUL).then_inc(S["c_in"], 1)

            def turn_on(q, p):
                pool.wait_ge(S["c_g"], 2 * (2 * q + p + 1))
                tten(RC[p][1], RC[p][3], tab[:, 3, :], MUL).then_inc(S["c_t2"], 1)

            def square(q, p):
                for m in (1, 3):
                    pool.wait_ge(S["h_relu"], 4 * (2 * q + p) + m + 1)
                    tten(tmp[p][4 + m][:, 0:L], tmp[p][m][:, 0:L], tmp[p][m][:, 0:L], MUL).then_inc(S["h_sqp"], 1)

            soft_exp()
            for q in range(PAIRS):
                if q == 0:
                    norm_scale(0, q)
                    soft_plus()
                if q == 0:
                    norm_scale(1, q)
                else:
                    pool.wait_ge(S["ln_done"], ln_at(1, 3))
                    zero_rows(QS[0])
                if q == 0:
                    soft_log()
                    phases()
                    ones_rows()
                    zero_rows(KS[0])
                norm_scale(2, q)
                for p, b in enumerate(ids(q)):
                    pool.wait_ge(S["ln_done"], ln_at(2, b))
                    tten(r3(tmp[p][9][:, 0:L]), r3(xT[p][:, :]),
                         W("b_out").unsqueeze(1).broadcast_to([128, NT, 128]), ADD).then_inc(S["g_xb"], 1)
                for p, b in enumerate(ids(q)):
                    pool.wait_ge(S["g_mag"], at(b))
                    t = tmp[p][3][:, 0:L]
                    link(tten(t, tmp[p][2][:, 0:L], tmp[p][2][:, 0:L], MUL))
                    link(ts(t, t, -1.0, MUL, 1.0, ADD))
                    ts(t, t, 1e-6, MAX).then_inc(S["g_t"], 1)
                for p, b in enumerate(ids(q)):
                    pool.wait_ge(S["g_xr"], at(b))
                    pool.wait_ge(S["g_trig"], at(b))
                    a_, b_ = tmp[p][5][:, 0:L], tmp[p][6][:, 0:L]
                    tten(a_, tmp[p][1][:, 0:L], tmp[p][8][:, 0:L], MUL)
                    link(tten(b_, tmp[p][0][:, 0:L], tmp[p][7][:, 0:L], MUL))
                    tten(a_, a_, b_, SUB).then_inc(S["g_rot"], 1)
                b = 2 * q
                pool.wait_ge(S["g_scan"], at(b))
                a_, b_ = tmp[0][1][:, 0:L], tmp[0][6][:, 0:L]
                tten(a_, tmp[0][7][:, 0:L], tmp[0][3][:, 0:L], MUL)
                link(tten(b_, tmp[0][8][:, 0:L], tmp[0][4][:, 0:L], MUL))
                pool.wait_ge(S["g_hr"], at(b))
                tten(tmp[0][8][:, 0:L], a_, b_, ADD).then_inc(S["g_hi"], 1)
                if q == 0:
                    zero_rows(QS[1])
                norm_scale(3, q)
                if q == 0:
                    zero_rows(KS[1])
                for p, b in enumerate(ids(q)):
                    pool.wait_ge(S["f1_sq"], at(b))
                    tten(tmp[p][2][:, 0:L], tmp[p][0][:, 0:L], tmp[p][1][:, 0:L], ADD).then_inc(S["f1_ss"], 1)
                norm_scale(4, q)
                for p, b in enumerate(ids(q)):
                    spread(pool, p, b, at_ks[p], {(0, 1): (0,), (1, 1): (0, 1), (2, 1): (0, 1)})
                u0 = 2 * NG * q

                def negate(u):
                    v = u % 2
                    m = mx[:, v, :].rearrange("p (s x) -> p s x", s=2)
                    part = [mp[:, v, :].rearrange("p (s r x) -> p s r x", s=2, r=3)[:, :, r, :] for r in range(3)]
                    res = mres[:, v, :].rearrange("p (s x) -> p s x", s=2)
                    pool.wait_ge(S["at_max"], 8 * (u + 1))
                    if u >= 2:
                        pool.wait_ge(S["at_mt"], u - 1)
                    ts(part[0], m, -1.0, MUL)
                    link(ts(res, m, -1.0, MUL))
                    link(tten(res, res, part[0], SUB))
                    link(pool.tensor_copy(part[1], res))
                    tten(part[2], res, part[1], SUB).then_inc(S["at_mp"], 1)

                for u in range(u0, u0 + 2 * NG):
                    negate(u)
                    if u == u0 + 2 * NG - 2:
                        norm_scale(5, q, 0)
                norm_scale(5, q, 1)
                if q == 0:
                    pool.wait_ge(S["ln_done"], ln_at(5, 1))
                    tables_arg()
                for p, b in enumerate(ids(q)):
                    for e in range(E_MOE):
                        n = E_MOE * b + e
                        if q == 0 and n == 4:
                            tables()
                        pool.wait_ge(S["mo_t"], n + 1)
                        other = xT[p] if e == 0 else Y[p]
                        if e:
                            pool.wait_ge(S["mo_acc"], n)
                        tten(Y[p][:, :], ye[e % 2], other[:, :], ADD).then_inc(S["mo_acc"], 1)
                        if n + 1 in EARLY and EARLY[n + 1][0] == "turn":
                            norm_scale(0, 1, EARLY[n + 1][1] % 2)
                        if p == 0 and e == E_MOE - 1:
                            norm_scale(6, q, 0)
                        if p == 1 and e == 1:
                            turn_back(q, 0)
                        if p == 1 and e == 3:
                            turn_on(q, 0)
                        if p == 1 and e == 4:
                            norm_scale(7, q, 0)
                norm_scale(6, q, 1)
                square(q, 0)
                turn_back(q, 1)
                turn_on(q, 1)
                norm_scale(7, q, 1)
                norm_scale(8, q, 0)
                square(q, 1)
                if q == 0:
                    for b in (2, 3):
                        norm_scale(1, 1, b % 2, STAT[b])
                norm_scale(8, q, 1)

        @block.vector
        def _(dve):
            n_chain = [0]

            def link(ins):
                n_chain[0] += 1
                ins.then_inc(S["dchain"], 1)
                dve.wait_ge(S["dchain"], n_chain[0])

            def stt(out, a, s, b_, op0, op1):
                return dve.scalar_tensor_tensor(out, a, s, b_, op0, op1)

            def tt_(out, a, b_, op):
                return dve.tensor_tensor(out, a, b_, op)

            def ts(out, a, s1, op0, s2=None, op1=None):
                if op1 is None:
                    return dve.tensor_scalar(out, a, s1, None, op0)
                return dve.tensor_scalar(out, a, s1, s2, op0, op1)

            def stats(p, src):
                for t in range(NT):
                    last = dve.bn_stats(st6[:, p, t, :], src[:, t * 128:(t + 1) * 128])
                link(last)
                for t in range(NT):
                    last = dve.bn_aggr(mv[:, p, t, :], st6[:, p, t, :])
                last.then_inc(S["stats_mv"], 1)

            def scale_rows(n, p, b, dst, src):
                dve.wait_ge(S["rstd_set"], ln_at(n, b))
                for t in range(NT):
                    last = ts(dst[:, t * 128:(t + 1) * 128], src[:, t * 128:(t + 1) * 128],
                              mv[:, p, t, 0:1], SUB, rstd[:, p, t:t + 1], MUL)
                last.then_inc(S["ln_done"], 1)

            def norm(n, q):
                for p, b in enumerate(ids(q)):
                    scale_rows(n, p, b, xT[p], Y[p])

            def l0_step(what, b):
                out, p = l0_bank[b].get(what), b % 2
                if what == "v":
                    if b == 0:
                        dve.wait_ge(S["lam_set"], 1)
                    dve.wait_ge(S["l0_v"], at(b))
                    dve.tensor_tensor_scan(L0[b]["state"], C("lam").to_broadcast([128, L]), out, 0.0, MUL,
                                           ADD).then_inc(S["l0_state"], 1)
                elif what == "q":
                    dve.wait_ge(S["l0_q"], at(b))
                    dve.wait_ge(S["l0_state"], at(b))
                    tt_(L0[b]["yq"], L0[b]["state"], out, MUL).then_inc(S["l0_yq"], 1)
                elif what == "turn":
                    dve.wait_ge(S["l0_yt"], at(b))
                    stats(p, out)
                elif what == "norm":
                    scale_rows(0, p, b, L0[b]["n"], l0_bank[b]["turn"])
                else:
                    dve.wait_ge(S["l0_ng"], at(b))
                    dve.wait_ge(S["l0_sg"], at(b))
                    tt_(L0[b]["z"], L0[b]["ng"], L0[b]["sg"], MUL).then_inc(S["l0_z"], 1)

            def l0_attn(q):
                if q == 0:
                    for b in ids(q):
                        l0_step("v", b)
                        l0_step("q", b)
                    for what in ("turn", "norm", "z"):
                        for b in ids(q):
                            l0_step(what, b)
                    for b in ids(q):
                        l0_add(b)
                    for b in ids(q):
                        l0_norm(b)

            def l0_add(b):
                dve.wait_ge(S["l0_o"], at(b))
                dve.wait_ge(ld_t[b], 16)
                link(tt_(YR[b], P(b % 2, 1)[:, :], XR[b], ADD))
                stats(STAT[b], YR[b])

            def l0_norm(b):
                scale_rows(1, STAT[b], b, xT[b % 2], YR[b])

            def l0_ffn(q):
                for p, b in enumerate(ids(q)):
                    dve.wait_ge(S["f0_mix"], at(b))
                    x = xF[p][:, 1:1 + L]
                    stt(tmp[p][3][:, 0:L], x, vc("mu_k"), tmp[p][0][:, 0:L], MUL, ADD)
                    stt(tmp[p][2][:, 0:L], x, vc("mu_r"), tmp[p][1][:, 0:L], MUL, ADD).then_inc(S["f0_xrk"], 1)
                if q == 0:
                    hb = sv[:, S_["hbx"]:S_["hba"] + 1]
                    dve.wait_ge(S["wc_bias"], 1)
                    dve.wait_ge(S["mix_set"], 1)
                    link(tt_(hb, P(0, 3)[:, 256:258], vec[:, V["bg_x"]:V["bg_a"] + 1], ADD))
                    ts(hb, hb, 0.5, MUL).then_inc(S["bias_half"], 1)
                for p, b in enumerate(ids(q)):
                    dve.wait_ge(S["f0_v"], at(b))
                    dve.wait_ge(S["f0_tr"], at(b))
                    link(stt(tmp[p][7][:, 0:L], tmp[p][6][:, 0:L], 1.0, P(p, 2)[:, :], ADD, MUL))
                    if q:
                        dve.wait_ge(out_dma[b - 2], 16)
                    link(stt(Y[p][:, :], tmp[p][7][:, 0:L], 0.5, xT[p][:, :], MUL, ADD))
                    stats(p, Y[p])
                norm(2, q)

            def l1_attn(q):
                u, f, g, hi, lo = [[tmp[p][i][:, 0:L] for p in range(2)] for i in (4, 5, 6, 7, 8)]
                one = kone.to_broadcast([128, L])
                done = [0, 0]

                def step(p, ins):
                    n_chain[0] += 1
                    ins.then_inc(S["dchain"], 1)
                    done[p] = n_chain[0]

                def after_last(p):
                    dve.wait_ge(S["dchain"], done[p])

                for p, b in enumerate(ids(q)):
                    dve.wait_ge(S["g_ta"], at(b))
                    step(p, ts(f[p], u[p], MAGIC, ADD))
                for p in range(2):
                    after_last(p)
                    step(p, stt(f[p], f[p], MAGIC, u[p], SUB, SUB))
                for p in range(2):
                    after_last(p)
                    step(p, ts(g[p], f[p], MAGIC14, ADD, MAGIC14, SUB))
                for p in range(2):
                    after_last(p)
                    step(p, tt_(u[p], f[p], g[p], SUB))
                for p in range(2):
                    dve.tensor_tensor_scan(hi[p], one, g[p], 0.0, MUL, ADD)
                    after_last(p)
                    step(p, dve.tensor_tensor_scan(lo[p], one, u[p], 0.0, MUL, ADD))
                for p in range(2):
                    after_last(p)
                    step(p, ts(f[p], hi[p], MAGIC, ADD))
                for p in range(2):
                    after_last(p)
                    step(p, stt(f[p], f[p], MAGIC, hi[p], SUB, SUB))
                for p in range(2):
                    after_last(p)
                    step(p, tt_(u[p], f[p], lo[p], SUB))
                for p in range(2):
                    after_last(p)
                    ts(f[p], u[p], MAGIC, ADD)
                    step(p, ts(g[p], u[p], 0.25, ADD, MAGIC, ADD))
                for p in range(2):
                    after_last(p)
                    stt(f[p], f[p], MAGIC, u[p], SUB, SUB)
                    stt(g[p], g[p], MAGIC, u[p], SUB, SUB).then_inc(S["g_arg"], 1)
                for p, b in enumerate(ids(q)):
                    dve.wait_ge(S["g_w"], at(b))
                    dve.wait_ge(S["g_tx"], at(b))
                    dve.wait_ge(S["g_xh"], at(b))
                    w, xr, xi = tmp[p][3][:, 0:L], tmp[p][0][:, 0:L], tmp[p][1][:, 0:L]
                    link(stt(w, tmp[p][1][:, 0:L], 1.0, w, ADD, MUL))
                    stt(xr, P(p, 0)[:, :], vc("b_re"), w, ADD, MUL)
                    stt(xi, P(p, 1)[:, :], vc("b_im"), w, ADD, MUL).then_inc(S["g_xr"], 1)
                for p, b in enumerate(ids(q)):
                    w, xr, xi, c = [tmp[p][i][:, 0:L] for i in (3, 0, 1, 4)]
                    sn, cs = tmp[p][7][:, 0:L], tmp[p][8][:, 0:L]
                    dve.wait_ge(S["g_trig"], at(b))
                    dve.wait_ge(S["g_xr"], at(b))
                    tt_(w, xr, cs, MUL)
                    link(tt_(c, xi, sn, MUL))
                    link(tt_(w, w, c, ADD))
                    dve.tensor_tensor_scan(w, tmp[p][2][:, 0:L], w, 0.0, MUL, ADD)
                for p, b in enumerate(ids(q)):
                    dve.wait_ge(S["g_rot"], at(b))
                    dve.tensor_tensor_scan(tmp[p][4][:, 0:L], tmp[p][2][:, 0:L], tmp[p][5][:, 0:L], 0.0,
                                           MUL, ADD).then_inc(S["g_scan"], 1)
                for p, b in enumerate(ids(q)):
                    sn, cs = tmp[p][7][:, 0:L], tmp[p][8][:, 0:L]
                    re, im = tmp[p][3][:, 0:L], tmp[p][4][:, 0:L]
                    dve.wait_ge(S["g_scan"], at(b))
                    tt_(tmp[p][5][:, 0:L], cs, re, MUL)
                    if p:
                        tt_(tmp[p][1][:, 0:L], sn, re, MUL)
                        tt_(tmp[p][6][:, 0:L], cs, im, MUL)
                    link(tt_(tmp[p][0][:, 0:L], sn, im, MUL))
                    last = tt_(tmp[p][5][:, 0:L], tmp[p][5][:, 0:L], tmp[p][0][:, 0:L], SUB)
                    if p:
                        last = tt_(tmp[p][8][:, 0:L], tmp[p][1][:, 0:L], tmp[p][6][:, 0:L], ADD)
                    last.then_inc(S["g_hr"], 1)
                for p, b in enumerate(ids(q)):
                    dve.wait_ge(S["g_o"], at(b))
                    dve.wait_ge(S["g_xb"], at(b))
                    link(tt_(Y[p][:, :], P(p, 2)[:, :], tmp[p][9][:, 0:L], ADD))
                    stats(p, Y[p])
                norm(3, q)

            def l1_ffn(q):
                for p, b in enumerate(ids(q)):
                    dve.wait_ge(S["f1_rt"], at(b))
                    link(tt_(Y[p][:, :], tmp[p][3][:, 0:L], xT[p][:, :], ADD))
                    stats(p, Y[p])
                norm(4, q)

            def l2_attn(q):
                for p, b in enumerate(ids(q)):
                    for side in range(2):
                        dve.wait_ge(S["at_hi"], at(b, 2) - 1 + side)
                        tt_(tmp[p][side][:, 0:L], P(p, side)[:, :], parts[p][side][0], SUB).then_inc(S["at_r1"], 1)
                    for side in range(2):
                        dve.wait_ge(S["at_mid"], at(b, 2) - 1 + side)
                        last = tt_(parts[p][side][2], tmp[p][side][:, 0:L], parts[p][side][1], SUB)
                    last.then_inc(S["at_parts"], 1)
                u0 = 2 * NG * q

                def max_row(u):
                    dve.wait_ge(S["at_mt"], u + 1)
                    if u >= 2:
                        dve.wait_ge(at_m[u % 2], 16 * 2 * (u // 2))
                    dve.tensor_copy(mrow[:, u % 2, :], bank[7].bitcast(BF16)[0:48, 0:128]).then_inc(S["at_mrow"], 1)

                def out_rows(u):
                    v = u - u0
                    p, g = v // NG, v % NG
                    dve.wait_ge(S["at_ot"], u + 1)
                    o = bank[7][:, :].rearrange("p (n c) -> p n c", c=32)
                    link(dve.reciprocal(rden[:, u % 2, :], o[:, :, HD]))
                    dst = Y[p][:, :].rearrange("p (t g j d) -> p t g j d", t=NT, g=NG, j=4)[:, :, g, :, :]
                    tt_(dst, o[:, :, 0:HD].rearrange("p (t j) d -> p t j d", t=NT),
                        rden[:, u % 2, :].rearrange("p (t j) -> p t j", t=NT).unsqueeze(3).broadcast_to(
                            [128, NT, 4, HD]), MUL).then_inc(S["at_res"], 1)

                def maxima(u, i):
                    n = 8 * u + i
                    jj, qt = i % 2, i // 2
                    dve.wait_ge(S["at_s"], n + 1)
                    if i == 0 and u >= 2:
                        dve.wait_ge(S["at_mp"], u - 1)
                    dst = mx[:, u % 2, :].rearrange("p (s j t) -> p s j t", s=2, j=2)[:, :, jj, qt]
                    dve.reduce_max(dst, two[i % 2][:, :, :], AX.X).then_inc(S["at_max"], 1)

                def residual(p):
                    dve.wait_ge(S["at_res"], NG * (2 * q + p + 1))
                    link(tt_(Y[p][:, :], Y[p][:, :], xT[p][:, :], ADD))
                    stats(p, Y[p])

                for v in range(-2, 2 * NG):
                    u = u0 + v
                    for i in range(8):
                        if v + 2 < 2 * NG:
                            maxima(u + 2, i)
                        if i == (2 if v < 0 else 3) and v >= -1 and v + 1 < 2 * NG:
                            max_row(u + 1)
                        if i == 6 and v >= 1:
                            out_rows(u - 1)
                        if i == 1 and v == 2 * NG - 3:
                            residual(0)
                        if i == 4 and v == 2 * NG - 3:
                            scale_rows(5, 0, 2 * q, xT[0], Y[0])
                        if i == 0 and v == 2 * NG - 1:
                            route_scores(q, 0)
                        if i == 2 and v == 2 * NG - 1:
                            route(q, 0)
                out_rows(u0 + 2 * NG - 1)
                residual(1)
                scale_rows(5, 1, 2 * q + 1, xT[1], Y[1])

            def last_scales():
                dve.wait_ge(S["ld_c"], 32)
                fc, pj = wc[:, 0:4, :], wc[:, 4:8, :].rearrange("p t c -> p (t c)")
                dve.tensor_reduce(fsc[:, 0:4, 0:1], fc, AX.X, ADD, apply_absolute_value=True)
                link(dve.tensor_reduce(fsc[:, 4, 0:1], pj, AX.X, ADD, apply_absolute_value=True))
                ts(fsc[:, 0:4, 0], fsc[:, 0:4, 0], 1.0 / 128, MUL, 1e-5, MAX)
                link(ts(fsc[:, 4:5, 0], fsc[:, 4:5, 0], 1.0 / HID, MUL, 1e-5, MAX))
                ts(fsc[:, :, 1], fsc[:, :, 0], 0.5, MUL)
                link(ts(fsc[:, :, 2], fsc[:, :, 0], -0.5, MUL))

            def last_weights(step):
                pj = wc[:, 4:8, :].rearrange("p t c -> p (t c)")
                tiles = [(0, t, wc[:, t, :], slice(t * 128, (t + 1) * 128)) for t in range(4)]
                for s, t, w, c in tiles + [(1, 4, pj, slice(0, HID))]:
                    d, o = wq_s[s][:, c], wo_s[s][:, c]
                    if step == 0:
                        last = ts(o, w, fsc[:, t, 1:2], ALU.is_gt)
                    elif step == 1:
                        last = stt(d, w, fsc[:, t, 2:3], o, ALU.is_lt, SUB)
                    elif step == 2:
                        last = stt(o, d, -1.0, w, MUL, SUB)
                    elif step == 3:
                        last = tt_(d, w, o, ADD)
                    else:
                        last = ts(d, d, fsc[:, t, 0:1], MUL)
                link(last)
                if step == 4:
                    ts(fsc[:, :, 1], fsc[:, :, 1], 1.0, MUL).then_inc(S["q_fc"], 2)

            def route_scores(q, p):
                lg = bank[7][:, 0:NT * E_MOE].rearrange("p (t e) -> p t e", t=NT)
                dve.wait_ge(S["rt_l"], 2 * q + p + 1)
                link(dve.reduce_max(rs[:, p, 0, :], lg, AX.X))
                tt_(rt[:, p, 0, :, :], lg, rs[:, p, 0, :].unsqueeze(2).broadcast_to([128, NT, E_MOE]),
                    SUB).then_inc(S["rt_s"], 1)

            def route(q, p):
                b = 2 * q + p
                dve.wait_ge(S["rt_e"], at(b))
                pr = rt[:, p, 2, :, :]
                link(dve.reduce_sum(rs[:, p, 1, :], rt[:, p, 1, :, :], AX.X))
                link(dve.reciprocal(rs[:, p, 1, :], rs[:, p, 1, :]))
                link(tt_(pr, rt[:, p, 1, :, :], rs[:, p, 1, :].unsqueeze(2).broadcast_to([128, NT, E_MOE]), MUL))
                rk, above = [tmp[p][8][:, c:c + 256].rearrange("p (t e j) -> p t e j", t=NT, e=E_MOE)
                             for c in (0, 256)]
                for t in range(NT):
                    mine = pr[:, t, :].unsqueeze(2).broadcast_to([128, E_MOE, E_MOE])
                    all_ = pr[:, t, :].unsqueeze(1).broadcast_to([128, E_MOE, E_MOE])
                    last = tt_(rk[:, t, :, :], all_, mine, ALU.is_equal)
                link(last)
                for t in range(NT):
                    last = tt_(rk[:, t, :, :], rk[:, t, :, :], tri[:, :, :], MUL)
                link(last)
                for t in range(NT):
                    mine = pr[:, t, :].unsqueeze(2).broadcast_to([128, E_MOE, E_MOE])
                    all_ = pr[:, t, :].unsqueeze(1).broadcast_to([128, E_MOE, E_MOE])
                    last = tt_(above[:, t, :, :], all_, mine, ALU.is_gt)
                link(last)
                for t in range(NT):
                    last = tt_(rk[:, t, :, :], rk[:, t, :, :], above[:, t, :, :], ADD)
                link(last)
                link(dve.reduce_sum(cmb[:, p, :, :], rk, AX.X))
                link(stt(cmb[:, p, :, :], cmb[:, p, :, :], 2.0, pr, ALU.is_lt, MUL))
                link(dve.reduce_sum(rs[:, p, 2, :], cmb[:, p, :, :], AX.X))
                link(ts(rs[:, p, 2, :], rs[:, p, 2, :], 1e-6, ADD))
                link(dve.reciprocal(rs[:, p, 2, :], rs[:, p, 2, :]))
                link(tt_(cmb[:, p, :, :], cmb[:, p, :, :],
                         rs[:, p, 2, :].unsqueeze(2).broadcast_to([128, NT, E_MOE]), MUL))

            def moe(q):
                def weigh(p, b, e):
                    n = E_MOE * b + e
                    dve.wait_ge(S["mo_y"], n + 1)
                    if n >= 2:
                        dve.wait_ge(S["mo_acc"], n - 1)
                    tt_(r3(ye[e % 2]), r3(bank[6 + e % 2][:, :]),
                        cmb[:, p, :, e].unsqueeze(2).broadcast_to([128, NT, 128]), MUL).then_inc(S["mo_t"], 1)

                work = [(p, b, e) for p, b in enumerate(ids(q)) for e in range(E_MOE)]
                for i, (p, b, e) in enumerate(work):
                    for m, (c0, cn) in enumerate(MT):
                        n = 3 * (E_MOE * b + e) + m
                        dve.wait_ge(S["mo_sg"], n + 1)
                        if e >= 2 or b:
                            dve.wait_ge(S["mo_y"], E_MOE * b + e - 1)
                        tt_(hm[3 * (e % 2) + m][0:cn, :], sg[n % 3][0:cn, :],
                            bank[2 * (n % 3) + 1][0:cn, :], MUL).then_inc(S["mo_h"], 1)
                    if i == 1:
                        route_scores(q, 1)
                    if i == 9:
                        dve.wait_ge(S["mo_acc"], E_MOE * (2 * q + 1))
                        stats(0, Y[0])
                    if i == 10:
                        scale_rows(6, 0, 2 * q, xT[0], Y[0])
                    if i == 13:
                        combine(q, 0)
                    if i == 14:
                        scale_rows(7, 0, 2 * q, xT[0], Y[0])
                    if i:
                        weigh(*work[i - 1])
                    if q == 0 and i in EARLY:
                        what, b2 = EARLY[i]
                        if what in ("v", "q", "turn"):
                            l0_step(what, b2)
                        if what == "turn":
                            l0_step("norm", b2)
                    if q == 0 and i in (13, 14):
                        l0_step("z", i - 11)
                    if i == 11:
                        scan_im(q, 0)
                    if i == 12:
                        scan_re(q, 0)
                    if i == 13:
                        add_rc(q, 0, 7)
                    if i == 2:
                        route(q, 1)
                    if q == 0 and i == 3:
                        last_scales()
                    if q == 0 and i in (4, 5, 8, 9, 10):
                        last_weights((4, 5, 8, 9, 10).index(i))
                weigh(*work[-1])
                dve.wait_ge(S["mo_acc"], E_MOE * (2 * q + 2))
                stats(1, Y[1])
                scale_rows(6, 1, 2 * q + 1, xT[1], Y[1])

            def scan_im(q, p):
                if q == 0 and p == 0:
                    dve.wait_ge(S["tab_set"], 1)
                dve.wait_ge(S["xf_set"], xf_at(6, 2 * q + p))
                link(tt_(RC[p][1], xF[p][:, 1:1 + L], tab[:, 1, :], MUL))
                dve.tensor_tensor_scan(RC[p][3], C("m").to_broadcast([128, L]), RC[p][1], vc("lc_im"),
                                       MUL, ADD).then_inc(S["c_g"], 1)

            def scan_re(q, p):
                dve.wait_ge(S["c_in"], 2 * q + p + 1)
                dve.tensor_tensor_scan(RC[p][2], C("m").to_broadcast([128, L]), RC[p][0], vc("lc_re"),
                                       MUL, ADD).then_inc(S["c_g"], 1)

            def combine(q, p):
                dve.wait_ge(S["c_g"], 2 * (2 * q + p + 1))
                link(tt_(RC[p][0], RC[p][2], tab[:, 2, :], MUL))
                dve.wait_ge(S["c_t2"], 2 * q + p + 1)
                tt_(RC[p][0], RC[p][0], RC[p][1], SUB).then_inc(S["c_y"], 1)

            def add_rc(q, p, bk):
                dve.wait_ge(S["c_t"], 2 * q + p + 1)
                link(tt_(Y[p][:, :], bank[bk], xT[p][:, :], ADD))
                stats(p, Y[p])

            def square(q, p):
                for m in (0, 2):
                    dve.wait_ge(S["h_relu"], 4 * (2 * q + p) + m + 1)
                    tt_(tmp[p][4 + m][:, 0:L], tmp[p][m][:, 0:L], tmp[p][m][:, 0:L], MUL).then_inc(S["h_sqd"], 1)

            def add_ffn(q, p):
                dve.wait_ge(S["h_o"], 2 * q + p + 1)
                link(tt_(Y[p][:, :], P(p, 0)[:, :], xT[p][:, :], ADD))
                stats(p, Y[p])

            def l3(q):
                if q == 0:
                    dve.wait_ge(S["q_uv"], 1)
                    dve.wait_ge(S["q_ft"], 2)
                    link(dve.tensor_copy(fcT[:, :], P(0, 2)[:, :]))
                    stt(fcT[:, :], P(0, 1)[:, :], vc("gate"), fcT[:, :], MUL, ADD).then_inc(S["q_fe"], 1)
                square(q, 0)
                scan_im(q, 1)
                scan_re(q, 1)
                combine(q, 1)
                add_rc(q, 1, 4)
                add_ffn(q, 0)
                scale_rows(7, 1, 2 * q + 1, xT[1], Y[1])
                scale_rows(8, 0, 2 * q, Y[0], Y[0])
                square(q, 1)
                if q == 0:
                    l0_add(2)
                    l0_add(3)
                    l0_norm(2)
                add_ffn(q, 1)
                if q == 0:
                    l0_norm(3)
                scale_rows(8, 1, 2 * q + 1, Y[1], Y[1])

            dve.memset(QS[0][:, :, :].bitcast(F32), 0.0).then_inc(S["rows_zero"], 1)
            kone = kc[:, 6:7]
            dve.memset(kone, 1.0)
            for q in range(PAIRS):
                l0_attn(q)
                l0_ffn(q)
                l1_attn(q)
                l1_ffn(q)
                l2_attn(q)
                moe(q)
                l3(q)


def _arrays(i):
    import numpy as np
    g = {n: np.asarray(a) for n, a in i.items()}
    x = g["L0_attn_x"]
    f32 = x.dtype

    def T(a):
        return np.asarray(a).T

    def diag(w):
        d = np.zeros((256, 128), f32)
        for n in range(16):
            d[16 * n:16 * n + 16, 8 * n:8 * n + 8] = w[n]
        return d

    def halves(w):
        return w.reshape(128, NH // 2, 2, HD).transpose(0, 2, 3, 1).reshape(128, 128)

    bdx, bda = diag(g["L1_attn_Wg_x"]), diag(g["L1_attn_Wg_a"])
    w_in, w_out = g["L1_attn_W_in"], g["L1_attn_W_out"]
    blocks = {
        "l0_q": T(g["L0_attn_Wq"]), "l0_v": T(g["L0_attn_Wv"]), "l0_g": T(g["L0_attn_Wg"]), "l0_o": T(g["L0_attn_Wo"]),
        "ident": np.eye(128, dtype=f32),
        "f0_r": T(g["L0_ffn_W_r"]), "f0_k": T(g["L0_ffn_W_k"]), "f0_v": T(g["L0_ffn_W_v"]),
        "in_re": w_in[:, :128], "in_im": w_in[:, 128:], "inT0": T(w_in)[:128], "inT1": T(w_in)[128:],
        "bdx0": bdx[:128], "bdx1": bdx[128:], "bda0": bda[:128], "bda1": bda[128:],
        "out0": w_out[:128], "out1": w_out[128:], "b_out": np.broadcast_to(g["L1_attn_b_out"], (128, 128)),
        "th": g["L1_ffn_theta"], "thn": g["L1_ffn_theta_noise"], "phi": g["L1_ffn_phi"], "phin": g["L1_ffn_phi_noise"],
        "a_q": halves(T(g["L2_attn_Wq"])), "a_k": halves(T(g["L2_attn_Wk"])), "a_v": T(g["L2_attn_Wv"]),
    }
    for t in range(4):
        blocks[f"fc{t}"] = g["L3_ffn_w_fc"][t * 128:(t + 1) * 128]
        blocks[f"pj{t}"] = g["L3_ffn_w_proj"][:, t * 128:(t + 1) * 128]
    vecs = {
        "beta": np.repeat(g["L0_attn_beta"], 8), "gamma": g["L0_attn_ln_gamma"], "lnb": g["L0_attn_ln_beta"],
        "mu_r": g["L0_ffn_mu_r"], "mu_k": g["L0_ffn_mu_k"], "b_re": g["L1_attn_b_in"][:128], "b_im": g["L1_attn_b_in"][128:],
        "bg_x": g["L1_attn_bg_x"], "bg_a": g["L1_attn_bg_a"], "a_re": g["L1_attn_a_real_param"],
        "a_im": g["L1_attn_a_imag_param"], "ph_re": g["L3_attn_phazor_init_re"], "ph_im": g["L3_attn_phazor_init_im"],
        "ph_ang": g["L3_attn_phazor_angle"], "ph_ln": g["L3_attn_ln_minus_ln_phazor_abs"],
        "lc_re": g["L3_attn_last_conv_re"], "lc_im": g["L3_attn_last_conv_im"], "ph_sc": g["L3_attn_ln_phazor_scale"],
        "gate": np.broadcast_to(g["L3_ffn_gate"], (128,)),
    }
    dn = np.zeros((128, 8 * 3, 128), f32)
    for e in range(8):
        for m, (c0, cn) in enumerate(MT):
            dn[:cn, 3 * e + m] = g["L2_ffn_w_down"][e, c0:c0 + cn]
    ar = {
        "xt": x.reshape(B, NT, 128, D).transpose(2, 0, 1, 3).reshape(128, B, L),
        "xf": x.transpose(2, 0, 1),
        "vec": np.stack([vecs[n] for n in VEC], axis=1),
        "wa": np.stack([blocks[n] for n in WA], axis=1),
        "wb": np.stack([blocks[n] for n in WB], axis=1),
        "wc": np.stack([blocks[n] for n in WC], axis=1),
        "small": np.concatenate([T(g["L3_ffn_u"]), g["L3_ffn_v"], T(g["L3_ffn_fast_b"])], axis=1),
        "rt": g["L2_ffn_router_w"],
        "gu": np.stack([g["L2_ffn_w_gate"], g["L2_ffn_w_up"]]).transpose(2, 0, 1, 3),
        "dn": dn,
        "iota": np.broadcast_to(np.arange(1, L + 1, dtype=f32), (128, L)),
        "tri": np.broadcast_to(np.tril(np.ones((8, 8), f32), -1), (128, 8, 8)),
    }
    return {n: np.ascontiguousarray(a) for n, a in ar.items()}


def kernel(**inputs):
    import numpy as _np
    import concourse.bacc as _bacc
    from concourse import mybir as _mybir
    from concourse.bass_utils import run_bass_kernel_spmd as _run

    nc = _bacc.Bacc("TRN2", target_bir_lowering=False, num_devices=1)
    arrays = _arrays(inputs)
    args = [nc.dram_tensor("in_" + n, a.shape, _mybir.dt.from_np(a.dtype), kind="ExternalInput").ap() for n, a in arrays.items()]
    out = nc.dram_tensor("out", (128, B, L), _mybir.dt.float32, kind="ExternalOutput").ap()
    build(nc, *args, out)
    r = _run(nc, [{"in_" + n: a for n, a in arrays.items()}], core_ids=[0])
    y = r.results[0]["out"]
    return _np.ascontiguousarray(_np.asarray(y).reshape(128, B, NT, D).transpose(1, 2, 0, 3).reshape(B, L, D))
```
